# Optimizing a Trainium2 kernel written in Bass

```python
import numpy as np
import jax
import jax.numpy as jnp

def _softmax(x, axis=-1):
    return jax.nn.softmax(x, axis=axis)

def _gelu(x):
    return jax.nn.gelu(x, approximate=True)

def _silu(x):
    return jax.nn.silu(x)

def _sigmoid(x):
    return jax.nn.sigmoid(x)

def _layernorm(x, axis=-1, eps=1e-05):
    m = jnp.mean(x, axis=axis, keepdims=True)
    v = jnp.var(x, axis=axis, keepdims=True)
    return (x - m) / jnp.sqrt(v + eps)

def _scatter_add(tgt, idx, src, axis=0):
    return tgt.at[idx].add(src)

def _segment_sum(src, seg, n):
    return jax.ops.segment_sum(src, seg, n)
kernel_name = 'mk_decoder_preln_d1_seqx_r4_150d87'

def setup_inputs(seed: int=0):
    np.random.seed(seed)
    _w = jnp.asarray

    def _rec_inputs():
        import jax
        import jax.numpy as jnp
        _rk = jax.random.key(seed)
        x = -0.000125 + 0.9999 * jax.random.normal(jax.random.fold_in(_rk, 1), (4, 512, 512), jnp.float32)
        _lenS = 512 - jax.random.randint(jax.random.fold_in(_rk, 7), (4,), 0, max(1, 512 // 4) + 1, jnp.int32)
        _lenS2 = 512 - jax.random.randint(jax.random.fold_in(_rk, 8), (4,), 0, max(1, 512 // 4) + 1, jnp.int32)
        itok_BxS_13_99985 = jax.random.randint(jax.random.fold_in(_rk, 11), (4, 512), 13, 99986, jnp.int32)
        _ctx_2048P = jax.random.normal(jax.random.fold_in(_rk, 12), (4, 16, 512), jnp.float32)
        _ctx_2048c = jax.random.dirichlet(jax.random.fold_in(_rk, 512), 0.3 * jnp.ones((16,), jnp.float32), (4, 512))
        _ctx_2048t = jnp.einsum('bsk,bkd->bsd', _ctx_2048c, _ctx_2048P)
        _ctx_2048t = _ctx_2048t * jax.lax.rsqrt(jnp.mean(jnp.square(_ctx_2048t)) + 1e-12) * 0.953939
        ctx_2048 = 6.82029e-06 + 0.0200006 * (_ctx_2048t + 0.3 * jax.random.normal(jax.random.fold_in(_rk, 612), (4, 512, 512), jnp.float32))
        return (x, itok_BxS_13_99985, ctx_2048)
    x, itok_BxS_13_99985, ctx_2048 = _rec_inputs()

    def _L0_attn_setup():
        import jax, jax.numpy as jnp
        import numpy as np
        EMBED_DIM = 512
        NUM_HEADS = 16
        Q_LORA = 128
        KV_LORA = 128
        ROPE_DIM = 64
        NOPE_DIM = EMBED_DIM // NUM_HEADS
        V_DIM = EMBED_DIM // NUM_HEADS
        Q_HEAD_DIM = NOPE_DIM + ROPE_DIM
        BASE = 10000.0

        def rope(x, offset=0, base=BASE):
            b, n, h, d = x.shape
            inv_freq = base ** (-jnp.arange(0, d, 2, dtype=jnp.float32) / d)
            pos = jnp.arange(offset, offset + n, dtype=jnp.float32)
            ang = pos[:, None] * inv_freq[None, :]
            cos = jnp.cos(ang)[None, :, None, :]
            sin = jnp.sin(ang)[None, :, None, :]
            x1 = x[..., 0::2]
            x2 = x[..., 1::2]
            o1 = x1 * cos - x2 * sin
            o2 = x1 * sin + x2 * cos
            return jnp.stack([o1, o2], axis=-1).reshape(b, n, h, d)
        key = jax.random.key(seed)
        ks = jax.random.split(key, 6)
        s = 0.02
        x = jax.random.normal(ks[0], (2, 512, EMBED_DIM), dtype=jnp.float32)
        Wqa = jax.random.normal(ks[1], (EMBED_DIM, Q_LORA), dtype=jnp.float32) * s
        Wqb = jax.random.normal(ks[2], (Q_LORA, NUM_HEADS * Q_HEAD_DIM), dtype=jnp.float32) * s
        Wkva = jax.random.normal(ks[3], (EMBED_DIM, KV_LORA + ROPE_DIM), dtype=jnp.float32) * s
        Wkvb = jax.random.normal(ks[4], (KV_LORA, NUM_HEADS * (NOPE_DIM + V_DIM)), dtype=jnp.float32) * s
        Wo = jax.random.normal(ks[5], (NUM_HEADS * V_DIM, EMBED_DIM), dtype=jnp.float32) * s
        return {'x': x, 'Wqa': Wqa, 'Wqb': Wqb, 'Wkva': Wkva, 'Wkvb': Wkvb, 'Wo': Wo}
    _L0_attn_all = _L0_attn_setup()
    _L0_attn_in = {k: v for k, v in _L0_attn_all.items() if k in ('Wqa', 'Wqb', 'Wkva', 'Wkvb', 'Wo')}
    del _L0_attn_all

    def _L0_xattn_setup():
        import jax, jax.numpy as jnp
        import numpy as np
        B, S, D = (4, 1024, 512)
        E = 4
        F = 2048 // E
        VOCAB = 25000
        key = jax.random.key(seed)
        k1, k2, k3, k4, k5 = jax.random.split(key, 5)
        hidden_states = jax.random.normal(k1, (B, S, D), dtype=jnp.float32)
        token_ids = jax.random.randint(k2, (B, S), 0, VOCAB, dtype=jnp.int64)
        Wg = jax.random.normal(k3, (E, F, D), dtype=jnp.float32) * 0.02
        Wu = jax.random.normal(k4, (E, F, D), dtype=jnp.float32) * 0.02
        Wd = jax.random.normal(k5, (E, D, F), dtype=jnp.float32) * 0.02
        return {'hidden_states': hidden_states, 'token_ids': token_ids, 'Wg': Wg, 'Wu': Wu, 'Wd': Wd}
    _L0_xattn_all = _L0_xattn_setup()
    _L0_xattn_in = {k: v for k, v in _L0_xattn_all.items() if k in ()}
    del _L0_xattn_all

    def _L0_ffn_setup():
        import jax, jax.numpy as jnp
        import numpy as np
        TOP_K = 2
        NUM_EXPERTS = 8
        ROUTE_SCALE = 1.0
        key = jax.random.key(seed)
        ks = jax.random.split(key, 8)
        bs, slen, dim, hidden, E = (4, 256, 512, 256, NUM_EXPERTS)
        s = 0.02
        return {'x': jax.random.normal(ks[0], (bs, slen, dim), jnp.float32), 'gate_w': jax.random.normal(ks[1], (E, dim), jnp.float32) * s, 'w1': jax.random.normal(ks[2], (E, hidden, dim), jnp.float32) * s, 'w2': jax.random.normal(ks[3], (E, dim, hidden), jnp.float32) * s, 'w3': jax.random.normal(ks[4], (E, hidden, dim), jnp.float32) * s, 'ws1': jax.random.normal(ks[5], (hidden, dim), jnp.float32) * s, 'ws2': jax.random.normal(ks[6], (dim, hidden), jnp.float32) * s, 'ws3': jax.random.normal(ks[7], (hidden, dim), jnp.float32) * s}
    _L0_ffn_all = _L0_ffn_setup()
    _L0_ffn_in = {k: v for k, v in _L0_ffn_all.items() if k in ('gate_w', 'w1', 'w2', 'w3', 'ws1', 'ws2', 'ws3')}
    del _L0_ffn_all
    return {'x': x, 'itok_BxS_13_99985': itok_BxS_13_99985, 'ctx_2048': ctx_2048, 'L0_attn_Wqa': _L0_attn_in['Wqa'], 'L0_attn_Wqb': _L0_attn_in['Wqb'], 'L0_attn_Wkva': _L0_attn_in['Wkva'], 'L0_attn_Wkvb': _L0_attn_in['Wkvb'], 'L0_attn_Wo': _L0_attn_in['Wo'], 'L0_ffn_gate_w': _L0_ffn_in['gate_w'], 'L0_ffn_w1': _L0_ffn_in['w1'], 'L0_ffn_w2': _L0_ffn_in['w2'], 'L0_ffn_w3': _L0_ffn_in['w3'], 'L0_ffn_ws1': _L0_ffn_in['ws1'], 'L0_ffn_ws2': _L0_ffn_in['ws2'], 'L0_ffn_ws3': _L0_ffn_in['ws3']}

def reference(x, itok_BxS_13_99985, ctx_2048, L0_attn_Wqa, L0_attn_Wqb, L0_attn_Wkva, L0_attn_Wkvb, L0_attn_Wo, L0_ffn_gate_w, L0_ffn_w1, L0_ffn_w2, L0_ffn_w3, L0_ffn_ws1, L0_ffn_ws2, L0_ffn_ws3):
    import jax
    import jax.numpy as jnp

    def _L0_attn_ref(x, Wqa, Wqb, Wkva, Wkvb, Wo):
        import jax, jax.numpy as jnp
        import numpy as np
        EMBED_DIM = 512
        NUM_HEADS = 16
        Q_LORA = 128
        KV_LORA = 128
        ROPE_DIM = 64
        NOPE_DIM = EMBED_DIM // NUM_HEADS
        V_DIM = EMBED_DIM // NUM_HEADS
        Q_HEAD_DIM = NOPE_DIM + ROPE_DIM
        BASE = 10000.0

        def rope(x, offset=0, base=BASE):
            b, n, h, d = x.shape
            inv_freq = base ** (-jnp.arange(0, d, 2, dtype=jnp.float32) / d)
            pos = jnp.arange(offset, offset + n, dtype=jnp.float32)
            ang = pos[:, None] * inv_freq[None, :]
            cos = jnp.cos(ang)[None, :, None, :]
            sin = jnp.sin(ang)[None, :, None, :]
            x1 = x[..., 0::2]
            x2 = x[..., 1::2]
            o1 = x1 * cos - x2 * sin
            o2 = x1 * sin + x2 * cos
            return jnp.stack([o1, o2], axis=-1).reshape(b, n, h, d)
        b, n, d = x.shape
        h = NUM_HEADS
        q = x @ Wqa @ Wqb
        q = q.reshape(b, n, h, Q_HEAD_DIM)
        q_nope, q_pe = (q[..., :NOPE_DIM], q[..., NOPE_DIM:])
        ckv = x @ Wkva
        compressed_kv, k_pe = (ckv[..., :KV_LORA], ckv[..., KV_LORA:])
        k_pe = jnp.broadcast_to(k_pe[:, :, None, :], (b, n, h, ROPE_DIM))
        kv = (compressed_kv @ Wkvb).reshape(b, n, h, NOPE_DIM + V_DIM)
        k_nope, v = (kv[..., :NOPE_DIM], kv[..., NOPE_DIM:])
        q_pe = rope(q_pe)
        k_pe = rope(k_pe)
        qf = jnp.concatenate([q_nope, q_pe], axis=-1)
        kf = jnp.concatenate([k_nope, k_pe], axis=-1)
        vf = jnp.pad(v, ((0, 0), (0, 0), (0, 0), (0, Q_HEAD_DIM - V_DIM)))
        scale = 1.0 / jnp.sqrt(jnp.asarray(Q_HEAD_DIM, dtype=qf.dtype))
        scores = jnp.einsum('bnhd,bmhd->bhnm', qf, kf) * scale
        mask = jnp.tril(jnp.ones((n, n), dtype=bool))
        scores = jnp.where(mask[None, None], scores, jnp.finfo(scores.dtype).min)
        probs = jax.nn.softmax(scores, axis=-1)
        out = jnp.einsum('bhnm,bmhd->bnhd', probs, vf)
        out = out[..., :V_DIM].reshape(b, n, h * V_DIM)
        return out @ Wo

    def _L0_xattn_ref(hidden_states, token_ids, Wg, Wu, Wd):
        import jax, jax.numpy as jnp
        import numpy as np
        B, S, D = (4, 1024, 512)
        E = 4
        F = 2048 // E
        VOCAB = 25000
        tokens_per_expert = VOCAB // E
        tid = jnp.clip(token_ids, 0, VOCAB - 1)
        expert_ids = jnp.minimum(tid // tokens_per_expert, E - 1)
        out = jnp.zeros_like(hidden_states)
        for e in range(E):
            g = jax.nn.silu(jnp.einsum('bsd,fd->bsf', hidden_states, Wg[e]))
            u = jnp.einsum('bsd,fd->bsf', hidden_states, Wu[e])
            y = jnp.einsum('bsf,df->bsd', g * u, Wd[e])
            out = jnp.where((expert_ids == e)[..., None], y, out)
        return out

    def _L0_ffn_ref(x, gate_w, w1, w2, w3, ws1, ws2, ws3):
        import jax, jax.numpy as jnp
        import numpy as np
        TOP_K = 2
        NUM_EXPERTS = 8
        ROUTE_SCALE = 1.0
        bs, slen, dim = x.shape
        xf = x.reshape(-1, dim)
        logits = (xf @ gate_w.T).astype(jnp.float32)
        scores = jax.nn.sigmoid(logits)
        top_scores, sel_idx = jax.lax.top_k(scores, TOP_K)
        top_scores = top_scores * ROUTE_SCALE
        routed = jnp.zeros_like(xf)
        for k in range(TOP_K):
            xs = xf * top_scores[:, k][:, None]
            h1 = jnp.einsum('td,ehd->teh', xs, w1)
            h3 = jnp.einsum('td,ehd->teh', xs, w3)
            h = jax.nn.silu(h1) * h3
            onehot = jax.nn.one_hot(sel_idx[:, k], NUM_EXPERTS, dtype=h.dtype)
            routed = routed + jnp.einsum('teh,te,edh->td', h, onehot, w2)
        shared = jax.nn.silu(xf @ ws1.T) * (xf @ ws3.T) @ ws2.T
        out = (shared + routed).reshape(bs, slen, dim)
        return out
    x = x + _L0_attn_ref(_layernorm(x, axis=-1), L0_attn_Wqa, L0_attn_Wqb, L0_attn_Wkva, L0_attn_Wkvb, L0_attn_Wo)
    x = x + _L0_xattn_ref(_layernorm(x, axis=-1), itok_BxS_13_99985, ctx_2048, ctx_2048, ctx_2048)
    x = x + _L0_ffn_ref(_layernorm(x, axis=-1), L0_ffn_gate_w, L0_ffn_w1, L0_ffn_w2, L0_ffn_w3, L0_ffn_ws1, L0_ffn_ws2, L0_ffn_ws3)
    return x

_drawn_inputs = setup_inputs


def setup_inputs(seed=0):
    import zlib

    import numpy as np

    out = dict(_drawn_inputs(seed))
    spreads = {}
    factors = {'L0_attn_Wqa': 8.0,
     'L0_attn_Wqb': 8.0,
     'L0_attn_Wkva': 8.0,
     'L0_attn_Wkvb': 8.0,
     'L0_attn_Wo': 8.0,
     'L0_ffn_gate_w': 13.633,
     'L0_ffn_w1': 11.503,
     'L0_ffn_w2': 10.437,
     'L0_ffn_w3': 10.554,
     'ctx_2048': 8.0,
     'L0_ffn_ws1': 8.0,
     'L0_ffn_ws2': 8.0,
     'L0_ffn_ws3': 8.0}
    for name, (base, spread) in spreads.items():
        noise = np.random.default_rng([zlib.crc32(name.encode()), seed]).standard_normal(out[name].shape)
        drawn = base * np.exp(spread * noise) if base else spread * noise
        out[name] = jnp.asarray(drawn.astype(out[name].dtype))
    for name, factor in factors.items():
        out[name] = (out[name] * factor).astype(out[name].dtype)
    return out
```

```python
from contextlib import ExitStack

import concourse.bass as bass
from concourse import mybir

F32 = mybir.dt.float32
BF16 = mybir.dt.bfloat16
I32 = mybir.dt.int32
U32 = mybir.dt.uint32
ALU = mybir.AluOpType
ACT = mybir.ActivationFunctionType
AX = mybir.AxisListType

P = 128
BATCH, SEQ, DIM = 4, 512, 512
TOKENS = BATCH * SEQ
NT = TOKENS // P
TB = SEQ // P
DC = DIM // P
HEADS, NOPE, ROPE = 16, 32, 64
HALF = ROPE // 2
QK = NOPE + ROPE
VD = DIM // HEADS
LORA = 128
GROUP = P // NOPE
NG = HEADS // GROUP
LEAD = 4
UNITS = HEADS * TB
EPS = 1e-5
MASKED = -1e30

EX_B, VOCAB = 4, 25000
EX_C, TOPK, HID = 8, 2, 256
NB_B = NT + EX_B - 1
NB_C = NT * TOPK + EX_C - 1


class AttentionPlan:

    WORK = (0, 1, 2, 6)
    PT = (3, 4)
    OUT = 5
    PROJ = 7

    def __init__(self):
        self.tiles = {}
        self.uses = {s: [0] * 8 for s in ("pro", "units", "epi")}
        pro = [("xT", c) for c in range(DC)] + [("qa",), ("ckv",)]
        pro += [(k, 0) for k in "EONK"] + [("kpe",)] + [("V", t) for t in range(TB)]
        for n, name in enumerate(pro):
            self.take("pro", name, self.WORK[n % LEAD])
        for u in range(UNITS):
            self.take("units", ("S", u), self.WORK[u % LEAD])
            self.take("units", ("PT", u), self.PT[u % 2])
        for g in range(NG):
            self.take("units", ("out", g), self.OUT)
        for g in range(NG):
            for k in "EONK" * (g + 1 < NG):
                self.take("units", (k, g + 1), self.PROJ)
            if g > 0:
                self.take("units", ("R", g - 1), self.PROJ)
        epi = [("R", NG - 1)] + [("Wo", t) for t in range(TB)]
        for n, name in enumerate(epi):
            self.take("epi", name, self.WORK[n % LEAD])

    def take(self, section, name, bank):
        self.tiles[section, name] = (bank, self.uses[section][bank])
        self.uses[section][bank] += 1

    def place(self, section, name, b):
        bank, nth = self.tiles[section, name]
        p, u, e = (self.uses[s][bank] for s in ("pro", "units", "epi"))
        first = isinstance(b, int) and b == 0
        last = isinstance(b, int) and b == BATCH - 1
        if section == "pro":
            before = 0 if first else (b - 1) * (p + u + e) + (p + u)
        elif section == "units":
            before = b * (p + u + e) + p
        else:
            before = b * (p + u + e) + (p + u) + (0 if last else p)
        return bank, before + nth


def attention_block(nc, ext, keep):
    plan = AttentionPlan()
    x1, ident, arena, pos_b, xs_b = keep.x1, keep.ident, keep.arena, keep.pos_b, keep.xs_b
    s_x0, s_xr = keep.s_x0, keep.s_xr
    with ExitStack() as ctx:
        def sb(name, shape, dt=F32):
            return ctx.enter_context(nc.sbuf_tensor(name, shape, dt))

        def sem(name):
            return ctx.enter_context(nc.semaphore(name))

        wqa = sb("wqa", [P, DC, LORA])
        wkva = sb("wkva", [P, DC, LORA + 2 * ROPE])
        wqb = sb("wqb", [P, NG * 3, P])
        wk = sb("wk", [P, NG, P])
        wv = sb("wv", [P, HEADS * VD])
        wo = sb("wo", [P, DC, DIM])
        cos4 = sb("cos4", [P, SEQ])
        sin4 = sb("sin4", [P, SEQ])
        kcs = sb("kcs", [P, SEQ])
        identb = sb("identb", [P, P], BF16)
        maskb = sb("maskb", [P, P], BF16)
        half = sb("half", [P, TB])
        epsc = sb("epsc", [P, TB])
        st1 = sb("st1", [P, TB, 6])
        mv1 = sb("mv1", [P, TB, 2])
        var1 = sb("var1", [P, TB])
        rstd1 = sb("rstd1", [P, TB])
        st2 = sb("st2", [P, TB, 6])
        mv2 = sb("mv2", [P, TB, 2])
        var2 = sb("var2", [P, TB])
        rstd2 = sb("rstd2", [P, TB])
        xn = sb("xn", [P, TB, DIM])
        xT = sb("xT", [P, DC, SEQ])
        qaT = sb("qaT", [P, SEQ])
        cT = sb("cT", [P, SEQ])
        rot = sb("rot", [P, 4, SEQ])
        rEO = sb("rEO", [P, 2, SEQ])
        kpt = sb("kpt", [ROPE, 2, SEQ])
        half_arena = 2 * GROUP * SEQ
        QT = arena[0:QK, 0:half_arena].rearrange("p (s q) -> p s q", q=SEQ)
        KT = arena[0:QK, half_arena:].rearrange("p (s q) -> p s q", q=SEQ)
        V = sb("V", [P, TB, DIM])
        negmax = sb("negmax", [P, 2 * LEAD])
        probs = sb("probs", [P, LEAD, SEQ])
        PTs = sb("PTs", [P, 2, GROUP, SEQ])
        sums = sb("sums", [P, 2, TB, GROUP])
        rinv = sb("rinv", [P, TB * GROUP])
        rsum = sb("rsum", [P, TB * GROUP, VD])
        osb = sb("osb", [P, SEQ])
        OT = sb("OT", [P, DC, SEQ])
        xo = xn
        pos_cur = sb("pos_cur", [P, TB], I32)
        bank = [ctx.enter_context(nc.psum_tensor(f"bank{k}", [P, 512], F32)) for k in range(8)]

        filled = [sem(f"filled{k}") for k in range(8)]
        free = [sem(f"free{k}") for k in range(8)]
        s_wp = sem("proj_weights_loaded")
        s_wo = sem("wo_loaded")
        s_cst = sem("constants_ready")
        s_ones = sem("ones_ready")
        s_mv1, s_rs1, s_xn = sem("stats1_ready"), sem("rstd1_ready"), sem("xn_ready")
        s_mv2, s_rs2, s_xo = sem("stats2_ready"), sem("rstd2_ready"), sem("xn2_ready")
        s_p1, s_p2 = sem("pool_var1"), sem("pool_var2")
        s_c1, s_c2, s_c3 = sem("dve_ln1"), sem("dve_ln2"), sem("dve_norm")
        s_rot, s_rope, s_nk = sem("rot_products_ready"), sem("rotated_ready"), sem("nk_ready")
        s_qk = sem("qk_loaded")
        s_kpt, s_kpe = sem("kpe_products_ready"), sem("kpe_ready")
        s_kr = sem("kpe_repeated")
        s_nm, s_exp = sem("negmax_ready"), sem("probs_ready")
        s_rs = sem("sums_inverted")
        s_rb = sem("inverses_repeated")
        s_oc = sem("group_out_copied")
        s_on = sem("group_out_ready")
        s_scat = keep.s_xs_b
        s_pc = sem("positions_copied")
        s_aux = sem("unused_count")
        block = ctx.enter_context(nc.Block())
        QK_DMAS = 2 * GROUP
        PROJ_STEP = {0: "E", 1: "O", 3: "N", 5: "K"}

        def steps():
            for s in range(-LEAD, UNITS):
                yield s

        def proj_at(s):
            if s >= 0 and (s % 16) in PROJ_STEP and s // 16 + 1 < NG:
                return PROJ_STEP[s % 16], s // 16 + 1
            return None

        def inverted_at(s):
            return s // 16 - 1 if s >= 16 and s % 16 == 9 else None

        def quad_at(s):
            return (s - 2) // 4 if s >= 5 and s % 4 == 1 else None

        def unit(u):
            return u // 16, (u % 16) // GROUP, u % GROUP

        def evac_pt_by_act(u):
            return u % GROUP == GROUP - 1

        @block.sync
        def _(sp):
            for dst, src in ((wqa, "wqa"), (wkva, "wkva"), (wqb, "wqb"), (wk, "wk"), (wv, "wv"),
                             (cos4, "cos4"), (sin4, "sin4"), (kcs, "kcs")):
                sp.dma_start(dst.ap(), ext[src]).then_inc(s_wp, 16)
            sp.dma_start(wo.ap(), ext["wo"]).then_inc(s_wo, 16)
            load_rest_of_x(sp, ext, keep)

            def group(b, g):
                n = b * NG + g
                sp.wait_ge(s_rope, n * 2 + 2 + 2)
                for j in range(GROUP):
                    slot = (g % 2) * GROUP + j
                    rows = slice(j * 32, j * 32 + 32)
                    sp.dma_start(QT[0:32, slot, :], rEO[rows, 0, :]).then_inc(s_qk, 16)
                    sp.dma_start(QT[32:64, slot, :], rEO[rows, 1, :]).then_inc(s_qk, 16)

            def repeat_kpe(b):
                sp.wait_ge(s_kpe, b + 2)
                sp.dma_start(KT[0:ROPE, 1:2 * GROUP, :],
                             KT[0:ROPE, 0:1, :].to_broadcast([ROPE, 2 * GROUP - 1, SEQ])).then_inc(s_kr, 16)

            group(0, 0)
            repeat_kpe(0)
            with sp.Fori(0, BATCH - 1) as b:
                for g in range(1, NG):
                    group(b, g)
                group(b + 1, 0)
                repeat_kpe(b + 1)
            for g in range(1, NG):
                group(BATCH - 1, g)
            k, n = plan.place("units", ("out", NG - 1), BATCH - 1)
            sp.wait_ge(filled[k], n + 1)
            sp.dma_start(arena[:, :], ext["ctxT"]).then_inc(keep.s_ctx, 16)

        @block.gpsimd
        def _(pool):
            g = nc.gpsimd
            pool.sem_inc(s_rope, 2)
            pool.sem_inc(s_rb, 1)
            pool.sem_inc(s_kpe, 1)
            pool.sem_inc(s_qk, 16 * QK_DMAS)
            g.memset(half.ap(), -0.5).then_inc(s_cst, 1)
            g.memset(epsc.ap(), EPS).then_inc(s_ones, 1)
            g.memset(identb.ap(), 0.0).then_inc(s_cst, 1)
            g.memset(maskb.ap(), 0.0).then_inc(s_cst, 1)
            pool.wait_ge(s_cst, 3)
            pool.wait_ge(s_ones, 1)
            g.affine_select(out=identb.ap(), in_=identb.ap(), compare_op=ALU.not_equal, fill=1.0, base=0,
                            pattern=[[-1, P]], channel_multiplier=1).then_inc(s_cst, 1)
            g.affine_select(out=maskb.ap(), in_=maskb.ap(), compare_op=ALU.is_ge, fill=MASKED, base=0,
                            pattern=[[-1, P]], channel_multiplier=1).then_inc(s_cst, 1)

            def inverse_root(b, mv, var, rstd, s_mv, s_step, s_out):
                pool.wait_ge(s_mv, b * TB + TB)
                g.tensor_tensor(out=var.ap(), in0=mv[:, :, 1], in1=epsc.ap(), op=ALU.add).then_inc(s_step, 1)
                pool.wait_ge(s_step, b + 1)
                g.tensor_tensor(out=rstd.ap(), in0=var.ap(), in1=half.ap(), op=ALU.pow).then_inc(s_out, 1)

            def rope_sums(b, gi):
                n = b * NG + gi
                pool.wait_ge(s_rot, n * 4 + 4)
                pool.wait_ge(s_qk, n * (16 * QK_DMAS) + 16 * QK_DMAS)
                g.tensor_tensor(out=rEO[:, 0, :], in0=rot[:, 0, :], in1=rot[:, 2, :], op=ALU.subtract).then_inc(s_rope, 1)
                g.tensor_tensor(out=rEO[:, 1, :], in0=rot[:, 1, :], in1=rot[:, 3, :], op=ALU.add).then_inc(s_rope, 1)

            def pro(b):
                rope_sums(b, 0)
                pool.wait_ge(s_kpt, b * 2 + 2)
                g.tensor_tensor(out=KT[0:ROPE, 0, :], in0=kpt[:, 0, :], in1=kpt[:, 1, :], op=ALU.add).then_inc(s_kpe, 1)

            def repeat(b, gi):
                n = b * NG + gi
                pool.wait_ge(s_rs, n + 3)
                pool.wait_ge(s_on, n + 1)
                pool.sem_inc(s_aux, 1)
                g.tensor_copy(rsum[:, :, :], rinv[:, :].unsqueeze(2).to_broadcast([P, TB * GROUP, VD])).then_inc(s_rb, 1)

            def units(b, more):
                for gi in range(1, NG):
                    rope_sums(b, gi)
                    if gi > 1:
                        repeat(b, gi - 2)
                    if gi == 2 and more:
                        inverse_root(b + 1, mv1, var1, rstd1, s_mv1, s_p1, s_rs1)
                repeat(b, NG - 2)
                repeat(b, NG - 1)

            def epi(b):
                inverse_root(b, mv2, var2, rstd2, s_mv2, s_p2, s_rs2)
                pool.wait_ge(s_scat, b * (16 * TB) + 16)
                pool.sem_inc(s_aux, 1)
                g.tensor_copy(pos_cur[:, :], pos_b[:, bass.ds(b * TB, TB)]).then_inc(s_pc, 1)
                for t in range(TB):
                    pool.wait_ge(s_pc, b + 1)
                    pool.sem_inc(s_aux, 1)
                    pool.wait_ge(s_xo, b * TB + t + 1)
                    pool.sem_inc(s_aux, 1)
                    g.indirect_dma_start(out=xs_b, out_offset=bass.IndirectOffsetOnAxis(ap=pos_cur[:, t:t + 1].bitcast(U32), axis=0),
                                         in_=xo[:, t, :], in_offset=None).then_inc(s_scat, 16)

            clear_scratch(pool, keep)
            inverse_root(0, mv1, var1, rstd1, s_mv1, s_p1, s_rs1)
            pro(0)
            with pool.Fori(0, BATCH - 1) as b:
                units(b, True)
                pro(b + 1)
                epi(b)
            units(BATCH - 1, False)
            epi(BATCH - 1)
            pool.wait_ge(s_scat, BATCH * (16 * TB) + 16)

        @block.vector
        def _(dve):
            v = nc.vector
            for k in range(8):
                dve.sem_inc(free[k], 1)
            dve.sem_inc(s_rs, 2)
            dve.sem_inc(s_on, 1)

            def tile(section, name, b):
                k, n = plan.place(section, name, b)
                dve.wait_ge(filled[k], n + 1)
                return bank[k], free[k]

            def rows(b, t):
                return x1[:, bass.ds(b * TB + t, 1), :].rearrange("p a d -> p (a d)")

            def stats(b, t, src, st, mv, s_chain, s_out, before, per):
                v.bn_stats(st[:, t, :], src).then_inc(s_chain, 1)
                dve.wait_ge(s_chain, b * per + before + 1)
                dve.sem_inc(s_aux, 1)
                v.bn_aggr(mv[:, t, :], st[:, t, :]).then_inc(s_out, 1)

            def ln1_stats(b, t):
                stats(b, t, rows(b, t), st1, mv1, s_c1, s_mv1, t, TB)

            def ln1_norm(b, t):
                if t == 0:
                    if not isinstance(b, int):
                        dve.wait_ge(s_scat, b * (16 * TB) - (16 * TB - 16))
                        dve.sem_inc(s_aux, 1)
                    dve.wait_ge(s_rs1, b + 1)
                v.tensor_scalar(out=xn[:, t, :], in0=rows(b, t), scalar1=mv1[:, t, 0:1], scalar2=rstd1[:, t:t + 1],
                                op0=ALU.subtract, op1=ALU.mult).then_inc(s_xn, 1)

            def rope_products(section, kind, b, g):
                n = b * NG + g
                ps, done = tile(section, (kind, g), b)
                if kind == "E":
                    dve.wait_ge(s_rope, n * 2 + 2)
                    v.tensor_tensor(out=rot[:, 0, :], in0=ps[:, :], in1=cos4[:, :], op=ALU.mult).then_inc(s_rot, 1)
                    v.tensor_tensor(out=rot[:, 1, :], in0=ps[:, :], in1=sin4[:, :], op=ALU.mult).then_inc(s_rot, 1)
                    dve.wait_ge(s_rot, n * 4 + 2)
                else:
                    v.tensor_tensor(out=rot[:, 2, :], in0=ps[:, :], in1=sin4[:, :], op=ALU.mult).then_inc(s_rot, 1)
                    v.tensor_tensor(out=rot[:, 3, :], in0=ps[:, :], in1=cos4[:, :], op=ALU.mult).then_inc(s_rot, 1)
                    dve.wait_ge(s_rot, n * 4 + 4)
                dve.sem_inc(done, 1)

            def pro(b):
                for c in range(1, DC, 2):
                    ps, done = tile("pro", ("xT", c), b)
                    v.tensor_copy(xT[:, c, :], ps[:, :]).then_inc(done, 1)
                rope_products("pro", "E", b, 0)
                rope_products("pro", "O", b, 0)
                ps, done = tile("pro", ("kpe",), b)
                dve.wait_ge(s_kpe, b + 1)
                v.tensor_tensor(out=kpt[:, 0, :], in0=ps[0:ROPE, :], in1=kcs[0:ROPE, :], op=ALU.mult).then_inc(s_kpt, 1)
                v.tensor_tensor(out=kpt[:, 1, :], in0=ps[ROPE:P, :], in1=kcs[ROPE:P, :], op=ALU.mult).then_inc(s_kpt, 1)
                dve.wait_ge(s_kpt, b * 2 + 2)
                dve.sem_inc(done, 1)
                for t in range(1, TB, 2):
                    ps, done = tile("pro", ("V", t), b)
                    v.tensor_copy(V[:, t, :], ps[:, :]).then_inc(done, 1)

            def neg_max(b, u):
                _, i, _ = unit(u)
                ps, _ = tile("units", ("S", u), b)
                if u >= 2 * LEAD:
                    dve.wait_ge(s_exp, b * UNITS + u - 2 * LEAD + 1)
                v.tensor_reduce(out=negmax[:, u % (2 * LEAD):u % (2 * LEAD) + 1], in_=ps[:, 0:(i + 1) * P], axis=AX.X, op=ALU.max,
                                negate=True).then_inc(s_nm, 1)

            def evac_pt(b, u):
                _, i, j = unit(u)
                ps, done = tile("units", ("PT", u), b)
                v.tensor_copy(PTs[:, (u // GROUP) % 2, j, 0:(i + 1) * P], ps[:, 0:(i + 1) * P]).then_inc(done, 1)

            def invert(b, g):
                n = b * NG + g
                dve.wait_ge(s_exp, b * UNITS + (g + 1) * 16)
                dve.wait_ge(s_rb, n + 1)
                v.reciprocal(rinv[:, :], sums[:, g % 2, :, :].rearrange("p t j -> p (t j)")).then_inc(s_rs, 1)

            def group_out(section, b, g):
                n = b * NG + g
                ps, done = tile(section, ("R", g), b)
                dve.wait_ge(s_oc, n + 1)
                v.tensor_tensor(out=OT[:, g, :], in0=ps[:, :], in1=osb[:, :], op=ALU.mult).then_inc(s_on, 1)
                dve.wait_ge(s_on, n + 2)
                dve.sem_inc(done, 1)

            def units(b, more):
                for s in steps():
                    if s + LEAD < UNITS:
                        neg_max(b, s + LEAD)
                    p = proj_at(s)
                    if p and p[0] in "EO":
                        rope_products("units", p[0], b, p[1])
                    if 0 <= s + 1 < UNITS and not evac_pt_by_act(s + 1):
                        evac_pt(b, s + 1)
                    if inverted_at(s + 5) is not None:
                        invert(b, inverted_at(s + 5))
                    if inverted_at(s) is not None:
                        group_out("units", b, inverted_at(s))
                    if more and s in (20, 24, 28, 32):
                        ln1_stats(b + 1, (s - 20) // 4)
                    if more and s in (48, 50, 52, 54):
                        ln1_norm(b + 1, (s - 48) // 2)
                invert(b, NG - 1)

            def epi(b):
                group_out("epi", b, NG - 1)
                for t in range(TB):
                    ps, done = tile("epi", ("Wo", t), b)
                    v.tensor_tensor(out=rows(b, t), in0=ps[:, :], in1=rows(b, t), op=ALU.add).then_inc(s_c2, 1)
                    dve.wait_ge(s_c2, b * (2 * TB) + 2 * t + 1)
                    dve.sem_inc(done, 1)
                    v.bn_stats(st2[:, t, :], rows(b, t)).then_inc(s_c2, 1)
                    dve.wait_ge(s_c2, b * (2 * TB) + 2 * t + 2)
                    dve.sem_inc(s_aux, 1)
                    v.bn_aggr(mv2[:, t, :], st2[:, t, :]).then_inc(s_mv2, 1)
                dve.wait_ge(s_scat, b * (16 * TB) + 16)
                dve.sem_inc(s_aux, 1)
                dve.wait_ge(s_rs2, b + 1)
                for t in range(TB):
                    v.tensor_scalar(out=xo[:, t, :], in0=rows(b, t), scalar1=mv2[:, t, 0:1], scalar2=rstd2[:, t:t + 1],
                                    op0=ALU.subtract, op1=ALU.mult).then_inc(s_xo, 1)

            dve.wait_ge(s_x0, 16)
            for t in range(TB):
                ln1_stats(0, t)
            for t in range(TB):
                ln1_norm(0, t)
            dve.wait_ge(s_wp, 16 * 8)
            pro(0)
            dve.wait_ge(s_xr, 16)
            with dve.Fori(0, BATCH - 1) as b:
                units(b, True)
                pro(b + 1)
                epi(b)
            units(BATCH - 1, False)
            epi(BATCH - 1)

        @block.scalar
        def _(act):
            a = nc.scalar

            def tile(section, name, b):
                k, n = plan.place(section, name, b)
                act.wait_ge(filled[k], n + 1)
                return bank[k], free[k]

            def evac_nk(section, kind, b, g):
                n = b * NG + g
                ps, done = tile(section, (kind, g), b)
                for j in range(GROUP):
                    rows = slice(j * NOPE, (j + 1) * NOPE)
                    dst = (QT if kind == "N" else KT)[ROPE:QK, (g % 2) * GROUP + j, :]
                    a.activation(dst, ps[rows, :], ACT.Copy, scale=QK ** -0.5 if kind == "N" else 1.0).then_inc(s_nk, 1)
                act.wait_ge(s_nk, n * (2 * GROUP) + (GROUP if kind == "N" else 2 * GROUP))
                act.sem_inc(done, 1)

            def pro(b):
                for c in range(0, DC, 2):
                    ps, done = tile("pro", ("xT", c), b)
                    a.copy(xT[:, c, :], ps[:, :]).then_inc(done, 1)
                for name, dst in (("qa", qaT), ("ckv", cT)):
                    ps, done = tile("pro", (name,), b)
                    a.copy(dst[:, :], ps[:, :]).then_inc(done, 1)
                evac_nk("pro", "N", b, 0)
                evac_nk("pro", "K", b, 0)
                for t in range(0, TB, 2):
                    ps, done = tile("pro", ("V", t), b)
                    a.copy(V[:, t, :], ps[:, :]).then_inc(done, 1)

            def exps(b, u):
                g, i, j = unit(u)
                if u % 16 == 0:
                    act.wait_ge(s_rs, b * NG + g + 1)
                act.wait_ge(s_nm, b * UNITS + u + 1)
                ps, done = tile("units", ("S", u), b)
                if u >= LEAD:
                    k, n = plan.place("units", ("PT", u - LEAD), b)
                    act.wait_ge(filled[k], n + 1)
                a.activation(probs[:, u % LEAD, 0:(i + 1) * P], ps[:, 0:(i + 1) * P], ACT.Exp,
                             bias=negmax[:, u % (2 * LEAD):u % (2 * LEAD) + 1], accum_out=sums[:, g % 2, i, j:j + 1]).then_inc(s_exp, 1)
                act.wait_ge(s_exp, b * UNITS + u + 1)
                act.sem_inc(done, 1)

            def copy_out(b, g):
                n = b * NG + g
                ps, done = tile("units", ("out", g), b)
                act.wait_ge(s_on, n + 1)
                a.copy(osb[:, :], ps[:, :]).then_inc(s_oc, 1)
                act.wait_ge(s_oc, n + 1)
                act.sem_inc(done, 1)

            def units(b):
                for s in steps():
                    if s + LEAD < UNITS:
                        exps(b, s + LEAD)
                    p = proj_at(s)
                    if p and p[0] in "NK":
                        evac_nk("units", p[0], b, p[1])
                    if 0 <= s + 1 < UNITS and evac_pt_by_act(s + 1):
                        _, i, j = unit(s + 1)
                        ps, done = tile("units", ("PT", s + 1), b)
                        a.copy(PTs[:, ((s + 1) // GROUP) % 2, j, 0:(i + 1) * P], ps[:, 0:(i + 1) * P]).then_inc(done, 1)
                    q = quad_at(s)
                    if q is not None and q % TB == TB - 1:
                        copy_out(b, q // TB)
                copy_out(b, NG - 1)

            pro(0)
            with act.Fori(0, BATCH - 1) as b:
                units(b)
                pro(b + 1)
            units(BATCH - 1)

        @block.tensor
        def _(pe):
            te = nc.tensor

            def tile(section, name, b):
                k, n = plan.place(section, name, b)
                pe.wait_ge(free[k], n + 1)
                return bank[k], filled[k]

            def evacuated(section, name, b):
                k, n = plan.place(section, name, b)
                pe.wait_ge(free[k], n + 2)

            def mul(out, pairs, done):
                for n, (l, r) in enumerate(pairs):
                    last = te.matmul(out, l, r, start=(n == 0), stop=(n == len(pairs) - 1))
                last.then_inc(done, 1)

            def project(section, kind, b, g):
                ps, done = tile(section, (kind, g), b)
                w, src = {"E": (wqb[:, 3 * g, :], qaT), "O": (wqb[:, 3 * g + 1, :], qaT),
                          "N": (wqb[:, 3 * g + 2, :], qaT), "K": (wk[:, g, :], cT)}[kind]
                mul(ps[:, :], [(w, src[:, :])], done)

            def pro(b):
                pe.wait_ge(s_xn, b * TB + TB)
                for c in range(DC):
                    ps, done = tile("pro", ("xT", c), b)
                    for t in range(TB):
                        last = te.transpose(ps[:, t * P:(t + 1) * P], xn[:, t, c * P:(c + 1) * P], ident[:, :])
                    last.then_inc(done, 1)
                for c in range(DC):
                    evacuated("pro", ("xT", c), b)
                for name, w in (("qa", wqa[:, :, :]), ("ckv", wkva[:, :, 0:LORA])):
                    ps, done = tile("pro", (name,), b)
                    mul(ps[:, :], [(w[:, c, :], xT[:, c, :]) for c in range(DC)], done)
                evacuated("pro", ("qa",), b)
                for kind in "EON":
                    project("pro", kind, b, 0)
                evacuated("pro", ("ckv",), b)
                project("pro", "K", b, 0)
                ps, done = tile("pro", ("kpe",), b)
                mul(ps[:, :], [(wkva[:, c, LORA:], xT[:, c, :]) for c in range(DC)], done)
                for t in range(TB):
                    ps, done = tile("pro", ("V", t), b)
                    mul(ps[:, :], [(cT[:, t * P:(t + 1) * P], wv[:, :])], done)

            def scores(b, u):
                g, i, j = unit(u)
                slot = (g % 2) * GROUP + j
                if u % 16 == 0:
                    n = b * NG + g
                    pe.wait_ge(s_qk, n * (16 * QK_DMAS) + 2 * (16 * QK_DMAS))
                    pe.wait_ge(s_nk, n * (2 * GROUP) + 2 * GROUP)
                ps, done = tile("units", ("S", u), b)
                te.matmul(ps[:, 0:(i + 1) * P], QT[:, slot, i * P:(i + 1) * P], KT[:, slot, 0:(i + 1) * P],
                          start=True, stop=False)
                te.matmul(ps[:, i * P:(i + 1) * P], identb[:, :], maskb[:, :], start=False, stop=True).then_inc(done, 1)

            def transposes(b, u):
                _, i, _ = unit(u)
                pe.wait_ge(s_exp, b * UNITS + u + 1)
                ps, done = tile("units", ("PT", u), b)
                for j in range(i + 1):
                    last = te.transpose(ps[:, j * P:(j + 1) * P], probs[:, u % LEAD, j * P:(j + 1) * P], ident[:, :])
                last.then_inc(done, 1)

            def values(b, q):
                g, i = q // TB, q % TB
                for u in range(q * GROUP + 2, q * GROUP + GROUP):
                    evacuated("units", ("PT", u), b)
                if i == 0:
                    tile("units", ("out", g), b)
                k, _ = plan.place("units", ("out", g), b)
                for j in range(i + 1):
                    for h in range(GROUP):
                        last = te.matmul(bank[k][h * VD:(h + 1) * VD, i * P:(i + 1) * P],
                                         V[:, j, (g * GROUP + h) * VD:(g * GROUP + h + 1) * VD],
                                         PTs[:, q % 2, h, j * P:(j + 1) * P], start=(j == 0), stop=(j == i))
                if i == TB - 1:
                    last.then_inc(filled[k], 1)

            def spread(section, b, g):
                pe.wait_ge(s_rb, b * NG + g + 2)
                ps, done = tile(section, ("R", g), b)
                for i in range(TB):
                    last = te.transpose(ps[:, i * P:(i + 1) * P],
                                        rsum[:, i * GROUP:(i + 1) * GROUP, :].rearrange("p j d -> p (j d)"), ident[:, :])
                last.then_inc(done, 1)

            def units(b):
                pe.wait_ge(s_kr, b * 16 + 16)
                for t in range(TB):
                    evacuated("pro", ("V", t), b)
                for s in steps():
                    if s + LEAD < UNITS:
                        scores(b, s + LEAD)
                    p = proj_at(s)
                    if p:
                        project("units", p[0], b, p[1])
                    if inverted_at(s) is not None:
                        spread("units", b, inverted_at(s))
                    if 0 <= s + 1 < UNITS:
                        transposes(b, s + 1)
                    if quad_at(s) is not None:
                        values(b, quad_at(s))
                values(b, UNITS // GROUP - 1)

            def epi(b):
                spread("epi", b, NG - 1)
                pe.wait_ge(s_on, b * NG + NG + 1)
                for t in range(TB):
                    ps, done = tile("epi", ("Wo", t), b)
                    mul(ps[:, :], [(OT[:, c, t * P:(t + 1) * P], wo[:, c, :]) for c in range(DC)], done)

            pe.wait_ge(s_wp, 16 * 8)
            pe.wait_ge(s_cst, 5)
            pe.wait_ge(s_ones, 1)
            pro(0)
            pe.wait_ge(s_wo, 16)
            with pe.Fori(0, BATCH - 1) as b:
                units(b)
                pro(b + 1)
                epi(b)
            units(BATCH - 1)
            epi(BATCH - 1)


class Keep:

    def __init__(self, nc, ctx, ext):
        def sb(name, shape, dt=F32):
            return ctx.enter_context(nc.sbuf_tensor(name, shape, dt))

        def dram(name, shape):
            return nc.dram_tensor(name, shape, F32, kind="Internal").ap()

        self.x1 = sb("x1", [P, NT, DIM])
        self.ident = sb("ident", [P, P])
        self.arena = sb("arena", [P, 4 * GROUP * SEQ])
        self.upper = sb("upper", [P, P], BF16)
        self.ones = sb("ones", [P, P], BF16)
        self.full = sb("full", [P, NT])
        self.number = sb("number", [P, NB_C])
        self.one = sb("one", [P, NT * TOPK])
        self.pad = sb("pad", [P, ROW])
        self.token = sb("token", [P, NT], I32)
        self.pos_b = sb("pos_b", [P, NT], I32)
        self.ex_b = sb("ex_b", [P, NB_B], I32)
        self.xs_b = dram("xs_b", [NB_B * P, DIM])
        self.ys_b = dram("ys_b", [NB_B * P, DIM])
        self.xn_c = dram("xn_c", [TOKENS, DIM])
        self.xs_c = dram("xs_c", [NB_C * P, ROW])
        self.mean = sb("mean", [P, NT])
        self.rstd = sb("rstd", [P, NT])
        self.score = sb("score", [P, TOPK, NT])
        self.pos_c = sb("pos_c", [P, TOPK * NT], I32)
        self.ex_c = sb("ex_c", [P, NB_C], I32)
        self.s_x0 = ctx.enter_context(nc.semaphore("x_first_loaded"))
        self.s_xr = ctx.enter_context(nc.semaphore("x_rest_loaded"))
        self.s_xs_b = ctx.enter_context(nc.semaphore("xs_b_written"))
        self.s_xs_c = ctx.enter_context(nc.semaphore("xs_c_written"))
        self.s_add = ctx.enter_context(nc.semaphore("routed_rows_added"))
        self.s_ctx = ctx.enter_context(nc.semaphore("ctx_loaded"))
        self.out = ext["out"]


ROW = 576


def load_rest_of_x(sp, ext, keep):
    xv = ext["x"].rearrange("(t p) d -> p t d", p=P)
    sp.dma_start(keep.x1[:, TB:NT, :], xv[:, TB:NT, :]).then_inc(keep.s_xr, 16)


def clear_scratch(pool, keep):
    pool.dma_start(keep.xs_b.rearrange("(n p) d -> p n d", p=P),
                   keep.pad[:, 0:DIM].unsqueeze(1).to_broadcast([P, NB_B, DIM])).then_inc(keep.s_xs_b, 16)
    pool.dma_start(keep.xs_c.rearrange("(n p) d -> p n d", p=P),
                   keep.pad[:, :].unsqueeze(1).to_broadcast([P, NB_C, ROW])).then_inc(keep.s_xs_c, 16)
    pool.dma_start(keep.out[TOKENS:TOKENS + P, :], keep.pad[:, 0:DIM]).then_inc(keep.s_add, 16)


class Chain:

    def __init__(self, eng, s):
        self.eng, self.s, self.n = eng, s, 0

    def __call__(self, ins):
        self.n += 1
        ins.then_inc(self.s, 1)
        self.eng.wait_ge(self.s, self.n)


class Sorter:

    def __init__(self, sb, keep, name, experts, tiles, blocks):
        self.keep, self.e, self.n, self.b = keep, experts, tiles, blocks
        self.pick = sb(f"{name}_pick", [P, experts, tiles])
        self.pickb = sb(f"{name}_pickb", [P, experts, tiles], BF16)
        self.cnt = sb(f"{name}_cnt", [P, experts, tiles])
        self.run = sb(f"{name}_run", [P, experts, tiles])
        self.cmp = sb(f"{name}_cmp", [P, experts, NT])
        self.nb = sb(f"{name}_nb", [P, experts])
        self.ends = sb(f"{name}_ends", [P, experts])
        self.base = sb(f"{name}_base", [P, experts])
        self.off = sb(f"{name}_off", [P, experts, tiles])
        self.posf = sb(f"{name}_posf", [P, tiles])
        self.bcmp = sb(f"{name}_bcmp", [P, blocks, experts - 1])
        self.exf = sb(f"{name}_exf", [P, blocks])

    def on_tensor(self, te, ps):
        w = self.e * self.n
        flat = self.pickb[:, :, :].rearrange("p e n -> p (e n)")
        te.matmul(ps[:, 0:w], self.keep.upper[:, :], flat, start=True, stop=True)
        return te.matmul(ps[:, w:2 * w], self.keep.ones[:, :], flat, start=True, stop=True)

    def on_vector(self, v, do, ps, pos, ex):
        w, e, n = self.e * self.n, self.e, self.n
        above = ps[:, 0:w].rearrange("p (e n) -> p e n", e=e)
        count = ps[:, w:2 * w].rearrange("p (e n) -> p e n", e=e)
        do(v.tensor_copy(self.cnt[:, :, :], count))
        for i in range(e):
            do(v.tensor_tensor_scan(self.run[:, i, :], self.keep.one[:, 0:n], self.cnt[:, i, :], 0.0,
                                    ALU.mult, ALU.add))
        total = self.run[:, :, n - 1:n]
        do(v.tensor_tensor(out=self.cmp[:, :, :], in0=total.to_broadcast([P, e, NT]),
                           in1=self.keep.full[:, :].unsqueeze(1).to_broadcast([P, e, NT]), op=ALU.is_gt))
        do(v.tensor_reduce(out=self.nb[:, :], in_=self.cmp[:, :, :], axis=AX.X, op=ALU.add))
        do(v.tensor_tensor_scan(self.ends[:, :], self.keep.one[:, 0:e], self.nb[:, :], 0.0, ALU.mult, ALU.add))
        do(v.tensor_tensor(out=self.base[:, :], in0=self.ends[:, :], in1=self.nb[:, :], op=ALU.subtract))
        do(v.tensor_tensor(out=self.off[:, :, :], in0=self.run[:, :, :], in1=self.cnt[:, :, :], op=ALU.subtract))
        do(v.scalar_tensor_tensor(out=self.off[:, :, :], in0=self.base[:, :].unsqueeze(2).to_broadcast([P, e, n]),
                                  scalar=float(P), in1=self.off[:, :, :], op0=ALU.mult, op1=ALU.add))
        do(v.tensor_tensor(out=self.off[:, :, :], in0=above, in1=self.off[:, :, :], op=ALU.add))
        do(v.tensor_tensor(out=self.off[:, :, :], in0=self.off[:, :, :], in1=self.pick[:, :, :], op=ALU.mult))
        do(v.tensor_reduce(out=self.posf[:, :], in_=self.off[:, :, :].rearrange("p e n -> p n e"), axis=AX.X, op=ALU.add))
        do(v.tensor_copy(pos, self.posf[:, :]))
        b = self.b
        do(v.tensor_tensor(out=self.bcmp[:, :, :],
                           in0=self.keep.number[:, 0:b].unsqueeze(2).to_broadcast([P, b, e - 1]),
                           in1=self.ends[:, 0:e - 1].unsqueeze(1).to_broadcast([P, b, e - 1]), op=ALU.is_ge))
        do(v.tensor_reduce(out=self.exf[:, :], in_=self.bcmp[:, :, :], axis=AX.X, op=ALU.add))
        do(v.tensor_copy(ex, self.exf[:, :]))


def setup_block(nc, ext, keep):
    with ExitStack() as ctx:
        def sb(name, shape, dt=F32):
            return ctx.enter_context(nc.sbuf_tensor(name, shape, dt))

        def sem(name):
            return ctx.enter_context(nc.semaphore(name))

        ids = sb("ids", [P, NT], I32)
        idf = sb("idf", [P, NT])
        eid = sb("eid", [P, NT])
        sort = Sorter(sb, keep, "sb", EX_B, NT, NB_B)
        ps = ctx.enter_context(nc.psum_tensor("rank_ps", [P, 512], F32))
        s_ids, s_pool, s_chain = sem("ids_loaded"), sem("setup_constants"), sem("setup_chain")
        s_pick, s_rank = sem("setup_pick_ready"), sem("setup_rank_ready")
        block = ctx.enter_context(nc.Block())

        @block.sync
        def _(sp):
            sp.dma_start(ids[:, :], ext["ids"]).then_inc(s_ids, 16)
            sp.dma_start(keep.x1[:, 0:TB, :], ext["x"].rearrange("(t p) d -> p t d", p=P)[:, 0:TB, :]).then_inc(keep.s_x0, 16)

        @block.gpsimd
        def _(pool):
            g = nc.gpsimd
            g.memset(keep.ident[:, :], 0.0).then_inc(s_pool, 1)
            g.memset(keep.upper[:, :], 1.0).then_inc(s_pool, 1)
            g.memset(keep.ones[:, :], 1.0).then_inc(s_pool, 1)
            g.memset(keep.one[:, :], 1.0).then_inc(s_pool, 1)
            g.memset(keep.pad[:, :], 0.0).then_inc(s_pool, 1)
            g.iota(keep.full[:, :], [[P, NT]], base=0, channel_multiplier=0,
                   allow_small_or_imprecise_dtypes=True).then_inc(s_pool, 1)
            g.iota(keep.number[:, :], [[1, NB_C]], base=0, channel_multiplier=0,
                   allow_small_or_imprecise_dtypes=True).then_inc(s_pool, 1)
            g.iota(keep.token[:, :], [[P, NT]], base=0, channel_multiplier=1).then_inc(s_pool, 1)
            pool.wait_ge(s_pool, 8)
            g.iota(keep.pad[:, DIM:DIM + 1].bitcast(I32), [[0, 1]], base=TOKENS, channel_multiplier=1).then_inc(s_pool, 1)
            g.affine_select(out=keep.ident[:, :], in_=keep.ident[:, :], compare_op=ALU.not_equal, fill=1.0, base=0,
                            pattern=[[-1, P]], channel_multiplier=1).then_inc(s_pool, 1)
            g.affine_select(out=keep.upper[:, :], in_=keep.upper[:, :], compare_op=ALU.is_gt, fill=0.0, base=0,
                            pattern=[[1, P]], channel_multiplier=-1).then_inc(s_pool, 1)
            pool.wait_ge(s_pool, 11)

        @block.vector
        def _(dve):
            v = nc.vector
            do = Chain(dve, s_chain)
            dve.wait_ge(s_ids, 16)
            do(v.tensor_copy(idf[:, :], ids[:, :]))
            step = VOCAB // EX_B
            do(v.tensor_scalar(out=eid[:, :], in0=idf[:, :], scalar1=float(step), scalar2=None, op0=ALU.is_ge))
            for i in range(2, EX_B):
                do(v.scalar_tensor_tensor(out=eid[:, :], in0=idf[:, :], scalar=float(i * step), in1=eid[:, :],
                                          op0=ALU.is_ge, op1=ALU.add))
            for i in range(EX_B):
                do(v.tensor_scalar(out=sort.pick[:, i, :], in0=eid[:, :], scalar1=float(i), scalar2=None, op0=ALU.is_equal))
            v.tensor_copy(sort.pickb[:, :, :], sort.pick[:, :, :]).then_inc(s_pick, 1)
            dve.wait_ge(s_rank, 1)
            sort.on_vector(v, do, ps, keep.pos_b[:, :], keep.ex_b[:, :])

        @block.tensor
        def _(pe):
            pe.wait_ge(s_pool, 11)
            pe.wait_ge(s_pick, 1)
            sort.on_tensor(nc.tensor, ps).then_inc(s_rank, 1)


class Experts:

    def __init__(self, nc, ctx, keep, name, w1, w2, left, right, width):
        def sb(n, shape, dt=F32):
            return ctx.enter_context(nc.sbuf_tensor(f"{name}_{n}", shape, dt))

        def sem(n):
            return ctx.enter_context(nc.semaphore(f"{name}_{n}"))

        def ps(n):
            return ctx.enter_context(nc.psum_tensor(f"{name}_{n}", [P, 512], F32))

        self.nc, self.keep, self.w1, self.w2 = nc, keep, w1, w2
        self.left, self.right = left, right
        self.hid = left[1] - left[0]
        self.kc = self.hid // P
        self.rows = [sb(f"rows{p}", [P, width]) for p in range(2)]
        self.xT = sb("xT", [P, 2, DC, P])
        self.sil = sb("sil", [P, 2, self.hid])
        self.a = sb("a", [P, 2, self.hid])
        self.aT = sb("aT", [P, 2, self.kc, P])
        self.y = [sb(f"y{p}", [P, DIM]) for p in range(2)]
        self.TX, self.HB = [ps(f"TX{p}") for p in range(2)], [ps(f"H{p}") for p in range(2)]
        self.TA, self.YB = ps("TA"), [ps(f"Y{p}") for p in range(2)]
        self.loaded = [sem(f"rows_loaded{p}") for p in range(2)]
        self.s_T, self.s_H, self.s_sil = sem("rows_transposed"), sem("first_product"), sem("silu_ready")
        self.s_xT = sem("xT_ready")
        self.s_a = sem("act_ready")
        self.s_T2 = sem("act_transposed")
        self.s_aT = sem("aT_ready")
        self.s_Y = sem("second_product")
        self.s_yf = sem("product_taken")

    def start(self, pe):
        for s, n in ((self.s_xT, 2), (self.s_a, 2), (self.s_T2, 2), (self.s_aT, 1), (self.s_Y, 2), (self.s_yf, 2)):
            pe.sem_inc(s, n)

    def T(self, pe, it, p):
        j = it * 2 + p
        pe.wait_ge(self.loaded[p], it * 16 + 16)
        pe.wait_ge(self.s_xT, j + 1)
        for c in range(DC):
            last = self.nc.tensor.transpose(self.TX[p][:, c * P:(c + 1) * P], self.rows[p][:, c * P:(c + 1) * P],
                                            self.keep.ident[:, :])
        last.then_inc(self.s_T, 1)

    def weights(self, w, e, c):
        if isinstance(e, int):
            return w[:, e, c, :]
        return w[:, bass.ds(e, 1), c, :].rearrange("p a n -> p (a n)")

    def H(self, pe, it, p, e):
        j = it * 2 + p
        pe.wait_ge(self.s_xT, j + 3)
        pe.wait_ge(self.s_a, j + 1)
        for c in range(DC):
            last = self.nc.tensor.matmul(self.HB[p][:, :], self.xT[:, p, c, :], self.weights(self.w1, e, c),
                                         start=(c == 0), stop=(c == DC - 1))
        last.then_inc(self.s_H, 1)

    def T2(self, pe, it, p):
        j = it * 2 + p
        pe.wait_ge(self.s_a, j + 3)
        pe.wait_ge(self.s_aT, j + 1)
        for c in range(self.kc):
            last = self.nc.tensor.transpose(self.TA[:, c * P:(c + 1) * P], self.a[:, p, c * P:(c + 1) * P],
                                            self.keep.ident[:, :])
        last.then_inc(self.s_T2, 1)

    def Y(self, pe, it, p, e):
        j = it * 2 + p
        pe.wait_ge(self.s_aT, j + 2)
        pe.wait_ge(self.s_yf, j + 1)
        for c in range(self.kc):
            last = self.nc.tensor.matmul(self.YB[p][:, :], self.aT[:, p, c, :], self.weights(self.w2, e, c),
                                         start=(c == 0), stop=(c == self.kc - 1))
        last.then_inc(self.s_Y, 1)

    def copy_xT(self, act, it, p):
        j = it * 2 + p
        act.wait_ge(self.s_T, j + 1)
        self.nc.scalar.copy(self.xT[:, p, :, :], self.TX[p][:, :].rearrange("p (c q) -> p c q", c=DC)).then_inc(self.s_xT, 1)

    def silu(self, act, it, p):
        j = it * 2 + p
        act.wait_ge(self.s_H, j + 1)
        act.wait_ge(self.s_a, j + 1)
        self.nc.scalar.activation(self.sil[:, p, :], self.HB[p][:, self.left[0]:self.left[1]], ACT.Silu).then_inc(self.s_sil, 1)

    def copy_aT(self, act, it, p):
        j = it * 2 + p
        act.wait_ge(self.s_T2, j + 3)
        act.wait_ge(self.s_Y, j + 1)
        self.nc.scalar.copy(self.aT[:, p, :, :],
                            self.TA[:, 0:self.hid].rearrange("p (c q) -> p c q", c=self.kc)).then_inc(self.s_aT, 1)

    def copy_y(self, act, it, p):
        j = it * 2 + p
        act.wait_ge(self.s_Y, j + 3)
        self.nc.scalar.copy(self.y[p][:, :], self.YB[p][:, :]).then_inc(self.s_yf, 1)

    def product(self, dve, it, p):
        j = it * 2 + p
        dve.wait_ge(self.s_sil, j + 1)
        dve.wait_ge(self.s_T2, j + 1)
        self.nc.vector.tensor_tensor(out=self.a[:, p, :], in0=self.HB[p][:, self.right[0]:self.right[1]],
                                     in1=self.sil[:, p, :], op=ALU.mult).then_inc(self.s_a, 1)


def load_c_weights(sp, ext, keep):
    for dst, src in ((keep.w13, "w13"), (keep.w2, "w2"), (keep.gate, "gate")):
        sp.dma_start(dst.ap(), ext[src]).then_inc(keep.s_wc, 16)


def id_expert_block(nc, ext, keep):
    with ExitStack() as ctx:
        ctxT = keep.arena[:, :].rearrange("p (e c n) -> p e c n", e=EX_B, c=DC)
        ex = Experts(nc, ctx, keep, "b", ctxT, ctxT, (0, DIM), (0, DIM), DIM)
        stored = [ctx.enter_context(nc.semaphore(f"b_stored{p}")) for p in range(2)]
        block = ctx.enter_context(nc.Block())
        PAIRS = NB_B // 2
        LAST = NB_B - 1
        xs = keep.xs_b.rearrange("(n p) d -> n p d", p=P)
        ys = keep.ys_b.rearrange("(n p) d -> n p d", p=P)

        def at(view, j):
            return view[j, :, :] if isinstance(j, int) else view[bass.ds(j, 1), :, :].rearrange("a p d -> (a p) d")

        @block.sync
        def _(sp):
            for p in range(2):
                sp.dma_start(ex.rows[p][:, :], at(xs, p)).then_inc(ex.loaded[p], 16)
            load_c_weights(sp, ext, keep)
            with sp.Fori(0, PAIRS - 1) as it:
                for p in range(2):
                    sp.wait_ge(ex.s_T, it * 2 + p + 1)
                    sp.dma_start(ex.rows[p][:, :], at(xs, it * 2 + p + 2)).then_inc(ex.loaded[p], 16)
            sp.wait_ge(ex.s_T, LAST - 1)
            sp.dma_start(ex.rows[0][:, :], at(xs, LAST)).then_inc(ex.loaded[0], 16)

        @block.scalar
        def _(act):
            def y_out(it, p):
                if not (isinstance(it, int) and it == 0):
                    act.wait_ge(stored[p], it * 16)
                ex.copy_y(act, it, p)
                act.wait_ge(ex.s_yf, it * 2 + p + 3)
                act.dma_start(at(ys, it * 2 + p), ex.y[p][:, :]).then_inc(stored[p], 16)

            def pair(it):
                for p in range(2):
                    nit, np_ = (it, 1) if p == 0 else (it + 1, 0)
                    ex.copy_xT(act, nit, np_)
                    ex.copy_aT(act, it, p)
                    ex.silu(act, nit, np_)
                    y_out(it, p)

            ex.copy_xT(act, 0, 0)
            ex.silu(act, 0, 0)
            pair(0)
            with act.Fori(1, PAIRS) as it:
                pair(it)
            ex.copy_aT(act, PAIRS, 0)
            y_out(PAIRS, 0)
            act.wait_ge(stored[0], (PAIRS + 1) * 16)
            act.wait_ge(stored[1], PAIRS * 16)

        @block.vector
        def _(dve):
            ex.product(dve, 0, 0)
            with dve.Fori(0, PAIRS) as it:
                ex.product(dve, it, 1)
                ex.product(dve, it + 1, 0)

        @block.tensor
        def _(pe):
            def expert(j):
                e = keep.ex_b[0:1, j:j + 1] if isinstance(j, int) else keep.ex_b[0:1, bass.ds(j, 1)]
                return pe.value_load(e, min_val=0, max_val=EX_B - 1)

            ex.start(pe)
            ex.T(pe, 0, 0)
            pe.wait_ge(keep.s_ctx, 16)
            ex.H(pe, 0, 0, expert(0))
            with pe.Fori(0, PAIRS) as it:
                for p in range(2):
                    nit, np_ = (it, 1) if p == 0 else (it + 1, 0)
                    ex.T(pe, nit, np_)
                    ex.T2(pe, it, p)
                    ex.H(pe, nit, np_, expert(it * 2 + p + 1))
                    ex.Y(pe, it, p, expert(it * 2 + p))
            ex.T2(pe, PAIRS, 0)
            ex.Y(pe, PAIRS, 0, expert(LAST))


def weights_c(nc, ctx, keep):
    keep.w13 = ctx.enter_context(nc.sbuf_tensor("w13", [P, EX_C + 1, DC, 2 * HID], F32))
    keep.w2 = ctx.enter_context(nc.sbuf_tensor("w2", [P, EX_C + 1, HID // P, DIM], F32))
    keep.gate = ctx.enter_context(nc.sbuf_tensor("gate", [P, DC, EX_C], F32))
    keep.s_wc = ctx.enter_context(nc.semaphore("c_weights_loaded"))


def gate_block(nc, ext, keep):
    x2 = keep.x1
    with ExitStack() as ctx:
        def sb(name, shape, dt=F32):
            return ctx.enter_context(nc.sbuf_tensor(name, shape, dt))

        def sem(name):
            return ctx.enter_context(nc.semaphore(name))

        def part(k):
            n = TB * DIM
            return keep.arena[:, k * n:(k + 1) * n].rearrange("p (t d) -> p t d", t=TB)

        yg, xn, xT = part(0), part(1), part(2)
        pos_cur = sb("gpos_cur", [P, TB], I32)
        st = sb("gst", [P, TB, 6])
        mv = sb("gmv", [P, TB, 2])
        var = sb("gvar", [P, TB])
        rstd = sb("grstd", [P, TB])
        half = sb("ghalf", [P, TB])
        epsc = sb("gepsc", [P, TB])
        lg = sb("logits", [EX_C, TB * P])
        sc = sb("scores", [P, TB, EX_C])
        best = sb("best", [P, TB, 8])
        besti = sb("besti", [P, TB, 8], U32)
        chosen = sb("chosen", [P, TOPK, NT])
        sort = Sorter(sb, keep, "sc", EX_C, NT * TOPK, NB_C)
        xb = [ctx.enter_context(nc.psum_tensor(f"gx{c}", [P, 512], F32)) for c in range(DC)]
        lps = ctx.enter_context(nc.psum_tensor("glogits", [P, 512], F32))
        tps = ctx.enter_context(nc.psum_tensor("gscores", [P, 512], F32))
        rps = ctx.enter_context(nc.psum_tensor("granks", [P, 512], F32))
        s_cst = sem("gate_constants")
        s_pos, s_g = sem("gate_positions"), [sem(f"gathered{r}") for r in range(TB)]
        s_x2 = sem("x2_ready")
        s_ch = sem("gate_chain")
        s_mv, s_var, s_rstd = sem("stats3_ready"), sem("var3_ready"), sem("rstd3_ready")
        s_xn = sem("xn3_ready")
        s_st = sem("xn3_stored")
        s_tx = sem("xn3_transposed")
        s_xT = sem("xT3_ready")
        s_lg, s_lc, s_lt = sem("logits_summed"), sem("logits_copied"), sem("logits_transposed")
        s_ex = sem("exp_ready")
        s_tk = sem("scores_taken")
        s_pick, s_rank = sem("gate_pick_ready"), sem("gate_rank_ready")
        s_aux = sem("gate_unused_count")
        block = ctx.enter_context(nc.Block())

        @block.sync
        def _(sp):
            sp.sem_inc(s_st, 16)
            view = keep.xn_c.rearrange("(q t p) d -> q p t d", p=P, t=TB)
            with sp.Fori(0, BATCH) as q:
                sp.wait_ge(s_xn, q * TB + TB)
                sp.sem_inc(s_aux, 1)
                sp.dma_start(view[bass.ds(q, 1), :, :, :].rearrange("a p t d -> p (a t) d"), xn).then_inc(s_st, 16)
            sp.wait_ge(s_st, 16 + 16 * BATCH)

        @block.gpsimd
        def _(pool):
            g = nc.gpsimd
            g.memset(half[:, :], -0.5).then_inc(s_cst, 1)
            g.memset(epsc[:, :], EPS).then_inc(s_cst, 1)
            pool.wait_ge(s_cst, 2)

            def gather(q):
                if not (isinstance(q, int) and q == 0):
                    for r in range(TB):
                        pool.wait_ge(s_g[r], q * 16)
                    pool.sem_inc(s_aux, 1)
                g.tensor_copy(pos_cur[:, :], keep.pos_b[:, bass.ds(q * TB, TB)]).then_inc(s_pos, 1)
                pool.wait_ge(s_pos, q + 1)
                for r in range(TB):
                    pool.wait_ge(s_x2, q * TB + r + 1)
                    pool.sem_inc(s_aux, 1)
                    g.indirect_dma_start(out=yg[:, r, :], out_offset=None, in_=keep.ys_b,
                                         in_offset=bass.IndirectOffsetOnAxis(ap=pos_cur[:, r:r + 1].bitcast(U32), axis=0)
                                         ).then_inc(s_g[r], 16)

            def inverse_root(q):
                pool.wait_ge(s_mv, q * TB + TB)
                g.tensor_tensor(out=var[:, :], in0=mv[:, :, 1], in1=epsc[:, :], op=ALU.add).then_inc(s_var, 1)
                pool.wait_ge(s_var, q + 1)
                g.tensor_tensor(out=rstd[:, :], in0=var[:, :], in1=half[:, :], op=ALU.pow).then_inc(s_rstd, 1)

            pool.wait_ge(s_x2, TB)
            gather(0)
            with pool.Fori(0, BATCH - 1) as q:
                gather(q + 1)
                inverse_root(q)
            inverse_root(BATCH - 1)

        @block.vector
        def _(dve):
            v = nc.vector
            dve.sem_inc(s_x2, TB)
            dve.sem_inc(s_tk, 12)

            def rows(q, r):
                return x2[:, bass.ds(q * TB + r, 1), :].rearrange("p a d -> p (a d)")

            def quarter(ap, q):
                return ap[:, bass.ds(q * TB, TB)]

            with dve.Fori(0, BATCH) as q:
                for r in range(TB):
                    dve.wait_ge(s_g[r], q * 16 + 16)
                    v.tensor_tensor(out=rows(q, r), in0=rows(q, r), in1=yg[:, r, :], op=ALU.add).then_inc(s_x2, 1)
                for r in range(TB):
                    dve.wait_ge(s_x2, q * TB + TB + r + 1)
                    dve.sem_inc(s_aux, 1)
                    v.bn_stats(st[:, r, :], rows(q, r)).then_inc(s_ch, 1)
                for r in range(TB):
                    dve.wait_ge(s_ch, q * TB + r + 1)
                    dve.sem_inc(s_aux, 1)
                    v.bn_aggr(mv[:, r, :], st[:, r, :]).then_inc(s_mv, 1)
                dve.wait_ge(s_st, q * 16 + 16)
                dve.sem_inc(s_aux, 1)
                dve.wait_ge(s_rstd, q + 1)
                for r in range(TB):
                    v.tensor_scalar(out=xn[:, r, :], in0=rows(q, r), scalar1=mv[:, r, 0:1], scalar2=rstd[:, r:r + 1],
                                    op0=ALU.subtract, op1=ALU.mult).then_inc(s_xn, 1)
                v.tensor_copy(quarter(keep.mean, q), mv[:, :, 0]).then_inc(s_aux, 1)
                v.tensor_copy(quarter(keep.rstd, q), rstd[:, :]).then_inc(s_aux, 1)
                dve.wait_ge(s_ex, q + 2)
                v.tensor_scalar(out=sc[:, :, :], in0=sc[:, :, :], scalar1=1.0, scalar2=None, op0=ALU.add).then_inc(s_tk, 1)
                dve.wait_ge(s_tk, q * 12 + 13)
                v.reciprocal(sc[:, :, :], sc[:, :, :]).then_inc(s_tk, 1)
                dve.wait_ge(s_tk, q * 12 + 14)
                dve.sem_inc(s_aux, 1)
                for r in range(TB):
                    v.max(best[:, r, :], sc[:, r, :]).then_inc(s_tk, 1)
                dve.wait_ge(s_tk, q * 12 + 18)
                dve.sem_inc(s_aux, 1)
                for r in range(TB):
                    v.max_index(besti[:, r, :], best[:, r, :], sc[:, r, :]).then_inc(s_tk, 1)
                dve.wait_ge(s_tk, q * 12 + 22)
                v.tensor_copy(keep.score[:, :, bass.ds(q * TB, TB)],
                              best[:, :, 0:TOPK].rearrange("p r k -> p k r")).then_inc(s_tk, 1)
                v.tensor_copy(chosen[:, :, bass.ds(q * TB, TB)],
                              besti[:, :, 0:TOPK].rearrange("p r k -> p k r")).then_inc(s_tk, 1)
            dve.wait_ge(s_tk, 12 * BATCH + 12)
            do = Chain(dve, s_pick)
            for e in range(EX_C):
                do(v.tensor_scalar(out=sort.pick[:, e, :], in0=chosen[:, :, :].rearrange("p k n -> p (k n)"),
                                   scalar1=float(e), scalar2=None, op0=ALU.is_equal))
            do(v.tensor_copy(sort.pickb[:, :, :], sort.pick[:, :, :]))
            dve.wait_ge(s_rank, 1)
            sort.on_vector(v, do, rps, keep.pos_c[:, :], keep.ex_c[:, :])

        @block.scalar
        def _(act):
            a = nc.scalar
            act.sem_inc(s_ex, 1)
            with act.Fori(0, BATCH) as q:
                for c in range(DC):
                    act.wait_ge(s_tx, q * DC + c + 1)
                    a.copy(xT[:, c, :], xb[c][:, :]).then_inc(s_xT, 1)
                act.wait_ge(s_lg, q + 1)
                a.copy(lg[:, :], lps[0:EX_C, :]).then_inc(s_lc, 1)
                act.wait_ge(s_lt, q + 1)
                act.wait_ge(s_tk, q * 12 + 12)
                a.activation(sc[:, :, :], tps[:, 0:TB * EX_C].rearrange("p (t e) -> p t e", e=EX_C), ACT.Exp,
                             scale=-1.0).then_inc(s_ex, 1)

        @block.tensor
        def _(pe):
            te = nc.tensor
            pe.wait_ge(keep.s_wc, 48)
            with pe.Fori(0, BATCH) as q:
                pe.wait_ge(s_xn, q * TB + TB)
                for c in range(DC):
                    for r in range(TB):
                        last = te.transpose(xb[c][:, r * P:(r + 1) * P], xn[:, r, c * P:(c + 1) * P], keep.ident[:, :])
                    last.then_inc(s_tx, 1)
                pe.wait_ge(s_xT, q * DC + DC)
                for c in range(DC):
                    last = te.matmul(lps[0:EX_C, :], keep.gate[:, c, :], xT[:, c, :], start=(c == 0), stop=(c == DC - 1))
                last.then_inc(s_lg, 1)
                pe.wait_ge(s_lc, q + 1)
                pe.wait_ge(s_ex, q + 1)
                pe.sem_inc(s_aux, 1)
                for r in range(TB):
                    last = te.transpose(tps[:, r * EX_C:(r + 1) * EX_C], lg[:, r * P:(r + 1) * P],
                                        keep.ident[0:EX_C, 0:EX_C])
                last.then_inc(s_lt, 1)
            pe.wait_ge(s_pick, EX_C + 1)
            sort.on_tensor(te, rps).then_inc(s_rank, 1)


def gate_expert_block(nc, ext, keep):
    x2 = keep.x1
    SHARED = EX_C
    S_PAIRS = NT // 2
    R_PAIRS = NB_C // 2
    LAST = S_PAIRS + R_PAIRS
    STEP = TB * TOPK
    with ExitStack() as ctx:
        def sb(name, shape, dt=F32):
            return ctx.enter_context(nc.sbuf_tensor(name, shape, dt))

        def sem(name):
            return ctx.enter_context(nc.semaphore(name))

        ex = Experts(nc, ctx, keep, "c", keep.w13, keep.w2, (0, HID), (HID, 2 * HID), ROW)
        stage = keep.arena[:, 0:STEP * ROW].rearrange("p (k t w) -> p k t w", w=ROW, t=TB)
        gain = sb("gain", [P, TOPK, NT])
        mean_cur = sb("mean_cur", [P, TB])
        gain_cur = sb("gain_cur", [P, TOPK, TB])
        slot_cur = sb("slot_cur", [P, TOPK, TB], I32)
        row_id = [sb(f"row_id{p}", [P, 1], I32) for p in range(2)]
        s_gain, s_cur = sem("gains_ready"), sem("gains_current")
        s_stage = sem("scaled_rows_ready")
        s_slot, s_sc = sem("slots_current"), keep.s_xs_c
        s_x3 = sem("shared_added")
        s_base = sem("base_rows_stored")
        s_id = sem("row_ids_copied")
        s_add = keep.s_add
        s_left = sem("y_buffer_steps")
        s_aux = sem("c_unused_count")
        block = ctx.enter_context(nc.Block())

        def at(view, j):
            return view[bass.ds(j, 1), :, :].rearrange("a p d -> (a p) d")

        @block.sync
        def _(sp):
            xn = keep.xn_c.rearrange("(n p) d -> n p d", p=P)
            xs = keep.xs_c.rearrange("(n p) d -> n p d", p=P)
            out = keep.out[0:TOKENS, :].rearrange("(n t p) d -> n p t d", p=P, t=2)
            for p in range(2):
                sp.dma_start(ex.rows[p][:, 0:DIM], at(xn, p)).then_inc(ex.loaded[p], 16)

            def store(it):
                sp.wait_ge(s_x3, it * 2 + 2)
                sp.sem_inc(s_aux, 1)
                sp.dma_start(out[bass.ds(it, 1), :, :, :].rearrange("a p t d -> p (a t) d"),
                             x2[:, bass.ds(it * 2, 2), :]).then_inc(s_base, 16)

            with sp.Fori(0, S_PAIRS - 1) as it:
                for p in range(2):
                    sp.wait_ge(ex.s_T, it * 2 + p + 1)
                    sp.sem_inc(s_aux, 1)
                    sp.dma_start(ex.rows[p][:, 0:DIM], at(xn, it * 2 + p + 2)).then_inc(ex.loaded[p], 16)
                store(it)
            sp.wait_ge(s_sc, 16 * TOPK * NT + 16)
            for p in range(2):
                sp.wait_ge(ex.s_T, S_PAIRS * 2 - 2 + p + 1)
                sp.dma_start(ex.rows[p][:, :], at(xs, p)).then_inc(ex.loaded[p], 16)
            store(S_PAIRS - 1)

            def load_routed(m, p):
                sp.wait_ge(ex.s_T, m + (2 * S_PAIRS - 1))
                sp.sem_inc(s_aux, 1)
                sp.wait_ge(s_id, m - 1)
                sp.sem_inc(s_aux, 1)
                sp.dma_start(ex.rows[p][:, :], at(xs, m)).then_inc(ex.loaded[p], 16)

            with sp.Fori(0, R_PAIRS - 1) as r:
                for p in range(2):
                    load_routed(r * 2 + (p + 2), p)
            load_routed(NB_C - 1, 0)

        @block.gpsimd
        def _(pool):
            g = nc.gpsimd
            pool.sem_inc(s_left, 1)
            with pool.Fori(0, BATCH) as q:
                pool.wait_ge(s_sc, q * (16 * STEP) + 16)
                pool.sem_inc(s_aux, 1)
                g.tensor_copy(slot_cur[:, :, :], keep.pos_c[:, :].rearrange("p (k n) -> p k n", k=TOPK)[:, :, bass.ds(q * TB, TB)]).then_inc(s_slot, 1)
                pool.wait_ge(s_slot, q + 1)
                for k in range(TOPK):
                    for t in range(TB):
                        pool.wait_ge(s_stage, q * (STEP + 1) + k * TB + t + 2)
                        pool.sem_inc(s_aux, 1)
                        g.indirect_dma_start(out=keep.xs_c, out_offset=bass.IndirectOffsetOnAxis(ap=slot_cur[:, k, t:t + 1].bitcast(U32), axis=0),
                                             in_=stage[:, k, t, :], in_offset=None).then_inc(s_sc, 16)
            pool.wait_ge(s_base, 16 * S_PAIRS)

            def add(it, m, p):
                pool.wait_ge(ex.loaded[p], it * 16 + 16)
                pool.wait_ge(s_add, m * 16 + 16)
                pool.sem_inc(s_left, 1)
                g.tensor_copy(row_id[p][:, :], ex.rows[p][:, DIM:DIM + 1].bitcast(I32)).then_inc(s_id, 1)
                pool.wait_ge(s_id, m + 1)
                pool.wait_ge(ex.s_yf, m + (2 * S_PAIRS + 3))
                pool.sem_inc(s_aux, 1)
                g.indirect_dma_start(out=keep.out, out_offset=bass.IndirectOffsetOnAxis(ap=row_id[p][:, 0:1].bitcast(U32), axis=0),
                                     in_=ex.y[p][:, :], in_offset=None, compute_op=ALU.add).then_inc(s_add, 16)

            with pool.Fori(0, R_PAIRS) as r:
                for p in range(2):
                    add(r + S_PAIRS, r * 2 + p, p)
            add(LAST, NB_C - 1, 0)
            pool.wait_ge(s_add, 16 * NB_C + 16)

        @block.vector
        def _(dve):
            v = nc.vector

            def rows(n):
                return x2[:, bass.ds(n, 1), :].rearrange("p a d -> p (a d)")

            def scale(q, k, t):
                v.tensor_scalar(out=stage[:, k, t, 0:DIM], in0=rows(q * TB + t), scalar1=mean_cur[:, t:t + 1],
                                scalar2=gain_cur[:, k, t:t + 1], op0=ALU.subtract, op1=ALU.mult).then_inc(s_stage, 1)

            def add_shared(it, p):
                j = it * 2 + p
                dve.wait_ge(ex.s_Y, j + 3)
                v.tensor_tensor(out=rows(j), in0=ex.YB[p][:, :], in1=rows(j), op=ALU.add).then_inc(s_x3, 1)
                dve.wait_ge(s_x3, j + 1)
                dve.sem_inc(ex.s_yf, 1)

            v.tensor_tensor(out=gain[:, :, :], in0=keep.score[:, :, :], in1=keep.rstd[:, :].unsqueeze(1).to_broadcast([P, TOPK, NT]),
                            op=ALU.mult).then_inc(s_gain, 1)
            dve.wait_ge(s_gain, 1)
            ex.product(dve, 0, 0)
            with dve.Fori(0, BATCH) as q:
                v.tensor_copy(mean_cur[:, :], keep.mean[:, bass.ds(q * TB, TB)]).then_inc(s_cur, 1)
                v.tensor_copy(gain_cur[:, :, :], gain[:, :, bass.ds(q * TB, TB)]).then_inc(s_cur, 1)
                dve.wait_ge(s_sc, q * (16 * STEP) + 16)
                v.tensor_copy(stage[:, :, :, DIM:DIM + 1].bitcast(I32).rearrange("p k t w -> p k (t w)"),
                              keep.token[:, bass.ds(q * TB, TB)].unsqueeze(1).to_broadcast([P, TOPK, TB])).then_inc(s_stage, 1)
                dve.wait_ge(s_cur, q * 2 + 2)
                for t in range(TB):
                    scale(q, 0, t)
                ex.product(dve, q, 1)
                for t in range(TB):
                    scale(q, 1, t)
                add_shared(q, 0)
                ex.product(dve, q + 1, 0)
                add_shared(q, 1)
            with dve.Fori(BATCH, S_PAIRS) as it:
                ex.product(dve, it, 1)
                add_shared(it, 0)
                ex.product(dve, it + 1, 0)
                add_shared(it, 1)
            with dve.Fori(S_PAIRS, LAST) as it:
                ex.product(dve, it, 1)
                ex.product(dve, it + 1, 0)

        @block.scalar
        def _(act):
            def y_out(it, p):
                j = it * 2 + p
                act.wait_ge(s_left, j - (2 * S_PAIRS - 1))
                ex.copy_y(act, it, p)

            def pair(it, routed):
                for p in range(2):
                    nit, np_ = (it, 1) if p == 0 else (it + 1, 0)
                    ex.copy_xT(act, nit, np_)
                    ex.copy_aT(act, it, p)
                    ex.silu(act, nit, np_)
                    if routed:
                        y_out(it, p)

            ex.copy_xT(act, 0, 0)
            ex.silu(act, 0, 0)
            with act.Fori(0, S_PAIRS) as it:
                pair(it, False)
            act.wait_ge(s_x3, 2 * S_PAIRS)
            with act.Fori(S_PAIRS, LAST) as it:
                pair(it, True)
            ex.copy_aT(act, LAST, 0)
            y_out(LAST, 0)

        @block.tensor
        def _(pe):
            def expert(m):
                e = keep.ex_c[0:1, m:m + 1] if isinstance(m, int) else keep.ex_c[0:1, bass.ds(m, 1)]
                return pe.value_load(e, min_val=0, max_val=EX_C - 1)

            def step(it, p, e_next, e):
                nit, np_ = (it, 1) if p == 0 else (it + 1, 0)
                ex.T(pe, nit, np_)
                ex.T2(pe, it, p)
                ex.H(pe, nit, np_, e_next())
                ex.Y(pe, it, p, e())

            def shared():
                return SHARED

            ex.start(pe)
            ex.T(pe, 0, 0)
            ex.H(pe, 0, 0, SHARED)
            with pe.Fori(0, S_PAIRS - 1) as it:
                for p in range(2):
                    step(it, p, shared, shared)
            step(S_PAIRS - 1, 0, shared, shared)
            step(S_PAIRS - 1, 1, lambda: expert(0), shared)
            with pe.Fori(0, R_PAIRS) as r:
                for p in range(2):
                    step(r + S_PAIRS, p, lambda: expert(r * 2 + (p + 1)), lambda: expert(r * 2 + p))
            ex.T2(pe, LAST, 0)
            ex.Y(pe, LAST, 0, expert(NB_C - 1))


def build(nc, ext):
    with ExitStack() as ctx:
        keep = Keep(nc, ctx, ext)
        setup_block(nc, ext, keep)
        attention_block(nc, ext, keep)
        weights_c(nc, ctx, keep)
        id_expert_block(nc, ext, keep)
        gate_block(nc, ext, keep)
        gate_expert_block(nc, ext, keep)


def _layout(np, x, itok_BxS_13_99985, ctx_2048, L0_attn_Wqa, L0_attn_Wqb, L0_attn_Wkva, L0_attn_Wkvb, L0_attn_Wo,
            L0_ffn_gate_w, L0_ffn_w1, L0_ffn_w2, L0_ffn_w3, L0_ffn_ws1, L0_ffn_ws2, L0_ffn_ws3):
    def rows(w):
        return w.reshape(w.shape[0] // P, P, w.shape[1]).transpose(1, 0, 2)

    def experts(ws):
        return np.stack([rows(w) for w in ws], axis=1)

    pe = L0_attn_Wkva[:, LORA:]
    even, odd = pe[:, 0::2], pe[:, 1::2]
    wqb = L0_attn_Wqb.reshape(LORA, NG, GROUP, QK)
    wqb = [wqb[..., NOPE::2], wqb[..., NOPE + 1::2], wqb[..., :NOPE]]
    wkvb = L0_attn_Wkvb.reshape(LORA, HEADS, NOPE + VD)

    freq = np.float32(10000.0) ** (-np.arange(0, ROPE, 2, dtype=np.float32) / np.float32(ROPE))
    angle = (np.arange(SEQ, dtype=np.float32)[:, None] * freq[None, :]).astype(np.float64).T
    cos, sin = np.cos(angle), np.sin(angle)
    return {
        "x": x.reshape(TOKENS, DIM),
        "ids": itok_BxS_13_99985.reshape(NT, P).T,
        "wqa": rows(L0_attn_Wqa),
        "wkva": rows(np.concatenate([L0_attn_Wkva[:, :LORA], even, odd, odd, even], axis=1)),
        "wqb": np.stack(wqb, axis=2).reshape(LORA, NG * 3, P),
        "wk": wkvb[..., :NOPE].reshape(LORA, NG, P),
        "wv": wkvb[..., NOPE:].reshape(LORA, HEADS * VD),
        "wo": rows(L0_attn_Wo),
        "cos4": np.tile(cos * QK ** -0.5, (GROUP, 1)).astype(np.float32),
        "sin4": np.tile(sin * QK ** -0.5, (GROUP, 1)).astype(np.float32),
        "kcs": np.concatenate([cos, cos, -sin, sin]).astype(np.float32),
        "ctxT": experts([w.T for w in ctx_2048]).reshape(P, EX_B * DC * DIM),
        "w13": experts([np.concatenate([a.T, b.T], axis=1) for a, b in
                        zip([*L0_ffn_w1, L0_ffn_ws1], [*L0_ffn_w3, L0_ffn_ws3])]),
        "w2": experts([w.T for w in [*L0_ffn_w2, L0_ffn_ws2]]),
        "gate": rows(L0_ffn_gate_w.T),
    }


def kernel(**inputs):
    import numpy as _np
    import concourse.bacc as _bacc
    from concourse.bass_utils import run_bass_kernel_spmd as _run

    laid = _layout(_np, **{name: _np.asarray(a) for name, a in inputs.items()})
    nc = _bacc.Bacc("TRN2", target_bir_lowering=False, num_devices=1)
    arrays, ext = {}, {}
    for name, a in laid.items():
        a = _np.ascontiguousarray(a)
        arrays[f"in_{name}"] = a
        ext[name] = nc.dram_tensor(f"in_{name}", a.shape, mybir.dt.from_np(a.dtype), kind="ExternalInput").ap()
    ext["out"] = nc.dram_tensor("out", (TOKENS + P, DIM), F32, kind="ExternalOutput").ap()
    build(nc, ext)
    r = _run(nc, [arrays], core_ids=[0])
    return r.results[0]["out"][:TOKENS].reshape(BATCH, SEQ, DIM)
```

```python
from contextlib import ExitStack

import concourse.bass as bass
from concourse import mybir

F32 = mybir.dt.float32
BF16 = mybir.dt.bfloat16
I32 = mybir.dt.int32
U32 = mybir.dt.uint32
ALU = mybir.AluOpType
ACT = mybir.ActivationFunctionType
AX = mybir.AxisListType

P = 128
BATCH, SEQ, DIM = 4, 512, 512
TOKENS = BATCH * SEQ
NT = TOKENS // P
TB = SEQ // P
DC = DIM // P
HEADS, NOPE, ROPE = 16, 32, 64
HALF = ROPE // 2
QK = NOPE + ROPE
VD = DIM // HEADS
LORA = 128
GROUP = P // NOPE
NG = HEADS // GROUP
LEAD = 4
UNITS = HEADS * TB
EPS = 1e-5
MASKED = -1e30

EX_B, VOCAB = 4, 25000
EX_C, TOPK, HID = 8, 2, 256
NB_B = NT + EX_B - 1
NB_C = NT * TOPK + EX_C - 1


class AttentionPlan:

    WORK = (0, 1, 2, 6)
    PT = (3, 4)
    OUT = 5
    PROJ = 7

    def __init__(self):
        self.tiles = {}
        self.uses = {s: [0] * 8 for s in ("pro", "units", "epi")}
        pro = [("xT", c) for c in range(DC)] + [("qa",), ("ckv",)]
        pro += [(k, 0) for k in "EONK"] + [("kpe",)] + [("V", t) for t in range(TB)]
        for n, name in enumerate(pro):
            self.take("pro", name, self.WORK[n % LEAD])
        for u in range(UNITS):
            self.take("units", ("S", u), self.WORK[u % LEAD])
            self.take("units", ("PT", u), self.PT[u % 2])
        for g in range(NG):
            self.take("units", ("out", g), self.OUT)
        for g in range(NG):
            for k in "EONK" * (g + 1 < NG):
                self.take("units", (k, g + 1), self.PROJ)
            if g > 0:
                self.take("units", ("R", g - 1), self.PROJ)
        epi = [("R", NG - 1)] + [("Wo", t) for t in range(TB)]
        for n, name in enumerate(epi):
            self.take("epi", name, self.WORK[n % LEAD])

    def take(self, section, name, bank):
        self.tiles[section, name] = (bank, self.uses[section][bank])
        self.uses[section][bank] += 1

    def place(self, section, name, b):
        bank, nth = self.tiles[section, name]
        p, u, e = (self.uses[s][bank] for s in ("pro", "units", "epi"))
        first = isinstance(b, int) and b == 0
        last = isinstance(b, int) and b == BATCH - 1
        if section == "pro":
            before = 0 if first else (b - 1) * (p + u + e) + (p + u)
        elif section == "units":
            before = b * (p + u + e) + p
        else:
            before = b * (p + u + e) + (p + u) + (0 if last else p)
        return bank, before + nth


def attention_block(nc, ext, keep):
    plan = AttentionPlan()
    x1, ident, pos_b, xs_b = keep.x1, keep.ident, keep.pos_b, keep.xs_b
    s_x0, s_xr = keep.s_x0, keep.s_xr
    with ExitStack() as ctx:
        def sb(name, shape, dt=F32):
            return ctx.enter_context(nc.sbuf_tensor(name, shape, dt))

        def sem(name):
            return ctx.enter_context(nc.semaphore(name))

        wqa = sb("wqa", [P, DC, LORA])
        wkva = sb("wkva", [P, DC, LORA + 2 * ROPE])
        wqb = sb("wqb", [P, NG * 3, P])
        wk = sb("wk", [P, NG, P])
        wv = sb("wv", [P, HEADS * VD])
        wo = sb("wo", [P, DC, DIM])
        cos4 = sb("cos4", [P, SEQ])
        sin4 = sb("sin4", [P, SEQ])
        kcs = sb("kcs", [P, SEQ])
        identb = sb("identb", [P, P], BF16)
        maskb = sb("maskb", [P, P], BF16)
        half = sb("half", [P, TB])
        epsc = sb("epsc", [P, TB])
        st1 = sb("st1", [P, TB, 6])
        mv1 = sb("mv1", [P, TB, 2])
        var1 = sb("var1", [P, TB])
        rstd1 = sb("rstd1", [P, TB])
        st2 = sb("st2", [P, TB, 6])
        mv2 = sb("mv2", [P, TB, 2])
        var2 = sb("var2", [P, TB])
        rstd2 = sb("rstd2", [P, TB])
        xn = sb("xn", [P, TB, DIM])
        xT = sb("xT", [P, DC, SEQ])
        qaT = sb("qaT", [P, SEQ])
        cT = sb("cT", [P, SEQ])
        rot = sb("rot", [P, 4, SEQ])
        rEO = sb("rEO", [P, 2, SEQ])
        QT = sb("QT", [QK, 2 * GROUP, SEQ])
        KT = sb("KT", [QK, 2 * GROUP, SEQ])
        V = sb("V", [P, TB, DIM])
        negmax = sb("negmax", [P, 2 * LEAD])
        probs = sb("probs", [P, LEAD, SEQ])
        PTs = sb("PTs", [P, 2, GROUP, SEQ])
        kpt = PTs[0:ROPE, 0, 0:2, :]
        sums = sb("sums", [P, 2, TB, GROUP])
        rinv = sb("rinv", [P, TB * GROUP])
        rsum = sb("rsum", [P, TB * GROUP, VD])
        osb = sb("osb", [P, SEQ])
        OT = sb("OT", [P, DC, SEQ])
        xo = xn
        pos_cur = sb("pos_cur", [P, TB], I32)
        pad = sb("pad", [P, ROW])
        bank = [ctx.enter_context(nc.psum_tensor(f"bank{k}", [P, 512], F32)) for k in range(8)]

        filled = [sem(f"filled{k}") for k in range(8)]
        free = [sem(f"free{k}") for k in range(8)]
        s_wp = sem("proj_weights_loaded")
        s_wo = sem("wo_loaded")
        s_cst = sem("constants_ready")
        s_ones = sem("ones_ready")
        s_mv1, s_rs1, s_xn = sem("stats1_ready"), sem("rstd1_ready"), sem("xn_ready")
        s_mv2, s_rs2, s_xo = sem("stats2_ready"), sem("rstd2_ready"), sem("xn2_ready")
        s_p1, s_p2 = sem("pool_var1"), sem("pool_var2")
        s_c1, s_c2, s_c3 = sem("dve_ln1"), sem("dve_ln2"), sem("dve_norm")
        s_rot, s_rope, s_nk = sem("rot_products_ready"), sem("rotated_ready"), sem("nk_ready")
        s_qk = sem("qk_loaded")
        s_kpt, s_kpe = sem("kpe_products_ready"), sem("kpe_ready")
        s_kr = sem("kpe_repeated")
        s_nm, s_exp = sem("negmax_ready"), sem("probs_ready")
        s_rs = sem("sums_inverted")
        s_rb = sem("inverses_repeated")
        s_oc = sem("group_out_copied")
        s_on = sem("group_out_ready")
        s_scat = keep.s_xs_b
        s_pc = sem("positions_copied")
        s_pad = sem("pad_ready")
        s_aux = sem("unused_count")
        block = ctx.enter_context(nc.Block())
        QK_DMAS = 2 * GROUP
        PROJ_STEP = {0: "E", 2: "O", 4: "N", 8: "K"}

        LN2_AT = (1, 3, 5, 7)

        R_STEP = 11

        def steps():
            for s in range(-LEAD, UNITS):
                yield s

        def proj_at(s):
            if s >= 0 and (s % 16) in PROJ_STEP and s // 16 + 1 < NG:
                return PROJ_STEP[s % 16], s // 16 + 1
            return None

        def inverted_at(s):
            return s // 16 - 1 if s >= 16 and s % 16 == R_STEP else None

        def quad_at(s):
            return (s - 2) // 4 if s >= 5 and s % 4 == 1 else None

        def unit(u):
            return u // 16, (u % 16) // GROUP, u % GROUP

        def evac_pt_by_act(u):
            return u % GROUP == GROUP - 1

        @block.sync
        def _(sp):
            for dst, src in ((wqa, "wqa"), (wkva, "wkva"), (wqb, "wqb"), (wk, "wk"), (wv, "wv"),
                             (cos4, "cos4"), (sin4, "sin4"), (kcs, "kcs")):
                sp.dma_start(dst.ap(), ext[src]).then_inc(s_wp, 16)

            def group(b, g):
                n = b * NG + g
                sp.wait_ge(s_rope, n * 2 + 2 + 2)
                for j in range(GROUP):
                    slot = (g % 2) * GROUP + j
                    rows = slice(j * 32, j * 32 + 32)
                    sp.dma_start(QT[0:32, slot, :], rEO[rows, 0, :]).then_inc(s_qk, 16)
                    sp.dma_start(QT[32:64, slot, :], rEO[rows, 1, :]).then_inc(s_qk, 16)

            def repeat_kpe(b):
                sp.wait_ge(s_kpe, b + 2)
                sp.dma_start(KT[0:ROPE, 1:2 * GROUP, :],
                             KT[0:ROPE, 0:1, :].to_broadcast([ROPE, 2 * GROUP - 1, SEQ])).then_inc(s_kr, 16)

            group(0, 0)
            repeat_kpe(0)
            load_rest_of_x(sp, ext, keep)
            sp.dma_start(wo.ap(), ext["wo"]).then_inc(s_wo, 16)
            sp.wait_ge(s_pad, 2)
            clear_b(sp, keep, pad)
            with sp.Fori(0, BATCH - 1) as b:
                for g in range(1, NG):
                    group(b, g)
                group(b + 1, 0)
                repeat_kpe(b + 1)
            for g in range(1, NG):
                group(BATCH - 1, g)

        @block.gpsimd
        def _(pool):
            g = nc.gpsimd
            pool.sem_inc(s_rope, 2)
            pool.sem_inc(s_rb, 1)
            pool.sem_inc(s_kpe, 1)
            pool.sem_inc(s_qk, 16 * QK_DMAS)
            g.memset(half.ap(), -0.5).then_inc(s_cst, 1)
            g.memset(epsc.ap(), EPS).then_inc(s_ones, 1)
            g.memset(identb.ap(), 0.0).then_inc(s_cst, 1)
            g.memset(maskb.ap(), 0.0).then_inc(s_cst, 1)
            pool.wait_ge(s_cst, 3)
            pool.wait_ge(s_ones, 1)
            g.affine_select(out=identb.ap(), in_=identb.ap(), compare_op=ALU.not_equal, fill=1.0, base=0,
                            pattern=[[-1, P]], channel_multiplier=1).then_inc(s_cst, 1)
            g.affine_select(out=maskb.ap(), in_=maskb.ap(), compare_op=ALU.is_ge, fill=MASKED, base=0,
                            pattern=[[-1, P]], channel_multiplier=1).then_inc(s_cst, 1)

            def inverse_root(b, mv, var, rstd, s_mv, s_step, s_out):
                pool.wait_ge(s_mv, b * TB + TB)
                g.tensor_tensor(out=var.ap(), in0=mv[:, :, 1], in1=epsc.ap(), op=ALU.add).then_inc(s_step, 1)
                pool.wait_ge(s_step, b + 1)
                g.tensor_tensor(out=rstd.ap(), in0=var.ap(), in1=half.ap(), op=ALU.pow).then_inc(s_out, 1)

            def rope_sums(b, gi):
                n = b * NG + gi
                pool.wait_ge(s_rot, n * 4 + 4)
                pool.wait_ge(s_qk, n * (16 * QK_DMAS) + 16 * QK_DMAS)
                g.tensor_tensor(out=rEO[:, 0, :], in0=rot[:, 0, :], in1=rot[:, 2, :], op=ALU.subtract).then_inc(s_rope, 1)
                g.tensor_tensor(out=rEO[:, 1, :], in0=rot[:, 1, :], in1=rot[:, 3, :], op=ALU.add).then_inc(s_rope, 1)

            def pro(b):
                rope_sums(b, 0)
                pool.wait_ge(s_kpt, b * 2 + 2)
                g.tensor_tensor(out=KT[0:ROPE, 0, :], in0=kpt[:, 0, :], in1=kpt[:, 1, :], op=ALU.add).then_inc(s_kpe, 1)

            def repeat(b, gi):
                n = b * NG + gi
                pool.wait_ge(s_rs, n + 3)
                pool.wait_ge(s_on, n + 1)
                pool.sem_inc(s_aux, 1)
                g.tensor_copy(rsum[:, :, :], rinv[:, :].unsqueeze(2).to_broadcast([P, TB * GROUP, VD])).then_inc(s_rb, 1)

            def units(b, more, before):
                for gi in range(1, NG):
                    rope_sums(b, gi)
                    if gi == 1 and before is not None:
                        scatter(before)
                    if gi > 1:
                        repeat(b, gi - 2)
                    if gi == 2 and more:
                        inverse_root(b + 1, mv1, var1, rstd1, s_mv1, s_p1, s_rs1)
                repeat(b, NG - 2)
                repeat(b, NG - 1)

            def epi(b):
                inverse_root(b, mv2, var2, rstd2, s_mv2, s_p2, s_rs2)

            def scatter(b):
                pool.wait_ge(s_scat, b * (16 * TB) + 16)
                pool.sem_inc(s_aux, 1)
                g.tensor_copy(pos_cur[:, :], pos_b[:, bass.ds(b * TB, TB)]).then_inc(s_pc, 1)
                for t in range(TB):
                    pool.wait_ge(keep.s_clr_b, 16)
                    pool.wait_ge(s_pc, b + 1)
                    pool.sem_inc(s_aux, 1)
                    pool.wait_ge(s_xo, b * TB + t + 1)
                    pool.sem_inc(s_aux, 1)
                    g.indirect_dma_start(out=xs_b, out_offset=bass.IndirectOffsetOnAxis(ap=pos_cur[:, t:t + 1].bitcast(U32), axis=0),
                                         in_=xo[:, t, :], in_offset=None).then_inc(s_scat, 16)

            g.memset(pad[:, :], 0.0).then_inc(s_pad, 1)
            pool.wait_ge(s_pad, 1)
            g.iota(pad[:, DIM:DIM + 1].bitcast(I32), [[0, 1]], base=TOKENS, channel_multiplier=1).then_inc(s_pad, 1)
            pool.wait_ge(s_pad, 2)
            clear_first(pool, keep, pad)
            inverse_root(0, mv1, var1, rstd1, s_mv1, s_p1, s_rs1)
            pro(0)
            units(0, True, None)
            with pool.Fori(0, BATCH - 2) as b:
                pro(b + 1)
                epi(b)
                units(b + 1, True, b)
            pro(BATCH - 1)
            epi(BATCH - 2)
            units(BATCH - 1, False, BATCH - 2)
            epi(BATCH - 1)
            scatter(BATCH - 1)
            pool.wait_ge(s_scat, BATCH * (16 * TB) + 16)

        @block.vector
        def _(dve):
            v = nc.vector
            for k in range(8):
                dve.sem_inc(free[k], 1)
            dve.sem_inc(s_rs, 2)
            dve.sem_inc(s_on, 1)

            def tile(section, name, b):
                k, n = plan.place(section, name, b)
                dve.wait_ge(filled[k], n + 1)
                return bank[k], free[k]

            def rows(b, t):
                return x1[:, bass.ds(b * TB + t, 1), :].rearrange("p a d -> p (a d)")

            def stats(b, t, src, st, mv, s_chain, s_out, before, per):
                v.bn_stats(st[:, t, :], src).then_inc(s_chain, 1)
                dve.wait_ge(s_chain, b * per + before + 1)
                dve.sem_inc(s_aux, 1)
                v.bn_aggr(mv[:, t, :], st[:, t, :]).then_inc(s_out, 1)

            def ln1_stats(b, t):
                stats(b, t, rows(b, t), st1, mv1, s_c1, s_mv1, t, TB)

            def ln1_norm(b, t):
                if t == 0:
                    if not isinstance(b, int):
                        dve.wait_ge(s_scat, b * (16 * TB) - (16 * TB - 16))
                        dve.sem_inc(s_aux, 1)
                    dve.wait_ge(s_rs1, b + 1)
                v.tensor_scalar(out=xn[:, t, :], in0=rows(b, t), scalar1=mv1[:, t, 0:1], scalar2=rstd1[:, t:t + 1],
                                op0=ALU.subtract, op1=ALU.mult).then_inc(s_xn, 1)

            def rope_products(section, kind, b, g):
                n = b * NG + g
                ps, done = tile(section, (kind, g), b)
                if kind == "E":
                    dve.wait_ge(s_rope, n * 2 + 2)
                    v.tensor_tensor(out=rot[:, 0, :], in0=ps[:, :], in1=cos4[:, :], op=ALU.mult).then_inc(s_rot, 1)
                    v.tensor_tensor(out=rot[:, 1, :], in0=ps[:, :], in1=sin4[:, :], op=ALU.mult).then_inc(s_rot, 1)
                    dve.wait_ge(s_rot, n * 4 + 2)
                else:
                    v.tensor_tensor(out=rot[:, 2, :], in0=ps[:, :], in1=sin4[:, :], op=ALU.mult).then_inc(s_rot, 1)
                    v.tensor_tensor(out=rot[:, 3, :], in0=ps[:, :], in1=cos4[:, :], op=ALU.mult).then_inc(s_rot, 1)
                    dve.wait_ge(s_rot, n * 4 + 4)
                dve.sem_inc(done, 1)

            def pro(b):
                for c in range(1, DC, 2):
                    ps, done = tile("pro", ("xT", c), b)
                    v.tensor_copy(xT[:, c, :], ps[:, :]).then_inc(done, 1)
                rope_products("pro", "E", b, 0)
                rope_products("pro", "O", b, 0)
                ps, done = tile("pro", ("kpe",), b)
                dve.wait_ge(s_kpe, b + 1)
                v.tensor_tensor(out=kpt[:, 0, :], in0=ps[0:ROPE, :], in1=kcs[0:ROPE, :], op=ALU.mult).then_inc(s_kpt, 1)
                v.tensor_tensor(out=kpt[:, 1, :], in0=ps[ROPE:P, :], in1=kcs[ROPE:P, :], op=ALU.mult).then_inc(s_kpt, 1)
                dve.wait_ge(s_kpt, b * 2 + 2)
                dve.sem_inc(done, 1)
                for t in range(1, TB, 2):
                    ps, done = tile("pro", ("V", t), b)
                    v.tensor_copy(V[:, t, :], ps[:, :]).then_inc(done, 1)

            def neg_max(b, u):
                _, i, _ = unit(u)
                ps, _ = tile("units", ("S", u), b)
                if u >= 2 * LEAD:
                    dve.wait_ge(s_exp, b * UNITS + u - 2 * LEAD + 1)
                v.tensor_reduce(out=negmax[:, u % (2 * LEAD):u % (2 * LEAD) + 1], in_=ps[:, 0:(i + 1) * P], axis=AX.X, op=ALU.max,
                                negate=True).then_inc(s_nm, 1)

            def evac_pt(b, u):
                _, i, j = unit(u)
                ps, done = tile("units", ("PT", u), b)
                v.tensor_copy(PTs[:, (u // GROUP) % 2, j, 0:(i + 1) * P], ps[:, 0:(i + 1) * P]).then_inc(done, 1)

            def invert(b, g):
                n = b * NG + g
                dve.wait_ge(s_exp, b * UNITS + (g + 1) * 16)
                dve.wait_ge(s_rb, n + 1)
                v.reciprocal(rinv[:, :], sums[:, g % 2, :, :].rearrange("p t j -> p (t j)")).then_inc(s_rs, 1)

            def group_out(section, b, g):
                n = b * NG + g
                ps, done = tile(section, ("R", g), b)
                dve.wait_ge(s_oc, n + 1)
                v.tensor_tensor(out=OT[:, g, :], in0=ps[:, :], in1=osb[:, :], op=ALU.mult).then_inc(s_on, 1)
                dve.wait_ge(s_on, n + 2)
                dve.sem_inc(done, 1)

            def units(b, more, before):
                for s in steps():
                    if s + LEAD < UNITS:
                        neg_max(b, s + LEAD)
                    p = proj_at(s)
                    if p and p[0] in "EO":
                        rope_products("units", p[0], b, p[1])
                    if 0 <= s + 1 < UNITS and not evac_pt_by_act(s + 1):
                        evac_pt(b, s + 1)
                    if inverted_at(s + 5) is not None:
                        invert(b, inverted_at(s + 5))
                    if inverted_at(s) is not None:
                        group_out("units", b, inverted_at(s))
                    if before is not None and s in LN2_AT:
                        ln2_norm(before, LN2_AT.index(s))
                    if more and s == 20:
                        dve.wait_ge(s_xr, 16)
                    if more and s in (20, 24, 28, 32):
                        ln1_stats(b + 1, (s - 20) // 4)
                    if more and s in (48, 50, 52, 54):
                        ln1_norm(b + 1, (s - 48) // 2)
                invert(b, NG - 1)

            def epi(b):
                group_out("epi", b, NG - 1)
                for t in range(TB):
                    ps, done = tile("epi", ("Wo", t), b)
                    v.tensor_tensor(out=rows(b, t), in0=ps[:, :], in1=rows(b, t), op=ALU.add).then_inc(s_c2, 1)
                    dve.wait_ge(s_c2, b * (2 * TB) + 2 * t + 1)
                    dve.sem_inc(done, 1)
                    v.bn_stats(st2[:, t, :], rows(b, t)).then_inc(s_c2, 1)
                    dve.wait_ge(s_c2, b * (2 * TB) + 2 * t + 2)
                    dve.sem_inc(s_aux, 1)
                    v.bn_aggr(mv2[:, t, :], st2[:, t, :]).then_inc(s_mv2, 1)

            def ln2_norm(b, t):
                if t == 0:
                    dve.wait_ge(s_scat, b * (16 * TB) + 16)
                    dve.sem_inc(s_aux, 1)
                    dve.wait_ge(s_rs2, b + 1)
                v.tensor_scalar(out=xo[:, t, :], in0=rows(b, t), scalar1=mv2[:, t, 0:1], scalar2=rstd2[:, t:t + 1],
                                op0=ALU.subtract, op1=ALU.mult).then_inc(s_xo, 1)

            dve.wait_ge(s_x0, 16)
            for t in range(TB):
                ln1_stats(0, t)
            for t in range(TB):
                ln1_norm(0, t)
            dve.wait_ge(s_wp, 16 * 8)
            pro(0)
            units(0, True, None)
            with dve.Fori(0, BATCH - 2) as b:
                pro(b + 1)
                epi(b)
                units(b + 1, True, b)
            pro(BATCH - 1)
            epi(BATCH - 2)
            units(BATCH - 1, False, BATCH - 2)
            epi(BATCH - 1)
            for t in range(TB):
                ln2_norm(BATCH - 1, t)

        @block.scalar
        def _(act):
            a = nc.scalar

            def tile(section, name, b):
                k, n = plan.place(section, name, b)
                act.wait_ge(filled[k], n + 1)
                return bank[k], free[k]

            def evac_nk(section, kind, b, g, heads=range(GROUP)):
                n = b * NG + g
                ps, done = tile(section, (kind, g), b)
                for j in heads:
                    rows = slice(j * NOPE, (j + 1) * NOPE)
                    dst = (QT if kind == "N" else KT)[ROPE:QK, (g % 2) * GROUP + j, :]
                    a.activation(dst, ps[rows, :], ACT.Copy, scale=QK ** -0.5 if kind == "N" else 1.0).then_inc(s_nk, 1)
                if GROUP - 1 not in heads:
                    return
                act.wait_ge(s_nk, n * (2 * GROUP) + (GROUP if kind == "N" else 2 * GROUP))
                act.sem_inc(done, 1)

            def pro(b):
                for c in range(0, DC, 2):
                    ps, done = tile("pro", ("xT", c), b)
                    a.copy(xT[:, c, :], ps[:, :]).then_inc(done, 1)
                for name, dst in (("qa", qaT), ("ckv", cT)):
                    ps, done = tile("pro", (name,), b)
                    a.copy(dst[:, :], ps[:, :]).then_inc(done, 1)
                evac_nk("pro", "N", b, 0)
                evac_nk("pro", "K", b, 0)
                for t in range(0, TB, 2):
                    ps, done = tile("pro", ("V", t), b)
                    a.copy(V[:, t, :], ps[:, :]).then_inc(done, 1)

            def exps(b, u):
                g, i, j = unit(u)
                if u % 16 == 0:
                    act.wait_ge(s_rs, b * NG + g + 1)
                act.wait_ge(s_nm, b * UNITS + u + 1)
                ps, done = tile("units", ("S", u), b)
                if u >= LEAD:
                    k, n = plan.place("units", ("PT", u - LEAD), b)
                    act.wait_ge(filled[k], n + 1)
                a.activation(probs[:, u % LEAD, 0:(i + 1) * P], ps[:, 0:(i + 1) * P], ACT.Exp,
                             bias=negmax[:, u % (2 * LEAD):u % (2 * LEAD) + 1], accum_out=sums[:, g % 2, i, j:j + 1]).then_inc(s_exp, 1)
                act.wait_ge(s_exp, b * UNITS + u + 1)
                act.sem_inc(done, 1)

            def copy_out(b, g):
                n = b * NG + g
                ps, done = tile("units", ("out", g), b)
                act.wait_ge(s_on, n + 1)
                a.copy(osb[:, :], ps[:, :]).then_inc(s_oc, 1)
                act.wait_ge(s_oc, n + 1)
                act.sem_inc(done, 1)

            def units(b, more):
                for s in steps():
                    if more and s > 0 and s % 4 == 0 and s // 4 <= CLEARS_C:
                        clear_c(act, keep, pad, b * CLEARS_C + (s // 4 - 1))
                    if s + LEAD < UNITS:
                        exps(b, s + LEAD)
                    p = proj_at(s)
                    if p and p[0] in "NK":
                        evac_nk("units", p[0], b, p[1], range(0, GROUP // 2))
                    p = proj_at(s - 1)
                    if p and p[0] in "NK":
                        evac_nk("units", p[0], b, p[1], range(GROUP // 2, GROUP))
                    if 0 <= s + 1 < UNITS and evac_pt_by_act(s + 1):
                        _, i, j = unit(s + 1)
                        ps, done = tile("units", ("PT", s + 1), b)
                        a.copy(PTs[:, ((s + 1) // GROUP) % 2, j, 0:(i + 1) * P], ps[:, 0:(i + 1) * P]).then_inc(done, 1)
                    q = quad_at(s)
                    if q is not None and q % TB == TB - 1:
                        copy_out(b, q // TB)
                copy_out(b, NG - 1)

            pro(0)
            act.wait_ge(s_pad, 2)
            with act.Fori(0, BATCH - 1) as b:
                units(b, True)
                pro(b + 1)
            act.dma_start(keep.arena[:, :], ext["ctxT"]).then_inc(keep.s_ctx, 16)
            units(BATCH - 1, False)

        @block.tensor
        def _(pe):
            te = nc.tensor

            def tile(section, name, b):
                k, n = plan.place(section, name, b)
                pe.wait_ge(free[k], n + 1)
                return bank[k], filled[k]

            def evacuated(section, name, b):
                k, n = plan.place(section, name, b)
                pe.wait_ge(free[k], n + 2)

            def mul(out, pairs, done):
                for n, (l, r) in enumerate(pairs):
                    last = te.matmul(out, l, r, start=(n == 0), stop=(n == len(pairs) - 1))
                last.then_inc(done, 1)

            def project(section, kind, b, g):
                ps, done = tile(section, (kind, g), b)
                w, src = {"E": (wqb[:, 3 * g, :], qaT), "O": (wqb[:, 3 * g + 1, :], qaT),
                          "N": (wqb[:, 3 * g + 2, :], qaT), "K": (wk[:, g, :], cT)}[kind]
                mul(ps[:, :], [(w, src[:, :])], done)

            def pro(b):
                pe.wait_ge(s_xn, b * TB + TB)
                for c in range(DC):
                    ps, done = tile("pro", ("xT", c), b)
                    for t in range(TB):
                        last = te.transpose(ps[:, t * P:(t + 1) * P], xn[:, t, c * P:(c + 1) * P], ident[:, :])
                    last.then_inc(done, 1)
                for c in range(DC):
                    evacuated("pro", ("xT", c), b)
                for name, w in (("qa", wqa[:, :, :]), ("ckv", wkva[:, :, 0:LORA])):
                    ps, done = tile("pro", (name,), b)
                    mul(ps[:, :], [(w[:, c, :], xT[:, c, :]) for c in range(DC)], done)
                evacuated("pro", ("qa",), b)
                for kind in "EON":
                    project("pro", kind, b, 0)
                evacuated("pro", ("ckv",), b)
                project("pro", "K", b, 0)
                ps, done = tile("pro", ("kpe",), b)
                mul(ps[:, :], [(wkva[:, c, LORA:], xT[:, c, :]) for c in range(DC)], done)
                for t in range(TB):
                    ps, done = tile("pro", ("V", t), b)
                    mul(ps[:, :], [(cT[:, t * P:(t + 1) * P], wv[:, :])], done)

            def scores(b, u):
                g, i, j = unit(u)
                slot = (g % 2) * GROUP + j
                if u % 16 == 0:
                    n = b * NG + g
                    pe.wait_ge(s_qk, n * (16 * QK_DMAS) + 2 * (16 * QK_DMAS))
                    pe.wait_ge(s_nk, n * (2 * GROUP) + 2 * GROUP)
                ps, done = tile("units", ("S", u), b)
                te.matmul(ps[:, 0:(i + 1) * P], QT[:, slot, i * P:(i + 1) * P], KT[:, slot, 0:(i + 1) * P],
                          start=True, stop=False)
                te.matmul(ps[:, i * P:(i + 1) * P], identb[:, :], maskb[:, :], start=False, stop=True).then_inc(done, 1)

            def transposes(b, u):
                _, i, _ = unit(u)
                pe.wait_ge(s_exp, b * UNITS + u + 1)
                ps, done = tile("units", ("PT", u), b)
                for j in range(i + 1):
                    last = te.transpose(ps[:, j * P:(j + 1) * P], probs[:, u % LEAD, j * P:(j + 1) * P], ident[:, :])
                last.then_inc(done, 1)

            def values(b, q):
                g, i = q // TB, q % TB
                for u in range(q * GROUP + 2, q * GROUP + GROUP):
                    evacuated("units", ("PT", u), b)
                if i == 0:
                    tile("units", ("out", g), b)
                k, _ = plan.place("units", ("out", g), b)
                for j in range(i + 1):
                    for h in range(GROUP):
                        last = te.matmul(bank[k][h * VD:(h + 1) * VD, i * P:(i + 1) * P],
                                         V[:, j, (g * GROUP + h) * VD:(g * GROUP + h + 1) * VD],
                                         PTs[:, q % 2, h, j * P:(j + 1) * P], start=(j == 0), stop=(j == i))
                if i == TB - 1:
                    last.then_inc(filled[k], 1)

            def spread(section, b, g):
                pe.wait_ge(s_rb, b * NG + g + 2)
                ps, done = tile(section, ("R", g), b)
                for i in range(TB):
                    last = te.transpose(ps[:, i * P:(i + 1) * P],
                                        rsum[:, i * GROUP:(i + 1) * GROUP, :].rearrange("p j d -> p (j d)"), ident[:, :])
                last.then_inc(done, 1)

            def units(b):
                pe.wait_ge(s_kr, b * 16 + 16)
                for t in range(TB):
                    evacuated("pro", ("V", t), b)
                for s in steps():
                    if s + LEAD < UNITS:
                        scores(b, s + LEAD)
                    p = proj_at(s)
                    if p:
                        project("units", p[0], b, p[1])
                    if inverted_at(s) is not None:
                        spread("units", b, inverted_at(s))
                    if 0 <= s + 1 < UNITS:
                        transposes(b, s + 1)
                    if quad_at(s) is not None:
                        values(b, quad_at(s))
                values(b, UNITS // GROUP - 1)

            def epi(b):
                pe.wait_ge(s_wo, 16)
                spread("epi", b, NG - 1)
                pe.wait_ge(s_on, b * NG + NG + 1)
                for t in range(TB):
                    ps, done = tile("epi", ("Wo", t), b)
                    mul(ps[:, :], [(OT[:, c, t * P:(t + 1) * P], wo[:, c, :]) for c in range(DC)], done)

            pe.wait_ge(s_wp, 16 * 8)
            pe.wait_ge(s_cst, 5)
            pe.wait_ge(s_ones, 1)
            pro(0)
            with pe.Fori(0, BATCH - 1) as b:
                units(b)
                pro(b + 1)
                epi(b)
            units(BATCH - 1)
            epi(BATCH - 1)


class Keep:

    def __init__(self, nc, ctx, ext):
        def sb(name, shape, dt=F32):
            return ctx.enter_context(nc.sbuf_tensor(name, shape, dt))

        def dram(name, shape):
            return nc.dram_tensor(name, shape, F32, kind="Internal").ap()

        self.x1 = sb("x1", [P, NT, DIM])
        self.ident = sb("ident", [P, P])
        self.arena = sb("arena", [P, EX_B * DC * DIM])
        self.upper = sb("upper", [P, P], BF16)
        self.ones = sb("ones", [P, P], BF16)
        self.full = sb("full", [P, NT])
        self.number = sb("number", [P, NB_C])
        self.one = sb("one", [P, NT * TOPK])
        self.token = sb("token", [P, NT], I32)
        self.pos_b = sb("pos_b", [P, NT], I32)
        self.ex_b = sb("ex_b", [P, NB_B], I32)
        self.xs_b = dram("xs_b", [NB_B * P, DIM])
        self.ys_b = dram("ys_b", [NB_B * P, DIM])
        self.xs_c = dram("xs_c", [NB_C * P, ROW])
        self.s_x0 = ctx.enter_context(nc.semaphore("x_first_loaded"))
        self.s_xr = ctx.enter_context(nc.semaphore("x_rest_loaded"))
        self.s_clr_b = ctx.enter_context(nc.semaphore("xs_b_cleared"))
        self.s_clr_c = ctx.enter_context(nc.semaphore("xs_c_cleared"))
        self.s_xs_b = ctx.enter_context(nc.semaphore("xs_b_written"))
        self.s_xs_c = [ctx.enter_context(nc.semaphore(f"xs_c_written{t}")) for t in range(TB)]
        self.s_add = ctx.enter_context(nc.semaphore("routed_rows_added"))
        self.s_ctx = ctx.enter_context(nc.semaphore("ctx_loaded"))
        self.out = ext["out"]


ROW = 576


def load_rest_of_x(sp, ext, keep):
    xv = ext["x"].rearrange("(t p) d -> p t d", p=P)
    sp.dma_start(keep.x1[:, TB:NT, :], xv[:, TB:NT, :]).then_inc(keep.s_xr, 16)


CLEARS_C = -(-(NB_C - TB) // (BATCH - 1))


def clear_first(pool, keep, pad):
    pool.dma_start(keep.xs_b[(NB_B - 1) * P:, :], pad[:, 0:DIM]).then_inc(keep.s_xs_b, 16)
    for t in range(TB):
        n = NB_C - TB + t
        pool.dma_start(keep.xs_c[n * P:(n + 1) * P, :], pad[:, :]).then_inc(keep.s_xs_c[t], 16)
    pool.dma_start(keep.out[TOKENS:TOKENS + P, :], pad[:, 0:DIM]).then_inc(keep.s_add, 16)


def clear_b(sp, keep, pad):
    sp.dma_start(keep.xs_b[0:(NB_B - 1) * P, :].rearrange("(n p) d -> p n d", p=P),
                 pad[:, 0:DIM].unsqueeze(1).to_broadcast([P, NB_B - 1, DIM])).then_inc(keep.s_clr_b, 16)


def clear_c(eng, keep, pad, n):
    xs = keep.xs_c[0:CLEARS_C * (BATCH - 1) * P, :].rearrange("(n p) d -> n p d", p=P)
    eng.dma_start(xs[bass.ds(n, 1), :, :].rearrange("a p d -> (a p) d"), pad[:, :]).then_inc(keep.s_clr_c, 16)


class Chain:

    def __init__(self, eng, s):
        self.eng, self.s, self.n = eng, s, 0

    def __call__(self, ins):
        self.n += 1
        ins.then_inc(self.s, 1)
        self.eng.wait_ge(self.s, self.n)


class Sorter:

    def __init__(self, sb, keep, name, experts, tiles, blocks):
        self.keep, self.e, self.n, self.b = keep, experts, tiles, blocks
        self.pick = sb(f"{name}_pick", [P, experts, tiles])
        self.pickb = sb(f"{name}_pickb", [P, experts, tiles], BF16)
        self.cnt = sb(f"{name}_cnt", [P, experts, tiles])
        self.run = sb(f"{name}_run", [P, experts, tiles])
        self.cmp = sb(f"{name}_cmp", [P, experts, NT])
        self.nb = sb(f"{name}_nb", [P, experts])
        self.ends = sb(f"{name}_ends", [P, experts])
        self.base = sb(f"{name}_base", [P, experts])
        self.off = sb(f"{name}_off", [P, experts, tiles])
        self.posf = sb(f"{name}_posf", [P, tiles])
        self.bcmp = sb(f"{name}_bcmp", [P, blocks, experts - 1])
        self.exf = sb(f"{name}_exf", [P, blocks])

    def on_tensor(self, te, ps):
        w = self.e * self.n
        flat = self.pickb[:, :, :].rearrange("p e n -> p (e n)")
        te.matmul(ps[:, 0:w], self.keep.upper[:, :], flat, start=True, stop=True)
        return te.matmul(ps[:, w:2 * w], self.keep.ones[:, :], flat, start=True, stop=True)

    def on_vector(self, v, do, ps, pos, ex):
        w, e, n = self.e * self.n, self.e, self.n
        above = ps[:, 0:w].rearrange("p (e n) -> p e n", e=e)
        count = ps[:, w:2 * w].rearrange("p (e n) -> p e n", e=e)
        do(v.tensor_copy(self.cnt[:, :, :], count))
        for i in range(e):
            do(v.tensor_tensor_scan(self.run[:, i, :], self.keep.one[:, 0:n], self.cnt[:, i, :], 0.0,
                                    ALU.mult, ALU.add))
        total = self.run[:, :, n - 1:n]
        do(v.tensor_tensor(out=self.cmp[:, :, :], in0=total.to_broadcast([P, e, NT]),
                           in1=self.keep.full[:, :].unsqueeze(1).to_broadcast([P, e, NT]), op=ALU.is_gt))
        do(v.tensor_reduce(out=self.nb[:, :], in_=self.cmp[:, :, :], axis=AX.X, op=ALU.add))
        do(v.tensor_tensor_scan(self.ends[:, :], self.keep.one[:, 0:e], self.nb[:, :], 0.0, ALU.mult, ALU.add))
        do(v.tensor_tensor(out=self.base[:, :], in0=self.ends[:, :], in1=self.nb[:, :], op=ALU.subtract))
        do(v.tensor_tensor(out=self.off[:, :, :], in0=self.run[:, :, :], in1=self.cnt[:, :, :], op=ALU.subtract))
        do(v.scalar_tensor_tensor(out=self.off[:, :, :], in0=self.base[:, :].unsqueeze(2).to_broadcast([P, e, n]),
                                  scalar=float(P), in1=self.off[:, :, :], op0=ALU.mult, op1=ALU.add))
        do(v.tensor_tensor(out=self.off[:, :, :], in0=above, in1=self.off[:, :, :], op=ALU.add))
        do(v.tensor_tensor(out=self.off[:, :, :], in0=self.off[:, :, :], in1=self.pick[:, :, :], op=ALU.mult))
        do(v.tensor_reduce(out=self.posf[:, :], in_=self.off[:, :, :].rearrange("p e n -> p n e"), axis=AX.X, op=ALU.add))
        do(v.tensor_copy(pos, self.posf[:, :]))
        b = self.b
        do(v.tensor_tensor(out=self.bcmp[:, :, :],
                           in0=self.keep.number[:, 0:b].unsqueeze(2).to_broadcast([P, b, e - 1]),
                           in1=self.ends[:, 0:e - 1].unsqueeze(1).to_broadcast([P, b, e - 1]), op=ALU.is_ge))
        do(v.tensor_reduce(out=self.exf[:, :], in_=self.bcmp[:, :, :], axis=AX.X, op=ALU.add))
        do(v.tensor_copy(ex, self.exf[:, :]))


def setup_block(nc, ext, keep):
    with ExitStack() as ctx:
        def sb(name, shape, dt=F32):
            return ctx.enter_context(nc.sbuf_tensor(name, shape, dt))

        def sem(name):
            return ctx.enter_context(nc.semaphore(name))

        ids = sb("ids", [P, NT], I32)
        idf = sb("idf", [P, NT])
        eid = sb("eid", [P, NT])
        sort = Sorter(sb, keep, "sb", EX_B, NT, NB_B)
        ps = ctx.enter_context(nc.psum_tensor("rank_ps", [P, 512], F32))
        s_ids, s_pool, s_chain = sem("ids_loaded"), sem("setup_constants"), sem("setup_chain")
        s_pick, s_rank = sem("setup_pick_ready"), sem("setup_rank_ready")
        block = ctx.enter_context(nc.Block())

        @block.sync
        def _(sp):
            sp.dma_start(ids[:, :], ext["ids"]).then_inc(s_ids, 16)
            sp.dma_start(keep.x1[:, 0:TB, :], ext["x"].rearrange("(t p) d -> p t d", p=P)[:, 0:TB, :]).then_inc(keep.s_x0, 16)

        @block.gpsimd
        def _(pool):
            g = nc.gpsimd
            g.memset(keep.ident[:, :], 0.0).then_inc(s_pool, 1)
            g.memset(keep.upper[:, :], 1.0).then_inc(s_pool, 1)
            g.memset(keep.ones[:, :], 1.0).then_inc(s_pool, 1)
            g.memset(keep.one[:, :], 1.0).then_inc(s_pool, 1)
            g.iota(keep.full[:, :], [[P, NT]], base=0, channel_multiplier=0,
                   allow_small_or_imprecise_dtypes=True).then_inc(s_pool, 1)
            g.iota(keep.number[:, :], [[1, NB_C]], base=0, channel_multiplier=0,
                   allow_small_or_imprecise_dtypes=True).then_inc(s_pool, 1)
            g.iota(keep.token[:, :], [[P, NT]], base=0, channel_multiplier=1).then_inc(s_pool, 1)
            pool.wait_ge(s_pool, 7)
            g.affine_select(out=keep.ident[:, :], in_=keep.ident[:, :], compare_op=ALU.not_equal, fill=1.0, base=0,
                            pattern=[[-1, P]], channel_multiplier=1).then_inc(s_pool, 1)
            g.affine_select(out=keep.upper[:, :], in_=keep.upper[:, :], compare_op=ALU.is_gt, fill=0.0, base=0,
                            pattern=[[1, P]], channel_multiplier=-1).then_inc(s_pool, 1)
            pool.wait_ge(s_pool, 9)

        @block.vector
        def _(dve):
            v = nc.vector
            do = Chain(dve, s_chain)
            dve.wait_ge(s_ids, 16)
            do(v.tensor_copy(idf[:, :], ids[:, :]))
            step = VOCAB // EX_B
            do(v.tensor_scalar(out=eid[:, :], in0=idf[:, :], scalar1=float(step), scalar2=None, op0=ALU.is_ge))
            for i in range(2, EX_B):
                do(v.scalar_tensor_tensor(out=eid[:, :], in0=idf[:, :], scalar=float(i * step), in1=eid[:, :],
                                          op0=ALU.is_ge, op1=ALU.add))
            for i in range(EX_B):
                do(v.tensor_scalar(out=sort.pick[:, i, :], in0=eid[:, :], scalar1=float(i), scalar2=None, op0=ALU.is_equal))
            v.tensor_copy(sort.pickb[:, :, :], sort.pick[:, :, :]).then_inc(s_pick, 1)
            dve.wait_ge(s_rank, 1)
            sort.on_vector(v, do, ps, keep.pos_b[:, :], keep.ex_b[:, :])

        @block.tensor
        def _(pe):
            pe.wait_ge(s_pool, 9)
            pe.wait_ge(s_pick, 1)
            sort.on_tensor(nc.tensor, ps).then_inc(s_rank, 1)


class Experts:

    def __init__(self, nc, ctx, keep, name, w1, w2, left, right, rows=None, untransposed=0):
        def sb(n, shape, dt=F32):
            return ctx.enter_context(nc.sbuf_tensor(f"{name}_{n}", shape, dt))

        def sem(n):
            return ctx.enter_context(nc.semaphore(f"{name}_{n}"))

        def ps(n):
            return ctx.enter_context(nc.psum_tensor(f"{name}_{n}", [P, 512], F32))

        self.nc, self.keep, self.w1, self.w2 = nc, keep, w1, w2
        self.left, self.right = left, right
        self.hid = left[1] - left[0]
        self.kc = self.hid // P
        self.rows = rows or [sb(f"rows{p}", [P, DIM]) for p in range(2)]
        self.skip = untransposed
        self.xT = sb("xT", [P, 2, DC, P])
        self.sil = sb("sil", [P, 2, self.hid])
        self.a = sb("a", [P, 2, self.hid])
        self.aT = sb("aT", [P, 2, self.kc, P])
        self.y = [sb(f"y{p}", [P, DIM]) for p in range(2)]
        self.TX, self.HB = [ps(f"TX{p}") for p in range(2)], [ps(f"H{p}") for p in range(2)]
        self.TA, self.YB = ps("TA"), [ps(f"Y{p}") for p in range(2)]
        self.loaded = [sem(f"rows_loaded{p}") for p in range(2)]
        self.s_T, self.s_H, self.s_sil = sem("rows_transposed"), sem("first_product"), sem("silu_ready")
        self.s_xT = sem("xT_ready")
        self.s_a = sem("act_ready")
        self.s_T2 = sem("act_transposed")
        self.s_aT = sem("aT_ready")
        self.s_Y = sem("second_product")
        self.s_yf = sem("product_taken")

    def start(self, pe):
        for s, n in ((self.s_xT, 2), (self.s_a, 2), (self.s_T2, 2), (self.s_aT, 1), (self.s_Y, 2), (self.s_yf, 2)):
            pe.sem_inc(s, n)

    def T(self, pe, it, p):
        j = it * 2 + p
        pe.wait_ge(self.loaded[p], it * 16 + (16 - self.skip // 2 * 16))
        pe.wait_ge(self.s_xT, j + 1)
        for c in range(DC):
            last = self.nc.tensor.transpose(self.TX[p][:, c * P:(c + 1) * P], self.rows[p][:, c * P:(c + 1) * P],
                                            self.keep.ident[:, :])
        last.then_inc(self.s_T, 1)

    def weights(self, w, e, c):
        if isinstance(e, int):
            return w[:, e, c, :]
        return w[:, bass.ds(e, 1), c, :].rearrange("p a n -> p (a n)")

    def H(self, pe, it, p, e):
        j = it * 2 + p
        pe.wait_ge(self.s_xT, j + 3)
        pe.wait_ge(self.s_a, j + 1)
        for c in range(DC):
            last = self.nc.tensor.matmul(self.HB[p][:, :], self.xT[:, p, c, :], self.weights(self.w1, e, c),
                                         start=(c == 0), stop=(c == DC - 1))
        last.then_inc(self.s_H, 1)

    def T2(self, pe, it, p):
        j = it * 2 + p
        pe.wait_ge(self.s_a, j + 3)
        pe.wait_ge(self.s_aT, j + 1)
        for c in range(self.kc):
            last = self.nc.tensor.transpose(self.TA[:, c * P:(c + 1) * P], self.a[:, p, c * P:(c + 1) * P],
                                            self.keep.ident[:, :])
        last.then_inc(self.s_T2, 1)

    def Y(self, pe, it, p, e):
        j = it * 2 + p
        pe.wait_ge(self.s_aT, j + 2)
        pe.wait_ge(self.s_yf, j + 1)
        for c in range(self.kc):
            last = self.nc.tensor.matmul(self.YB[p][:, :], self.aT[:, p, c, :], self.weights(self.w2, e, c),
                                         start=(c == 0), stop=(c == self.kc - 1))
        last.then_inc(self.s_Y, 1)

    def copy_xT(self, act, it, p):
        j = it * 2 + p
        act.wait_ge(self.s_T, j + (1 - self.skip))
        self.nc.scalar.copy(self.xT[:, p, :, :], self.TX[p][:, :].rearrange("p (c q) -> p c q", c=DC)).then_inc(self.s_xT, 1)

    def silu(self, act, it, p):
        j = it * 2 + p
        act.wait_ge(self.s_H, j + 1)
        act.wait_ge(self.s_a, j + 1)
        self.nc.scalar.activation(self.sil[:, p, :], self.HB[p][:, self.left[0]:self.left[1]], ACT.Silu).then_inc(self.s_sil, 1)

    def copy_aT(self, act, it, p):
        j = it * 2 + p
        act.wait_ge(self.s_T2, j + 3)
        act.wait_ge(self.s_Y, j + 1)
        self.nc.scalar.copy(self.aT[:, p, :, :],
                            self.TA[:, 0:self.hid].rearrange("p (c q) -> p c q", c=self.kc)).then_inc(self.s_aT, 1)

    def copy_y(self, act, it, p):
        j = it * 2 + p
        act.wait_ge(self.s_Y, j + 3)
        self.nc.scalar.copy(self.y[p][:, :], self.YB[p][:, :]).then_inc(self.s_yf, 1)

    def product(self, dve, it, p):
        j = it * 2 + p
        dve.wait_ge(self.s_sil, j + 1)
        dve.wait_ge(self.s_T2, j + 1)
        self.nc.vector.tensor_tensor(out=self.a[:, p, :], in0=self.HB[p][:, self.right[0]:self.right[1]],
                                     in1=self.sil[:, p, :], op=ALU.mult).then_inc(self.s_a, 1)


def load_expert_c(sp, ext, keep, e):
    for dst, src in ((keep.w13, "w13"), (keep.w2, "w2")):
        sp.dma_start(dst[:, bass.ds(e, 1), :, :].rearrange("p a c n -> p (a c) n"),
                     ext[src][:, bass.ds(e, 1), :, :].rearrange("p a c n -> p (a c) n")).then_inc(keep.s_wc, 16)


def id_expert_block(nc, ext, keep):
    with ExitStack() as ctx:
        ctxT = keep.arena[:, :].rearrange("p (e c n) -> p e c n", e=EX_B, c=DC)
        ex = Experts(nc, ctx, keep, "b", ctxT, ctxT, (0, DIM), (0, DIM))
        stored = [ctx.enter_context(nc.semaphore(f"b_stored{p}")) for p in range(2)]
        block = ctx.enter_context(nc.Block())
        PAIRS = NB_B // 2
        LAST = NB_B - 1
        xs = keep.xs_b.rearrange("(n p) d -> n p d", p=P)
        ys = keep.ys_b.rearrange("(n p) d -> n p d", p=P)

        def at(view, j):
            return view[j, :, :] if isinstance(j, int) else view[bass.ds(j, 1), :, :].rearrange("a p d -> (a p) d")

        @block.sync
        def _(sp):
            for p in range(2):
                sp.dma_start(ex.rows[p][:, :], at(xs, p)).then_inc(ex.loaded[p], 16)
            sp.dma_start(keep.gate[:, :, :], ext["gate"]).then_inc(keep.s_wc, 16)
            assert PAIRS - 1 == EX_C
            with sp.Fori(0, PAIRS - 1) as it:
                for p in range(2):
                    sp.wait_ge(ex.s_T, it * 2 + p + 1)
                    sp.dma_start(ex.rows[p][:, :], at(xs, it * 2 + p + 2)).then_inc(ex.loaded[p], 16)
                load_expert_c(sp, ext, keep, it)
            sp.wait_ge(ex.s_T, LAST - 1)
            sp.dma_start(ex.rows[0][:, :], at(xs, LAST)).then_inc(ex.loaded[0], 16)
            load_expert_c(sp, ext, keep, EX_C)

        @block.scalar
        def _(act):
            def y_out(it, p):
                if not (isinstance(it, int) and it == 0):
                    act.wait_ge(stored[p], it * 16)
                ex.copy_y(act, it, p)
                act.wait_ge(ex.s_yf, it * 2 + p + 3)
                act.dma_start(at(ys, it * 2 + p), ex.y[p][:, :]).then_inc(stored[p], 16)

            def step(it, p, more):
                nit, np_ = (it, 1) if p == 0 else (it + 1, 0)
                ex.copy_aT(act, it, p)
                ex.silu(act, nit, np_)
                if more:
                    ex.copy_xT(act, it + 1, p)
                y_out(it, p)

            ex.copy_xT(act, 0, 0)
            ex.copy_xT(act, 0, 1)
            ex.silu(act, 0, 0)
            step(0, 0, True)
            step(0, 1, True)
            with act.Fori(1, PAIRS - 1) as it:
                step(it, 0, True)
                step(it, 1, True)
            step(PAIRS - 1, 0, True)
            step(PAIRS - 1, 1, False)
            ex.copy_aT(act, PAIRS, 0)
            y_out(PAIRS, 0)
            act.wait_ge(stored[0], (PAIRS + 1) * 16)
            act.wait_ge(stored[1], PAIRS * 16)

        @block.vector
        def _(dve):
            ex.product(dve, 0, 0)
            with dve.Fori(0, PAIRS) as it:
                ex.product(dve, it, 1)
                ex.product(dve, it + 1, 0)

        @block.tensor
        def _(pe):
            def expert(j):
                e = keep.ex_b[0:1, j:j + 1] if isinstance(j, int) else keep.ex_b[0:1, bass.ds(j, 1)]
                return pe.value_load(e, min_val=0, max_val=EX_B - 1)

            def step(it, p, more):
                nit, np_ = (it, 1) if p == 0 else (it + 1, 0)
                ex.T2(pe, it, p)
                ex.H(pe, nit, np_, expert(it * 2 + p + 1))
                if more:
                    ex.T(pe, it + 1, p)
                ex.Y(pe, it, p, expert(it * 2 + p))

            ex.start(pe)
            ex.T(pe, 0, 0)
            ex.T(pe, 0, 1)
            pe.wait_ge(keep.s_ctx, 16)
            ex.H(pe, 0, 0, expert(0))
            with pe.Fori(0, PAIRS - 1) as it:
                step(it, 0, True)
                step(it, 1, True)
            step(PAIRS - 1, 0, True)
            step(PAIRS - 1, 1, False)
            ex.T2(pe, PAIRS, 0)
            ex.Y(pe, PAIRS, 0, expert(LAST))


def weights_c(nc, ctx, keep):
    keep.w13 = ctx.enter_context(nc.sbuf_tensor("w13", [P, EX_C + 1, DC, 2 * HID], F32))
    keep.w2 = ctx.enter_context(nc.sbuf_tensor("w2", [P, EX_C + 1, HID // P, DIM], F32))
    keep.gate = ctx.enter_context(nc.sbuf_tensor("gate", [P, DC, EX_C], F32))
    keep.s_wc = ctx.enter_context(nc.semaphore("c_weights_loaded"))


def gate_expert_block(nc, ext, keep):
    x2 = keep.x1
    Q = BATCH
    S_PAIRS = NT // 2
    FIRST = Q // 2
    SCALE = FIRST + 1
    R_PAIRS = NB_C // 2
    LAST = S_PAIRS + R_PAIRS
    SHARED = EX_C
    with ExitStack() as ctx:
        def sb(name, shape, dt=F32):
            return ctx.enter_context(nc.sbuf_tensor(name, shape, dt))

        def sem(name):
            return ctx.enter_context(nc.semaphore(name))

        def carve(region):
            used = [0]

            def take(name, shape, dt=F32):
                n = 1
                for k in shape[1:]:
                    n *= k
                words = n if dt != BF16 else n // 2
                flat = region[:, used[0]:used[0] + words]
                used[0] += words
                if dt != F32:
                    flat = flat.bitcast(dt)
                if len(shape) == 3:
                    flat = flat.rearrange("p (a b) -> p a b", a=shape[1])
                return flat
            return take

        xT_all = keep.arena[:, :].rearrange("p (t c q) -> p t c q", t=NT, c=DC)
        xn_flat = sb("gxn", [P, TB * DIM])
        xn = xn_flat[:, :].rearrange("p (t d) -> p t d", t=TB)
        rows = [xn_flat[:, p * ROW:(p + 1) * ROW] for p in range(2)]
        stage_flat = sb("gstage", [P, TB * ROW])
        yg = stage_flat[:, 0:TB * DIM].rearrange("p (t d) -> p t d", t=TB)
        stage = stage_flat[:, :].rearrange("p (t w) -> p t w", t=TB)
        between = carve(stage_flat)
        sort = Sorter(between, keep, "sc", EX_C, NT * TOPK, NB_C)
        ex = Experts(nc, ctx, keep, "c", keep.w13, keep.w2, (0, HID), (HID, 2 * HID), rows, NT)
        pos_cur = sb("gpos_cur", [P, TB], I32)
        st = sb("gst", [P, TB, 6])
        mv = sb("gmv", [P, TB, 2])
        var = sb("gvar", [P, TB])
        rstd = sb("grstd", [P, TB])
        half = sb("ghalf", [P, TB])
        epsc = sb("gepsc", [P, TB])
        lg = ex.y[1][0:EX_C, :]
        sc = sb("scores", [P, NT, EX_C])
        best = between("best", [P, NT, 8])
        besti = between("besti", [P, NT, 8], U32)
        chosen = between("chosen", [P, TOPK, NT])
        mean = sb("mean", [P, NT])
        dev = sb("dev", [P, NT])
        gain = sb("gain", [P, TOPK, NT])
        pos = sb("pos_c", [P, TOPK * NT], I32)
        ex_c = sb("ex_c", [P, NB_C], I32)
        mean_cur = sb("mean_cur", [P, TB])
        gain_cur = sb("gain_cur", [P, TOPK, TB])
        slot_cur = sb("slot_cur", [P, TOPK, 2 * TB], I32)
        tokens = sb("tokens", [P, NB_C], I32)
        tokens_cur = sb("tokens_cur", [P, 1], I32)
        lps = ctx.enter_context(nc.psum_tensor("glogits", [P, 512], F32))
        xb = [ex.TX[0], ex.TX[1], ex.HB[1], ex.YB[1]]
        tps = ex.YB[0]

        s_cst = sem("gate_constants")
        s_pos, s_g = sem("gate_positions"), [sem(f"gathered{r}") for r in range(TB)]
        s_x2 = sem("x2_ready")
        s_ch = sem("gate_chain")
        s_mv, s_var, s_rstd = sem("stats3_ready"), sem("var3_ready"), sem("rstd3_ready")
        s_xn = sem("xn3_ready")
        s_tx, s_tc = sem("xn3_transposed"), sem("xT3_ready")
        s_lg, s_lc, s_lt, s_ls = (sem("logits_summed"), sem("logits_copied"), sem("logits_transposed"),
                                  sem("logits_stored"))
        s_ex = sem("exp_ready")
        s_best, s_pick, s_rank = sem("best_ready"), sem("gate_pick_ready"), sem("gate_rank_ready")
        s_sort = sem("gate_sorted")
        s_cur = sem("gains_current")
        s_stage = sem("scaled_rows_ready")
        s_slot, s_sc = sem("slots_current"), keep.s_xs_c
        s_base0 = sem("quarter_rows_stored")
        s_base = [sem(f"base_rows_stored{p}") for p in range(2)]
        s_id, s_tok = sem("row_tokens_copied"), sem("tokens_current")
        s_add = keep.s_add
        s_left = sem("y_buffer_steps")
        s_aux = sem("c_unused_count")
        block = ctx.enter_context(nc.Block())
        STORES = (S_PAIRS - FIRST) * 16 + 16

        def at(view, j):
            return view[bass.ds(j, 1), :, :].rearrange("a p d -> (a p) d")

        def quarter(ap, q):
            return ap[:, bass.ds(q * TB, TB)]

        @block.sync
        def _(sp):
            xs = keep.xs_c.rearrange("(n p) d -> n p d", p=P)
            out = keep.out[0:TOKENS, :].rearrange("(n p) d -> n p d", p=P)
            sp.sem_inc(s_base0, 16)
            for p in range(2):
                sp.sem_inc(s_base[p], 16)

            def store(j, p, done):
                sp.wait_ge(ex.s_yf, j + 3)
                sp.sem_inc(s_aux, 1)
                sp.dma_start(at(out, j), ex.y[p][:, :]).then_inc(done, 16)

            with sp.Fori(0, Q) as q:
                store(q, 0, s_base0)
            with sp.Fori(FIRST, S_PAIRS - 1) as it:
                for p in range(2):
                    store(it * 2 + p, p, s_base[p])
            for t in range(TB):
                sp.wait_ge(s_sc[t], 16 * TOPK * Q + 16)
            for p in range(2):
                sp.dma_start(ex.rows[p], at(xs, p)).then_inc(ex.loaded[p], 16)
            for p in range(2):
                store(NT - 2 + p, p, s_base[p])

            def load_routed(m, p):
                sp.wait_ge(ex.s_T, m - 1)
                sp.sem_inc(s_aux, 1)
                sp.wait_ge(s_id, m - 1)
                sp.sem_inc(s_aux, 1)
                sp.dma_start(ex.rows[p], at(xs, m)).then_inc(ex.loaded[p], 16)

            with sp.Fori(0, R_PAIRS - 1) as r:
                for p in range(2):
                    load_routed(r * 2 + (p + 2), p)
            load_routed(NB_C - 1, 0)

        @block.gpsimd
        def _(pool):
            g = nc.gpsimd
            pool.sem_inc(s_left, 1)
            g.memset(half[:, :], -0.5).then_inc(s_cst, 1)
            g.memset(epsc[:, :], EPS).then_inc(s_cst, 1)
            pool.wait_ge(s_cst, 2)

            def gather(q):
                if not (isinstance(q, int) and q == 0):
                    for r in range(TB):
                        pool.wait_ge(s_g[r], q * 16)
                    pool.sem_inc(s_aux, 1)
                g.tensor_copy(pos_cur[:, :], keep.pos_b[:, bass.ds(q * TB, TB)]).then_inc(s_pos, 1)
                pool.wait_ge(s_pos, q + 1)
                for r in range(TB):
                    pool.wait_ge(s_x2, q * TB + r + 1)
                    pool.sem_inc(s_aux, 1)
                    g.indirect_dma_start(out=yg[:, r, :], out_offset=None, in_=keep.ys_b,
                                         in_offset=bass.IndirectOffsetOnAxis(ap=pos_cur[:, r:r + 1].bitcast(U32), axis=0)
                                         ).then_inc(s_g[r], 16)

            def inverse_root(q):
                pool.wait_ge(s_mv, q * TB + TB)
                g.tensor_tensor(out=var[:, :], in0=mv[:, :, 1], in1=epsc[:, :], op=ALU.add).then_inc(s_var, 1)
                pool.wait_ge(s_var, q + 1)
                g.tensor_tensor(out=rstd[:, :], in0=var[:, :], in1=half[:, :], op=ALU.pow).then_inc(s_rstd, 1)

            pool.wait_ge(s_x2, TB)
            gather(0)
            with pool.Fori(0, Q - 1) as q:
                gather(q + 1)
                inverse_root(q)
            inverse_root(Q - 1)

            pool.wait_ge(keep.s_clr_c, 16 * CLEARS_C * (BATCH - 1))
            pool.wait_ge(s_sort, SORTED)
            with pool.Fori(0, Q // 2) as h:
                for t in range(TB):
                    pool.wait_ge(s_sc[t], h * (2 * 16 * TOPK) + 16)
                pool.sem_inc(s_aux, 1)
                g.tensor_copy(slot_cur[:, :, :], pos[:, :].rearrange("p (k n) -> p k n", k=TOPK)[:, :, bass.ds(h * (2 * TB), 2 * TB)]
                              ).then_inc(s_slot, 1)
                pool.wait_ge(s_slot, h + 1)
                for n in range(2 * TOPK):
                    for t in range(TB):
                        pool.wait_ge(s_stage, h * (2 * TOPK * STAGED) + (n * STAGED + 2 * t + 3))
                        pool.sem_inc(s_aux, 1)
                        col = (n // TOPK) * TB + t
                        g.indirect_dma_start(out=keep.xs_c, in_=stage[:, t, :], in_offset=None,
                                             out_offset=bass.IndirectOffsetOnAxis(ap=slot_cur[:, n % TOPK, col:col + 1].bitcast(U32), axis=0)
                                             ).then_inc(s_sc[t], 16)
            pool.wait_ge(s_base0, 16 * Q + 16)
            for p in range(2):
                pool.wait_ge(s_base[p], STORES)

            def add(m, p):
                pool.wait_ge(s_id, m + 1)
                pool.wait_ge(s_add, m * 16 + 16)
                pool.sem_inc(s_left, 1)
                g.tensor_copy(tokens_cur[:, :], tokens[:, bass.ds(m, 1)]).then_inc(s_tok, 1)
                pool.wait_ge(s_tok, m + 1)
                pool.wait_ge(ex.s_yf, m + (2 * S_PAIRS + 3))
                pool.sem_inc(s_aux, 1)
                g.indirect_dma_start(out=keep.out, out_offset=bass.IndirectOffsetOnAxis(ap=tokens_cur[:, 0:1].bitcast(U32), axis=0),
                                     in_=ex.y[p][:, :], in_offset=None, compute_op=ALU.add).then_inc(s_add, 16)

            with pool.Fori(0, R_PAIRS) as r:
                for p in range(2):
                    add(r * 2 + p, p)
            add(NB_C - 1, 0)
            pool.wait_ge(s_add, 16 * NB_C + 16)

        @block.vector
        def _(dve):
            v = nc.vector
            dve.sem_inc(s_x2, TB)
            dve.sem_inc(s_stage, 1)

            def tile(n):
                return x2[:, bass.ds(n, 1), :].rearrange("p a d -> p (a d)")

            def add_experts(q):
                for r in range(TB):
                    dve.wait_ge(s_g[r], q * 16 + 16)
                    v.tensor_tensor(out=tile(q * TB + r), in0=tile(q * TB + r), in1=yg[:, r, :], op=ALU.add).then_inc(s_x2, 1)
                for r in range(TB):
                    dve.wait_ge(s_x2, q * TB + TB + r + 1)
                    dve.sem_inc(s_aux, 1)
                    v.bn_stats(st[:, r, :], tile(q * TB + r)).then_inc(s_ch, 1)
                for r in range(TB):
                    dve.wait_ge(s_ch, q * TB + r + 1)
                    dve.sem_inc(s_aux, 1)
                    v.bn_aggr(mv[:, r, :], st[:, r, :]).then_inc(s_mv, 1)

            def normalise(q):
                dve.wait_ge(s_rstd, q + 1)
                for r in range(TB):
                    v.tensor_scalar(out=xn[:, r, :], in0=tile(q * TB + r), scalar1=mv[:, r, 0:1], scalar2=rstd[:, r:r + 1],
                                    op0=ALU.subtract, op1=ALU.mult).then_inc(s_xn, 1)
                v.tensor_copy(quarter(mean, q), mv[:, :, 0]).then_inc(s_aux, 1)
                v.tensor_copy(quarter(dev, q), rstd[:, :]).then_inc(s_aux, 1)

            def base(j, p, guard, value):
                dve.wait_ge(guard, value)
                dve.sem_inc(s_aux, 1)
                dve.wait_ge(ex.s_Y, j + 3)
                v.tensor_tensor(out=ex.y[p][:, :], in0=ex.YB[p][:, :], in1=tile(j), op=ALU.add).then_inc(ex.s_yf, 1)

            def base_q(q):
                base(q, 0, s_base0, q * 16 + 16)

            def base_p(it, p):
                base(it * 2 + p, p, s_base[p], it * 16 - (16 * FIRST - 16))

            def quarter_product(q):
                dve.wait_ge(ex.s_sil, q + 1)
                v.tensor_tensor(out=ex.a[:, 0, :], in0=ex.HB[0][:, ex.right[0]:ex.right[1]], in1=ex.sil[:, 0, :],
                                op=ALU.mult).then_inc(ex.s_a, 1)

            add_experts(0)
            normalise(0)
            with dve.Fori(0, Q - 1) as q:
                add_experts(q + 1)
                quarter_product(q)
                normalise(q + 1)
                base_q(q)
            quarter_product(Q - 1)
            base_q(Q - 1)
            dve.wait_ge(s_base0, 16 * Q + 16)

            ex.product(dve, FIRST, 0)
            do = Chain(dve, s_best)
            dve.wait_ge(s_ex, 1)
            do(v.tensor_scalar(out=sc[:, :, :], in0=sc[:, :, :], scalar1=1.0, scalar2=None, op0=ALU.add))
            do(v.reciprocal(sc[:, :, :], sc[:, :, :]))
            for n in range(NT):
                v.max(best[:, n, :], sc[:, n, :]).then_inc(s_best, 1)
            ex.product(dve, FIRST, 1)
            base_p(FIRST, 0)
            dve.wait_ge(s_best, 2 + NT)
            for n in range(NT):
                v.max_index(besti[:, n, :], best[:, n, :], sc[:, n, :]).then_inc(s_best, 1)
            dve.wait_ge(s_best, 2 + 2 * NT)
            do = Chain(dve, s_pick)
            do(v.tensor_copy(chosen[:, :, :], besti[:, :, 0:TOPK].rearrange("p n k -> p k n")))
            for e in range(EX_C):
                v.tensor_scalar(out=sort.pick[:, e, :], in0=chosen[:, :, :].rearrange("p k n -> p (k n)"),
                                scalar1=float(e), scalar2=None, op0=ALU.is_equal).then_inc(s_pick, 1)
            dve.wait_ge(s_pick, 1 + EX_C)
            v.tensor_copy(sort.pickb[:, :, :], sort.pick[:, :, :]).then_inc(s_pick, 1)
            ex.product(dve, FIRST + 1, 0)
            base_p(FIRST, 1)
            do = Chain(dve, s_sort)
            dve.wait_ge(s_rank, 1)
            sort.on_vector(v, do, lps, pos[:, :], ex_c[:, :])
            do(v.tensor_tensor(out=gain[:, :, :], in0=best[:, :, 0:TOPK].rearrange("p n k -> p k n"),
                               in1=dev[:, :].unsqueeze(1).to_broadcast([P, TOPK, NT]), op=ALU.mult))
            assert do.n == SORTED

            def scale(q, k):
                for t in range(TB):
                    dve.wait_ge(s_sc[t], q * (16 * TOPK) + (16 * k + 16))
                    dve.sem_inc(s_aux, 1)
                    v.tensor_copy(stage[:, t, DIM:ROW].bitcast(I32),
                                  keep.token[:, bass.ds(q * TB + t, 1)].to_broadcast([P, ROW - DIM])).then_inc(s_stage, 1)
                    v.tensor_scalar(out=stage[:, t, 0:DIM], in0=tile(q * TB + t), scalar1=mean_cur[:, t:t + 1],
                                    scalar2=gain_cur[:, k, t:t + 1], op0=ALU.subtract, op1=ALU.mult).then_inc(s_stage, 1)

            with dve.Fori(0, Q) as q:
                it = q + SCALE
                dve.wait_ge(s_stage, q * (STAGED * TOPK) + 1)
                dve.sem_inc(s_aux, 1)
                v.tensor_copy(mean_cur[:, :], quarter(mean, q)).then_inc(s_cur, 1)
                v.tensor_copy(gain_cur[:, :, :], gain[:, :, bass.ds(q * TB, TB)]).then_inc(s_cur, 1)
                dve.wait_ge(s_cur, q * 2 + 2)
                ex.product(dve, it, 1)
                scale(q, 0)
                base_p(it, 0)
                ex.product(dve, it + 1, 0)
                scale(q, 1)
                base_p(it, 1)

            def take_tokens(it, p):
                dve.wait_ge(ex.loaded[p], it * 16 + (16 - S_PAIRS * 16))
                dve.sem_inc(s_aux, 1)
                v.tensor_copy(tokens[:, bass.ds(it * 2 + (p - 2 * S_PAIRS), 1)],
                              ex.rows[p][:, DIM:DIM + 1].bitcast(I32)).then_inc(s_id, 1)

            ex.product(dve, S_PAIRS - 1, 1)
            base_p(S_PAIRS - 1, 0)
            take_tokens(S_PAIRS, 0)
            ex.product(dve, S_PAIRS, 0)
            take_tokens(S_PAIRS, 1)
            base_p(S_PAIRS - 1, 1)
            with dve.Fori(S_PAIRS, LAST - 1) as it:
                ex.product(dve, it, 1)
                take_tokens(it + 1, 0)
                ex.product(dve, it + 1, 0)
                take_tokens(it + 1, 1)
            ex.product(dve, LAST - 1, 1)
            take_tokens(LAST, 0)
            ex.product(dve, LAST, 0)

        @block.scalar
        def _(act):
            a = nc.scalar

            def copy_tile(j, p):
                a.copy(ex.xT[:, p, :, :], xT_all[:, bass.ds(j, 1), :, :].rearrange("p a c q -> p (a c) q")).then_inc(ex.s_xT, 1)

            def copy_aT(it, p, j):
                act.wait_ge(ex.s_T2, j + 3)
                a.copy(ex.aT[:, p, :, :], ex.TA[:, 0:ex.hid].rearrange("p (c q) -> p c q", c=ex.kc)).then_inc(ex.s_aT, 1)

            with act.Fori(0, Q) as q:
                for c in range(DC):
                    act.wait_ge(s_tx, q * DC + c + 1)
                    a.copy(xT_all[:, bass.ds(q * TB, TB), c, :], xb[c][:, :].rearrange("p (t q) -> p t q", t=TB)).then_inc(s_tc, 1)
                act.wait_ge(s_tc, q * DC + DC)
                copy_tile(q, 0)
                act.wait_ge(ex.s_H, q + 1)
                a.activation(ex.sil[:, 0, :], ex.HB[0][:, ex.left[0]:ex.left[1]], ACT.Silu).then_inc(ex.s_sil, 1)
                act.wait_ge(s_lg, q + 1)
                a.copy(lg, lps[0:EX_C, :]).then_inc(s_lc, 1)
                act.wait_ge(s_lt, q + 1)
                a.copy(sc[:, bass.ds(q * TB, TB), :], tps[:, 0:TB * EX_C].rearrange("p (t e) -> p t e", e=EX_C)).then_inc(s_ls, 1)
                copy_aT(0, 0, q)
            act.wait_ge(s_ls, Q)
            a.activation(sc[:, :, :], sc[:, :, :], ACT.Exp, scale=-1.0).then_inc(s_ex, 1)
            copy_tile(2 * FIRST, 0)
            copy_tile(2 * FIRST + 1, 1)
            ex.silu(act, FIRST, 0)

            def y_out(it, p):
                act.wait_ge(s_left, it * 2 + (p - (2 * S_PAIRS - 1)))
                ex.copy_y(act, it, p)

            def step(it, p, fetch=None, routed=False):
                nit, np_ = (it, 1) if p == 0 else (it + 1, 0)
                ex.copy_aT(act, it, p)
                ex.silu(act, nit, np_)
                if fetch:
                    fetch(it + 1, p)
                if routed:
                    y_out(it, p)

            def shared_tile(it, p):
                copy_tile(it * 2 + p, p)

            def transposed(it, p):
                ex.copy_xT(act, it, p)

            with act.Fori(FIRST, S_PAIRS - 1) as it:
                for p in range(2):
                    step(it, p, shared_tile)
            for p in range(2):
                step(S_PAIRS - 1, p, transposed)
            act.wait_ge(ex.s_yf, 2 * S_PAIRS + 2)
            for p in range(2):
                act.wait_ge(s_base[p], STORES)
            with act.Fori(S_PAIRS, LAST - 1) as it:
                for p in range(2):
                    step(it, p, transposed, routed=True)
            step(LAST - 1, 0, transposed, routed=True)
            step(LAST - 1, 1, routed=True)
            ex.copy_aT(act, LAST, 0)
            y_out(LAST, 0)

        @block.tensor
        def _(pe):
            te = nc.tensor

            def expert(m):
                e = ex_c[0:1, m:m + 1] if isinstance(m, int) else ex_c[0:1, bass.ds(m, 1)]
                return pe.value_load(e, min_val=0, max_val=EX_C - 1)

            def gate_and_block(q):
                pe.wait_ge(s_xn, q * TB + TB)
                for c in range(DC):
                    for r in range(TB):
                        last = te.transpose(xb[c][:, r * P:(r + 1) * P], xn[:, r, c * P:(c + 1) * P], keep.ident[:, :])
                    last.then_inc(s_tx, 1)
                pe.wait_ge(ex.s_xT, q + 3)
                for c in range(DC):
                    last = te.matmul(ex.HB[0][:, :], ex.xT[:, 0, c, :], keep.w13[:, SHARED, c, :], start=(c == 0), stop=(c == DC - 1))
                last.then_inc(ex.s_H, 1)
                for c in range(DC):
                    last = te.matmul(lps[0:EX_C, :], keep.gate[:, c, :],
                                     xT_all[:, bass.ds(q * TB, TB), c, :],
                                     start=(c == 0), stop=(c == DC - 1))
                last.then_inc(s_lg, 1)
                pe.wait_ge(ex.s_a, q + 3)
                for c in range(ex.kc):
                    last = te.transpose(ex.TA[:, c * P:(c + 1) * P], ex.a[:, 0, c * P:(c + 1) * P], keep.ident[:, :])
                last.then_inc(ex.s_T2, 1)
                pe.wait_ge(ex.s_yf, q + 2)
                pe.wait_ge(s_lc, q + 1)
                pe.sem_inc(s_aux, 1)
                for r in range(TB):
                    last = te.transpose(tps[:, r * EX_C:(r + 1) * EX_C], lg[:, r * P:(r + 1) * P],
                                        keep.ident[0:EX_C, 0:EX_C])
                last.then_inc(s_lt, 1)
                pe.wait_ge(ex.s_aT, q + 2)
                for c in range(ex.kc):
                    last = te.matmul(ex.YB[0][:, :], ex.aT[:, 0, c, :], keep.w2[:, SHARED, c, :], start=(c == 0), stop=(c == ex.kc - 1))
                last.then_inc(ex.s_Y, 1)

            def shared():
                return SHARED

            def step(it, p, e_next, e, fetch):
                nit, np_ = (it, 1) if p == 0 else (it + 1, 0)
                ex.T2(pe, it, p)
                ex.H(pe, nit, np_, e_next())
                if fetch:
                    ex.T(pe, it + 1, p)
                ex.Y(pe, it, p, e())

            ex.start(pe)
            pe.wait_ge(keep.s_wc, 16 * (2 * (EX_C + 1) + 1))
            with pe.Fori(0, Q) as q:
                gate_and_block(q)
            pe.wait_ge(ex.s_yf, 2 * FIRST + 2)
            ex.H(pe, FIRST, 0, SHARED)
            for p in range(2):
                step(FIRST, p, shared, shared, False)
            pe.wait_ge(s_pick, EX_C + 2)
            sort.on_tensor(te, lps).then_inc(s_rank, 1)
            with pe.Fori(SCALE, S_PAIRS - 1) as it:
                for p in range(2):
                    step(it, p, shared, shared, False)
            step(S_PAIRS - 1, 0, shared, shared, True)
            step(S_PAIRS - 1, 1, lambda: expert(0), shared, True)
            with pe.Fori(0, R_PAIRS - 1) as r:
                for p in range(2):
                    step(r + S_PAIRS, p, lambda: expert(r * 2 + (p + 1)), lambda: expert(r * 2 + p), True)
            for p in range(2):
                m = (R_PAIRS - 1) * 2 + p
                step(LAST - 1, p, lambda: expert(m + 1), lambda: expert(m), p == 0)
            ex.T2(pe, LAST, 0)
            ex.Y(pe, LAST, 0, expert(NB_C - 1))


STAGED = 2 * TB
SORTED = EX_C + 15


def build(nc, ext):
    with ExitStack() as ctx:
        keep = Keep(nc, ctx, ext)
        setup_block(nc, ext, keep)
        attention_block(nc, ext, keep)
        weights_c(nc, ctx, keep)
        id_expert_block(nc, ext, keep)
        gate_expert_block(nc, ext, keep)


def _layout(np, x, itok_BxS_13_99985, ctx_2048, L0_attn_Wqa, L0_attn_Wqb, L0_attn_Wkva, L0_attn_Wkvb, L0_attn_Wo,
            L0_ffn_gate_w, L0_ffn_w1, L0_ffn_w2, L0_ffn_w3, L0_ffn_ws1, L0_ffn_ws2, L0_ffn_ws3):
    def rows(w):
        return w.reshape(w.shape[0] // P, P, w.shape[1]).transpose(1, 0, 2)

    def experts(ws):
        return np.stack([rows(w) for w in ws], axis=1)

    pe = L0_attn_Wkva[:, LORA:]
    even, odd = pe[:, 0::2], pe[:, 1::2]
    wqb = L0_attn_Wqb.reshape(LORA, NG, GROUP, QK)
    wqb = [wqb[..., NOPE::2], wqb[..., NOPE + 1::2], wqb[..., :NOPE]]
    wkvb = L0_attn_Wkvb.reshape(LORA, HEADS, NOPE + VD)

    freq = np.float32(10000.0) ** (-np.arange(0, ROPE, 2, dtype=np.float32) / np.float32(ROPE))
    angle = (np.arange(SEQ, dtype=np.float32)[:, None] * freq[None, :]).astype(np.float64).T
    cos, sin = np.cos(angle), np.sin(angle)
    return {
        "x": x.reshape(TOKENS, DIM),
        "ids": itok_BxS_13_99985.reshape(NT, P).T,
        "wqa": rows(L0_attn_Wqa),
        "wkva": rows(np.concatenate([L0_attn_Wkva[:, :LORA], even, odd, odd, even], axis=1)),
        "wqb": np.stack(wqb, axis=2).reshape(LORA, NG * 3, P),
        "wk": wkvb[..., :NOPE].reshape(LORA, NG, P),
        "wv": wkvb[..., NOPE:].reshape(LORA, HEADS * VD),
        "wo": rows(L0_attn_Wo),
        "cos4": np.tile(cos * QK ** -0.5, (GROUP, 1)).astype(np.float32),
        "sin4": np.tile(sin * QK ** -0.5, (GROUP, 1)).astype(np.float32),
        "kcs": np.concatenate([cos, cos, -sin, sin]).astype(np.float32),
        "ctxT": experts([w.T for w in ctx_2048]).reshape(P, EX_B * DC * DIM),
        "w13": experts([np.concatenate([a.T, b.T], axis=1) for a, b in
                        zip([*L0_ffn_w1, L0_ffn_ws1], [*L0_ffn_w3, L0_ffn_ws3])]),
        "w2": experts([w.T for w in [*L0_ffn_w2, L0_ffn_ws2]]),
        "gate": rows(L0_ffn_gate_w.T),
    }


def kernel(**inputs):
    import numpy as _np
    import concourse.bacc as _bacc
    from concourse.bass_utils import run_bass_kernel_spmd as _run

    laid = _layout(_np, **{name: _np.asarray(a) for name, a in inputs.items()})
    nc = _bacc.Bacc("TRN2", target_bir_lowering=False, num_devices=1)
    arrays, ext = {}, {}
    for name, a in laid.items():
        a = _np.ascontiguousarray(a)
        arrays[f"in_{name}"] = a
        ext[name] = nc.dram_tensor(f"in_{name}", a.shape, mybir.dt.from_np(a.dtype), kind="ExternalInput").ap()
    ext["out"] = nc.dram_tensor("out", (TOKENS + P, DIM), F32, kind="ExternalOutput").ap()
    build(nc, ext)
    r = _run(nc, [arrays], core_ids=[0])
    return r.results[0]["out"][:TOKENS].reshape(BATCH, SEQ, DIM)
```

```python
from contextlib import ExitStack

import concourse.bass as bass
from concourse import mybir

F32 = mybir.dt.float32
BF16 = mybir.dt.bfloat16
I32 = mybir.dt.int32
U32 = mybir.dt.uint32
F32R = mybir.dt.float32r
ALU = mybir.AluOpType
ACT = mybir.ActivationFunctionType
AX = mybir.AxisListType

P = 128
BATCH, SEQ, DIM = 4, 512, 512
TOKENS = BATCH * SEQ
NT = TOKENS // P
TB = SEQ // P
DC = DIM // P
HEADS, NOPE, ROPE = 16, 32, 64
HALF = ROPE // 2
QK = NOPE + ROPE
VD = DIM // HEADS
LORA = 128
GROUP = P // NOPE
NG = HEADS // GROUP
LEAD = 4
UNITS = HEADS * TB
EPS = 1e-5
MASKED = -1e30

EX_B, VOCAB = 4, 25000
EX_C, TOPK, HID = 8, 2, 256
NB_B = NT + EX_B - 1
NB_C = NT * TOPK + EX_C - 1


class AttentionPlan:

    WORK = (0, 1, 2, 6)
    PT = (3, 4)
    OUT = 5
    PROJ = 7

    def __init__(self):
        self.tiles = {}
        self.uses = {s: [0] * 8 for s in ("pro", "units", "epi")}
        pro = [("xT", c) for c in range(DC)] + [("qa",), ("ckv",)]
        pro += [(k, 0) for k in "EONK"] + [("kpe",)] + [("V", t) for t in range(TB)]
        for n, name in enumerate(pro):
            self.take("pro", name, self.WORK[n % LEAD])
        for u in range(UNITS):
            self.take("units", ("S", u), self.WORK[u % LEAD])
            self.take("units", ("PT", u), self.PT[u % 2])
        for g in range(NG):
            self.take("units", ("out", g), self.OUT)
        for g in range(NG):
            for k in "EONK" * (g + 1 < NG):
                self.take("units", (k, g + 1), self.PROJ)
            if g > 0:
                self.take("units", ("R", g - 1), self.PROJ)
        epi = [("R", NG - 1)] + [("Wo", t) for t in range(TB)]
        for n, name in enumerate(epi):
            self.take("epi", name, self.WORK[n % LEAD])

    def take(self, section, name, bank):
        self.tiles[section, name] = (bank, self.uses[section][bank])
        self.uses[section][bank] += 1

    def place(self, section, name, b):
        bank, nth = self.tiles[section, name]
        p, u, e = (self.uses[s][bank] for s in ("pro", "units", "epi"))
        first = isinstance(b, int) and b == 0
        last = isinstance(b, int) and b == BATCH - 1
        if section == "pro":
            before = 0 if first else (b - 1) * (p + u + e) + (p + u)
        elif section == "units":
            before = b * (p + u + e) + p
        else:
            before = b * (p + u + e) + (p + u) + (0 if last else p)
        return bank, before + nth


def attention_block(nc, ext, keep):
    plan = AttentionPlan()
    x1, ident, pos_b, xs_b = keep.x1, keep.ident, keep.pos_b, keep.xs_b
    s_x0, s_xr = keep.s_x0, keep.s_xr
    with ExitStack() as ctx:
        def sb(name, shape, dt=F32):
            return ctx.enter_context(nc.sbuf_tensor(name, shape, dt))

        def sem(name):
            return ctx.enter_context(nc.semaphore(name))

        places = iter(range(0, EX_B * DC * DIM, DIM))

        def early(n):
            start = next(places)
            for _ in range(DC * n // DIM - 1):
                next(places)
            return keep.arena[:, start:start + DC * n].rearrange("p (c n) -> p c n", c=DC)

        kcs = early(SEQ // DC).rearrange("p c n -> p (c n)")
        xT = early(SEQ)
        wo = early(DIM)
        wqa = early(LORA)
        wkva = early(LORA + 2 * ROPE)
        wqb = sb("wqb", [P, NG * 3, P])
        wk = sb("wk", [P, NG, P])
        wv = sb("wv", [P, HEADS * VD])
        wo_high, wo_low = sb("wo_high", [P, DC, DIM], F32R), sb("wo_low", [P, DC, DIM], F32R)
        cos4 = sb("cos4", [P, SEQ])
        sin4 = sb("sin4", [P, SEQ])
        identb = sb("identb", [P, P], BF16)
        maskb = sb("maskb", [P, P], BF16)
        half = sb("half", [P, TB])
        epsc = sb("epsc", [P, TB])
        st1 = sb("st1", [P, TB, 6])
        mv1 = sb("mv1", [P, TB, 2])
        var1 = sb("var1", [P, TB])
        rstd1 = sb("rstd1", [P, TB])
        st2 = sb("st2", [P, TB, 6])
        mv2 = sb("mv2", [P, TB, 2])
        var2 = sb("var2", [P, TB])
        rstd2 = sb("rstd2", [P, TB])
        xn = keep.xn[:, :].rearrange("p (t d) -> p t d", t=TB)
        qaT = sb("qaT", [P, SEQ])
        cT = sb("cT", [P, SEQ])
        rot = sb("rot", [P, 4, SEQ])
        rEO = sb("rEO", [P, 2, SEQ])
        QT = sb("QT", [QK, 2 * GROUP, SEQ])
        KT = sb("KT", [QK, 2 * GROUP, SEQ])
        V = sb("V", [P, TB, DIM])
        negmax = sb("negmax", [P, 2 * LEAD])
        probs = sb("probs", [P, LEAD, SEQ])
        PTs = sb("PTs", [P, 2, GROUP, SEQ])
        kpt = PTs[0:ROPE, 0, 0:2, :]
        sums = sb("sums", [P, 2, TB, GROUP])
        rinv = sb("rinv", [P, TB * GROUP])
        rsum = sb("rsum", [P, TB * GROUP, VD])
        osb = sb("osb", [P, SEQ])
        OT_high = sb("OT_high", [P, DC, SEQ], F32R)
        OT_low = sb("OT_low", [P, DC, SEQ], F32R)
        sort = Sorter(carve(osb), keep, "sb", EX_B, NT, NB_B)
        xo = xn
        pos_cur = keep.pos_cur
        pad = sb("pad", [P, ROW])
        bank = [ctx.enter_context(nc.psum_tensor(f"bank{k}", [P, 512], F32)) for k in range(8)]

        filled = [sem(f"filled{k}") for k in range(8)]
        free = [sem(f"free{k}") for k in range(8)]
        s_wa, s_wp = sem("first_weights_loaded"), sem("proj_weights_loaded")
        s_wo, s_wh, s_wl = sem("wo_loaded"), sem("wo_high_ready"), sem("wo_low_ready")
        s_og, s_oh = sem("group_divided"), sem("group_high_ready")
        s_cst = sem("constants_ready")
        s_ones = sem("ones_ready")
        s_mv1, s_rs1, s_xn = sem("stats1_ready"), sem("rstd1_ready"), sem("xn_ready")
        s_mv2, s_rs2, s_xo = sem("stats2_ready"), sem("rstd2_ready"), sem("xn2_ready")
        s_p1, s_p2 = sem("pool_var1"), sem("pool_var2")
        s_c1, s_c2, s_c3 = sem("dve_ln1"), sem("dve_ln2"), sem("dve_norm")
        s_rot, s_rope, s_nk = sem("rot_products_ready"), sem("rotated_ready"), sem("nk_ready")
        s_qk = sem("qk_loaded")
        s_kpt, s_kpe = sem("kpe_products_ready"), sem("kpe_ready")
        s_kr = sem("kpe_repeated")
        s_nm, s_exp = sem("negmax_ready"), sem("probs_ready")
        s_rs = sem("sums_inverted")
        s_rb = sem("inverses_repeated")
        s_oc = sem("group_out_copied")
        s_on = sem("group_out_ready")
        s_scat = keep.s_xs_b
        s_pc = sem("positions_copied")
        s_pad = sem("pad_ready")
        s_chain, s_pick, s_rank = sem("sort_chain"), sem("pick_ready"), sem("rank_ready")
        s_aux = sem("unused_count")
        block = ctx.enter_context(nc.Block())
        QK_DMAS = 2 * GROUP
        PROJ_STEP = {0: "E", 2: "O", 4: "N", 8: "K"}

        LN2_AT = (1, 3, 5, 7)

        R_STEP = 11

        def steps():
            for s in range(-LEAD, UNITS):
                yield s

        def proj_at(s):
            if s >= 0 and (s % 16) in PROJ_STEP and s // 16 + 1 < NG:
                return PROJ_STEP[s % 16], s // 16 + 1
            return None

        def inverted_at(s):
            return s // 16 - 1 if s >= 16 and s % 16 == R_STEP else None

        def quad_at(s):
            return (s - 2) // 4 if s >= 5 and s % 4 == 1 else None

        def unit(u):
            return u // 16, (u % 16) // GROUP, u % GROUP

        def evac_pt_by_act(u):
            return u % GROUP == GROUP - 1

        @block.sync
        def _(sp):
            FIRST_LOADS = ("wqa", "wkva")
            EARLY = FIRST_LOADS + ("kcs",)
            for dst, src in ((wqa, "wqa"), (wkva, "wkva"), (wqb, "wqb"), (wk, "wk"), (wv, "wv"),
                             (cos4, "cos4"), (sin4, "sin4"), (kcs, "kcs")):
                sp.dma_start(dst if src in EARLY else dst.ap(), ext[src]).then_inc(s_wa if src in FIRST_LOADS else s_wp, 16)

            sp.dma_start(wo, ext["wo"]).then_inc(s_wo, 16)

            def load_x(b):
                xv = ext["x"].rearrange("(b t p) d -> p b t d", p=P, t=TB)
                sp.dma_start(x1[:, bass.ds(b * TB, TB), :],
                             xv[:, bass.ds(b, 1), :, :].rearrange("p a t d -> p (a t) d")).then_inc(s_xr, 16)

            def group(b, g):
                n = b * NG + g
                sp.wait_ge(s_rope, n * 2 + 2 + 2)
                for j in range(GROUP):
                    slot = (g % 2) * GROUP + j
                    rows = slice(j * 32, j * 32 + 32)
                    sp.dma_start(QT[0:32, slot, :], rEO[rows, 0, :]).then_inc(s_qk, 16)
                    sp.dma_start(QT[32:64, slot, :], rEO[rows, 1, :]).then_inc(s_qk, 16)

            def repeat_kpe(b):
                sp.wait_ge(s_kpe, b + 2)
                sp.dma_start(KT[0:ROPE, 1:2 * GROUP, :],
                             KT[0:ROPE, 0:1, :].to_broadcast([ROPE, 2 * GROUP - 1, SEQ])).then_inc(s_kr, 16)

            group(0, 0)
            repeat_kpe(0)
            with sp.Fori(0, BATCH - 1) as b:
                group(b, 1)
                load_x(b + 1)
                for g in range(2, NG):
                    group(b, g)
                group(b + 1, 0)
                repeat_kpe(b + 1)
            for g in range(1, NG):
                group(BATCH - 1, g)

        @block.gpsimd
        def _(pool):
            g = nc.gpsimd
            pool.sem_inc(s_rope, 2)
            pool.sem_inc(s_rb, 1)
            pool.sem_inc(s_kpe, 1)
            pool.sem_inc(s_qk, 16 * QK_DMAS)
            g.memset(half.ap(), -0.5).then_inc(s_cst, 1)
            g.memset(epsc.ap(), EPS).then_inc(s_ones, 1)
            g.memset(identb.ap(), 0.0).then_inc(s_cst, 1)
            g.memset(maskb.ap(), 0.0).then_inc(s_cst, 1)
            pool.wait_ge(s_cst, 3)
            pool.wait_ge(s_ones, 1)
            g.affine_select(out=identb.ap(), in_=identb.ap(), compare_op=ALU.not_equal, fill=1.0, base=0,
                            pattern=[[-1, P]], channel_multiplier=1).then_inc(s_cst, 1)
            g.affine_select(out=maskb.ap(), in_=maskb.ap(), compare_op=ALU.is_ge, fill=MASKED, base=0,
                            pattern=[[-1, P]], channel_multiplier=1).then_inc(s_cst, 1)

            def inverse_root(b, mv, var, rstd, s_mv, s_step, s_out):
                pool.wait_ge(s_mv, b * TB + TB)
                g.tensor_tensor(out=var.ap(), in0=mv[:, :, 1], in1=epsc.ap(), op=ALU.add).then_inc(s_step, 1)
                pool.wait_ge(s_step, b + 1)
                g.tensor_tensor(out=rstd.ap(), in0=var.ap(), in1=half.ap(), op=ALU.pow).then_inc(s_out, 1)

            def rope_sums(b, gi):
                n = b * NG + gi
                pool.wait_ge(s_rot, n * 4 + 4)
                pool.wait_ge(s_qk, n * (16 * QK_DMAS) + 16 * QK_DMAS)
                g.tensor_tensor(out=rEO[:, 0, :], in0=rot[:, 0, :], in1=rot[:, 2, :], op=ALU.subtract).then_inc(s_rope, 1)
                g.tensor_tensor(out=rEO[:, 1, :], in0=rot[:, 1, :], in1=rot[:, 3, :], op=ALU.add).then_inc(s_rope, 1)

            def pro(b):
                rope_sums(b, 0)
                pool.wait_ge(s_kpt, b * 2 + 2)
                g.tensor_tensor(out=KT[0:ROPE, 0, :], in0=kpt[:, 0, :], in1=kpt[:, 1, :], op=ALU.add).then_inc(s_kpe, 1)

            def repeat(b, gi):
                n = b * NG + gi
                pool.wait_ge(s_rs, n + 3)
                pool.wait_ge(s_on, n + 1)
                pool.sem_inc(s_aux, 1)
                g.tensor_copy(rsum[:, :, :], rinv[:, :].unsqueeze(2).to_broadcast([P, TB * GROUP, VD])).then_inc(s_rb, 1)

            def split(b, gi):
                n = b * NG + gi
                pool.wait_ge(s_og, n + 1)
                pool.sem_inc(s_aux, 1)
                g.tensor_copy(OT_high[:, gi, :], osb[:, :]).then_inc(s_oh, 1)
                pool.wait_ge(s_oh, n + 1)
                pool.sem_inc(s_aux, 1)
                g.tensor_tensor(out=OT_low[:, gi, :], in0=osb[:, :], in1=OT_high[:, gi, :].bitcast(F32),
                                op=ALU.subtract).then_inc(s_on, 1)

            def split_wo():
                pool.wait_ge(s_wo, 16)
                for c in range(DC):
                    g.tensor_copy(wo_high[:, c, :], wo[:, c, :]).then_inc(s_wh, 1)
                for c in range(DC):
                    pool.wait_ge(s_wh, c + 1)
                    g.tensor_tensor(out=wo_low[:, c, :], in0=wo[:, c, :], in1=wo_high[:, c, :].bitcast(F32),
                                    op=ALU.subtract).then_inc(s_wl, 1)

            def units(b, more, before):
                for gi in range(1, NG):
                    rope_sums(b, gi)
                    if gi == 1 and isinstance(b, int) and b == 0:
                        split_wo()
                    if gi == 1 and before is not None:
                        scatter(before)
                    if gi > 1:
                        repeat(b, gi - 2)
                        split(b, gi - 2)
                    if gi == 2 and more:
                        inverse_root(b + 1, mv1, var1, rstd1, s_mv1, s_p1, s_rs1)
                repeat(b, NG - 2)
                split(b, NG - 2)
                repeat(b, NG - 1)

            def epi(b):
                split(b, NG - 1)
                inverse_root(b, mv2, var2, rstd2, s_mv2, s_p2, s_rs2)

            def places(b):
                pool.wait_ge(s_scat, b * (16 * TB) + 16)
                pool.sem_inc(s_aux, 1)
                g.tensor_copy(pos_cur[:, :], pos_b[:, bass.ds(b * TB, TB)]).then_inc(s_pc, 1)

            def scatter(b):
                places(b)
                for t in range(TB):
                    pool.wait_ge(keep.s_clr_b, 16 * (NB_B - 1))
                    pool.wait_ge(s_pc, b + 1)
                    pool.sem_inc(s_aux, 1)
                    pool.wait_ge(s_xo, b * TB + t + 1)
                    pool.sem_inc(s_aux, 1)
                    g.indirect_dma_start(out=xs_b, out_offset=bass.IndirectOffsetOnAxis(ap=pos_cur[:, t:t + 1].bitcast(U32), axis=0),
                                         in_=xo[:, t, :], in_offset=None).then_inc(s_scat, 16)

            inverse_root(0, mv1, var1, rstd1, s_mv1, s_p1, s_rs1)
            g.memset(pad[:, :], 0.0).then_inc(s_pad, 1)
            pool.wait_ge(s_pad, 1)
            g.iota(pad[:, DIM:DIM + 1].bitcast(I32), [[0, 1]], base=TOKENS, channel_multiplier=1).then_inc(s_pad, 1)
            pool.wait_ge(s_pad, 2)
            pro(0)
            clear_first(pool, keep, pad)
            units(0, True, None)
            with pool.Fori(0, BATCH - 2) as b:
                pro(b + 1)
                epi(b)
                units(b + 1, True, b)
            pro(BATCH - 1)
            epi(BATCH - 2)
            units(BATCH - 1, False, BATCH - 2)
            epi(BATCH - 1)
            places(BATCH - 1)
            pool.wait_ge(keep.s_clr_b, 16 * (NB_B - 1))
            pool.wait_ge(s_pc, BATCH)

        @block.vector
        def _(dve):
            v = nc.vector
            for k in range(8):
                if k != plan.OUT:
                    dve.sem_inc(free[k], 1)
            dve.sem_inc(s_rs, 2)
            dve.sem_inc(s_on, 1)

            def tile(section, name, b):
                k, n = plan.place(section, name, b)
                dve.wait_ge(filled[k], n + 1)
                return bank[k], free[k]

            def sort_tokens():
                do = Chain(dve, s_chain)
                idf, eid = sort.posf, sort.cmp[:, 0, :]
                dve.wait_ge(keep.s_ids, 16)
                do(v.tensor_copy(idf[:, :], keep.ids[:, :]))
                step = VOCAB // EX_B
                do(v.tensor_scalar(out=eid, in0=idf[:, :], scalar1=float(step), scalar2=None, op0=ALU.is_ge))
                for i in range(2, EX_B):
                    do(v.scalar_tensor_tensor(out=eid, in0=idf[:, :], scalar=float(i * step), in1=eid,
                                              op0=ALU.is_ge, op1=ALU.add))
                for i in range(EX_B):
                    do(v.tensor_scalar(out=sort.pick[:, i, :], in0=eid, scalar1=float(i), scalar2=None, op0=ALU.is_equal))
                v.tensor_copy(sort.pickb[:, :, :], sort.pick[:, :, :]).then_inc(s_pick, 1)
                dve.wait_ge(s_rank, 1)
                sort.on_vector(v, do, bank[plan.OUT], keep.pos_b[:, :], keep.ex_b[:, :])
                dve.sem_inc(free[plan.OUT], 1)

            def rows(b, t):
                return x1[:, bass.ds(b * TB + t, 1), :].rearrange("p a d -> p (a d)")

            def stats(b, t, src, st, mv, s_chain, s_out, before, per):
                v.bn_stats(st[:, t, :], src).then_inc(s_chain, 1)
                dve.wait_ge(s_chain, b * per + before + 1)
                dve.sem_inc(s_aux, 1)
                v.bn_aggr(mv[:, t, :], st[:, t, :]).then_inc(s_out, 1)

            def ln1_stats(b, t):
                stats(b, t, rows(b, t), st1, mv1, s_c1, s_mv1, t, TB)

            def ln1_norm(b, t):
                if t == 0:
                    if not isinstance(b, int):
                        dve.wait_ge(s_scat, b * (16 * TB) - (16 * TB - 16))
                        dve.sem_inc(s_aux, 1)
                    dve.wait_ge(s_rs1, b + 1)
                v.tensor_scalar(out=xn[:, t, :], in0=rows(b, t), scalar1=mv1[:, t, 0:1], scalar2=rstd1[:, t:t + 1],
                                op0=ALU.subtract, op1=ALU.mult).then_inc(s_xn, 1)

            def rope_products(section, kind, b, g):
                n = b * NG + g
                ps, done = tile(section, (kind, g), b)
                if kind == "E":
                    dve.wait_ge(s_rope, n * 2 + 2)
                    v.tensor_tensor(out=rot[:, 0, :], in0=ps[:, :], in1=cos4[:, :], op=ALU.mult).then_inc(s_rot, 1)
                    v.tensor_tensor(out=rot[:, 1, :], in0=ps[:, :], in1=sin4[:, :], op=ALU.mult).then_inc(s_rot, 1)
                    dve.wait_ge(s_rot, n * 4 + 2)
                else:
                    v.tensor_tensor(out=rot[:, 2, :], in0=ps[:, :], in1=sin4[:, :], op=ALU.mult).then_inc(s_rot, 1)
                    v.tensor_tensor(out=rot[:, 3, :], in0=ps[:, :], in1=cos4[:, :], op=ALU.mult).then_inc(s_rot, 1)
                    dve.wait_ge(s_rot, n * 4 + 4)
                dve.sem_inc(done, 1)

            def pro(b):
                for c in range(1, DC, 2):
                    ps, done = tile("pro", ("xT", c), b)
                    v.tensor_copy(xT[:, c, :], ps[:, :]).then_inc(done, 1)
                dve.wait_ge(s_wp, 16 * 6)
                rope_products("pro", "E", b, 0)
                rope_products("pro", "O", b, 0)
                ps, done = tile("pro", ("kpe",), b)
                dve.wait_ge(s_kpe, b + 1)
                v.tensor_tensor(out=kpt[:, 0, :], in0=ps[0:ROPE, :], in1=kcs[0:ROPE, :], op=ALU.mult).then_inc(s_kpt, 1)
                v.tensor_tensor(out=kpt[:, 1, :], in0=ps[ROPE:P, :], in1=kcs[ROPE:P, :], op=ALU.mult).then_inc(s_kpt, 1)
                dve.wait_ge(s_kpt, b * 2 + 2)
                dve.sem_inc(done, 1)
                for t in range(1, TB, 2):
                    ps, done = tile("pro", ("V", t), b)
                    v.tensor_copy(V[:, t, :], ps[:, :]).then_inc(done, 1)

            def neg_max(b, u):
                _, i, _ = unit(u)
                ps, _ = tile("units", ("S", u), b)
                if u >= 2 * LEAD:
                    dve.wait_ge(s_exp, b * UNITS + u - 2 * LEAD + 1)
                v.tensor_reduce(out=negmax[:, u % (2 * LEAD):u % (2 * LEAD) + 1], in_=ps[:, 0:(i + 1) * P], axis=AX.X, op=ALU.max,
                                negate=True).then_inc(s_nm, 1)

            def evac_pt(b, u):
                _, i, j = unit(u)
                ps, done = tile("units", ("PT", u), b)
                v.tensor_copy(PTs[:, (u // GROUP) % 2, j, 0:(i + 1) * P], ps[:, 0:(i + 1) * P]).then_inc(done, 1)

            def invert(b, g):
                n = b * NG + g
                dve.wait_ge(s_exp, b * UNITS + (g + 1) * 16)
                dve.wait_ge(s_rb, n + 1)
                v.reciprocal(rinv[:, :], sums[:, g % 2, :, :].rearrange("p t j -> p (t j)")).then_inc(s_rs, 1)

            def group_out(section, b, g):
                n = b * NG + g
                ps, done = tile(section, ("R", g), b)
                dve.wait_ge(s_oc, n + 1)
                v.tensor_tensor(out=osb[:, :], in0=ps[:, :], in1=osb[:, :], op=ALU.mult).then_inc(s_og, 1)
                dve.wait_ge(s_og, n + 1)
                dve.sem_inc(done, 1)

            def units(b, more, before):
                for s in steps():
                    if s + LEAD < UNITS:
                        neg_max(b, s + LEAD)
                    p = proj_at(s)
                    if p and p[0] in "EO":
                        rope_products("units", p[0], b, p[1])
                    if 0 <= s + 1 < UNITS and not evac_pt_by_act(s + 1):
                        evac_pt(b, s + 1)
                    if inverted_at(s + 5) is not None:
                        invert(b, inverted_at(s + 5))
                    if inverted_at(s) is not None:
                        group_out("units", b, inverted_at(s))
                    if before is not None and 0 <= s + LEAD <= TB - TB // 2:
                        ln2_later(before, TB // 2 + s + LEAD)
                    if before is not None and s in LN2_AT:
                        ln2_norm(before, LN2_AT.index(s))
                    if more and s == 20:
                        dve.wait_ge(s_xr, b * 16 + 16)
                    if more and s in (20, 24, 28, 32):
                        ln1_stats(b + 1, (s - 20) // 4)
                    if more and s in (48, 50, 52, 54):
                        ln1_norm(b + 1, (s - 48) // 2)
                invert(b, NG - 1)

            def ln2_stats(b, t):
                k, n = plan.place("epi", ("Wo", t), b)
                dve.wait_ge(free[k], n + 2)
                dve.sem_inc(s_aux, 1)
                v.bn_stats(st2[:, t, :], rows(b, t)).then_inc(s_c2, 1)

            def ln2_aggregate(b, t):
                dve.wait_ge(s_c2, b * TB + t + 1)
                dve.sem_inc(s_aux, 1)
                v.bn_aggr(mv2[:, t, :], st2[:, t, :]).then_inc(s_mv2, 1)

            def ln2_later(b, t):
                if t < TB:
                    ln2_stats(b, t)
                ln2_aggregate(b, t - 1)

            def epi(b):
                group_out("epi", b, NG - 1)

                def add(t):
                    ps, done = tile("epi", ("Wo", t), b)
                    v.tensor_tensor(out=rows(b, t), in0=ps[:, :], in1=rows(b, t), op=ALU.add).then_inc(done, 1)

                for t in range(TB):
                    add(t)
                    if 1 <= t < TB - 1:
                        ln2_stats(b, t - 1)
                    if 2 <= t < TB - 1:
                        ln2_aggregate(b, t - 2)

            def ln2_norm(b, t):
                if t == 0:
                    dve.wait_ge(s_scat, b * (16 * TB) + 16)
                    dve.sem_inc(s_aux, 1)
                    dve.wait_ge(s_rs2, b + 1)
                v.tensor_scalar(out=xo[:, t, :], in0=rows(b, t), scalar1=mv2[:, t, 0:1], scalar2=rstd2[:, t:t + 1],
                                op0=ALU.subtract, op1=ALU.mult).then_inc(s_xo, 1)

            dve.wait_ge(s_x0, 16)
            for t in range(TB):
                ln1_stats(0, t)
            for t in range(TB):
                ln1_norm(0, t)
            pro(0)
            sort_tokens()
            units(0, True, None)
            with dve.Fori(0, BATCH - 2) as b:
                pro(b + 1)
                epi(b)
                units(b + 1, True, b)
            pro(BATCH - 1)
            epi(BATCH - 2)
            units(BATCH - 1, False, BATCH - 2)
            epi(BATCH - 1)
            for t in range(TB // 2, TB + 1):
                ln2_later(BATCH - 1, t)
            for t in range(TB):
                ln2_norm(BATCH - 1, t)

        @block.scalar
        def _(act):
            a = nc.scalar

            def tile(section, name, b):
                k, n = plan.place(section, name, b)
                act.wait_ge(filled[k], n + 1)
                return bank[k], free[k]

            def evac_nk(section, kind, b, g, heads=range(GROUP)):
                n = b * NG + g
                ps, done = tile(section, (kind, g), b)
                for j in heads:
                    rows = slice(j * NOPE, (j + 1) * NOPE)
                    dst = (QT if kind == "N" else KT)[ROPE:QK, (g % 2) * GROUP + j, :]
                    a.activation(dst, ps[rows, :], ACT.Copy, scale=QK ** -0.5 if kind == "N" else 1.0).then_inc(s_nk, 1)
                if GROUP - 1 not in heads:
                    return
                act.wait_ge(s_nk, n * (2 * GROUP) + (GROUP if kind == "N" else 2 * GROUP))
                act.sem_inc(done, 1)

            def pro(b):
                for c in range(0, DC, 2):
                    ps, done = tile("pro", ("xT", c), b)
                    a.copy(xT[:, c, :], ps[:, :]).then_inc(done, 1)
                for name, dst in (("qa", qaT), ("ckv", cT)):
                    ps, done = tile("pro", (name,), b)
                    a.copy(dst[:, :], ps[:, :]).then_inc(done, 1)
                evac_nk("pro", "N", b, 0)
                evac_nk("pro", "K", b, 0)
                for t in range(0, TB, 2):
                    ps, done = tile("pro", ("V", t), b)
                    a.copy(V[:, t, :], ps[:, :]).then_inc(done, 1)

            def exps(b, u):
                g, i, j = unit(u)
                if u % 16 == 0:
                    act.wait_ge(s_rs, b * NG + g + 1)
                act.wait_ge(s_nm, b * UNITS + u + 1)
                ps, done = tile("units", ("S", u), b)
                if u >= LEAD:
                    k, n = plan.place("units", ("PT", u - LEAD), b)
                    act.wait_ge(filled[k], n + 1)
                a.activation(probs[:, u % LEAD, 0:(i + 1) * P], ps[:, 0:(i + 1) * P], ACT.Exp,
                             bias=negmax[:, u % (2 * LEAD):u % (2 * LEAD) + 1], accum_out=sums[:, g % 2, i, j:j + 1]).then_inc(s_exp, 1)
                act.wait_ge(s_exp, b * UNITS + u + 1)
                act.sem_inc(done, 1)

            def copy_out(b, g):
                n = b * NG + g
                ps, done = tile("units", ("out", g), b)
                act.wait_ge(s_on, n + 1)
                a.copy(osb[:, :], ps[:, :]).then_inc(s_oc, 1)
                act.wait_ge(s_oc, n + 1)
                act.sem_inc(done, 1)

            def background(b, s):
                if isinstance(b, int) and b == 0:
                    if s % 3 == 0 and 1 <= s // 3 < NB_B:
                        clear_b(act, keep, pad, s // 3 - 1)
                elif s % 4 == 0 and 1 <= s // 4 <= CLEARS_C:
                    clear_c(act, keep, pad, b * CLEARS_C + (s // 4 - 1 - CLEARS_C))
                if isinstance(b, int) and b == BATCH - 1 and s % 4 == 2 and 3 <= s // 4 < 3 + EX_B:
                    e, n = s // 4 - 3, DC * DIM
                    act.wait_ge(s_wl, DC)
                    act.dma_start(keep.arena[:, e * n:(e + 1) * n], ext["ctxT"][:, e * n:(e + 1) * n]).then_inc(keep.s_ctx, 16)

            def units(b):
                for s in steps():
                    background(b, s)
                    if s + LEAD < UNITS:
                        exps(b, s + LEAD)
                    p = proj_at(s)
                    if p and p[0] in "NK":
                        evac_nk("units", p[0], b, p[1], range(0, GROUP // 2))
                    p = proj_at(s - 1)
                    if p and p[0] in "NK":
                        evac_nk("units", p[0], b, p[1], range(GROUP // 2, GROUP))
                    if 0 <= s + 1 < UNITS and evac_pt_by_act(s + 1):
                        _, i, j = unit(s + 1)
                        ps, done = tile("units", ("PT", s + 1), b)
                        a.copy(PTs[:, ((s + 1) // GROUP) % 2, j, 0:(i + 1) * P], ps[:, 0:(i + 1) * P]).then_inc(done, 1)
                    q = quad_at(s)
                    if q is not None and q % TB == TB - 1:
                        copy_out(b, q // TB)
                copy_out(b, NG - 1)

            pro(0)
            act.wait_ge(s_pad, 2)
            units(0)
            with act.Fori(1, BATCH - 1) as b:
                pro(b)
                units(b)
            pro(BATCH - 1)
            units(BATCH - 1)
            act.wait_ge(keep.s_clr_c, 16 * CLEARS_C * (BATCH - 1))

        @block.tensor
        def _(pe):
            te = nc.tensor

            def tile(section, name, b):
                k, n = plan.place(section, name, b)
                pe.wait_ge(free[k], n + 1)
                return bank[k], filled[k]

            def evacuated(section, name, b):
                k, n = plan.place(section, name, b)
                pe.wait_ge(free[k], n + 2)

            def mul(out, pairs, done):
                for n, (l, r) in enumerate(pairs):
                    last = te.matmul(out, l, r, start=(n == 0), stop=(n == len(pairs) - 1))
                last.then_inc(done, 1)

            def project(section, kind, b, g):
                ps, done = tile(section, (kind, g), b)
                w, src = {"E": (wqb[:, 3 * g, :], qaT), "O": (wqb[:, 3 * g + 1, :], qaT),
                          "N": (wqb[:, 3 * g + 2, :], qaT), "K": (wk[:, g, :], cT)}[kind]
                mul(ps[:, :], [(w, src[:, :])], done)

            def pro(b):
                pe.wait_ge(s_xn, b * TB + TB)
                for c in range(DC):
                    ps, done = tile("pro", ("xT", c), b)
                    for t in range(TB):
                        last = te.transpose(ps[:, t * P:(t + 1) * P], xn[:, t, c * P:(c + 1) * P], ident[:, :])
                    last.then_inc(done, 1)
                for c in range(DC):
                    evacuated("pro", ("xT", c), b)
                pe.wait_ge(s_wa, 16 * 2)
                for name, w in (("qa", wqa[:, :, :]), ("ckv", wkva[:, :, 0:LORA])):
                    ps, done = tile("pro", (name,), b)
                    mul(ps[:, :], [(w[:, c, :], xT[:, c, :]) for c in range(DC)], done)
                evacuated("pro", ("qa",), b)
                pe.wait_ge(s_wp, 16 * 6)
                for kind in "EON":
                    project("pro", kind, b, 0)
                evacuated("pro", ("ckv",), b)
                project("pro", "K", b, 0)
                ps, done = tile("pro", ("kpe",), b)
                mul(ps[:, :], [(wkva[:, c, LORA:], xT[:, c, :]) for c in range(DC)], done)
                for t in range(TB):
                    ps, done = tile("pro", ("V", t), b)
                    mul(ps[:, :], [(cT[:, t * P:(t + 1) * P], wv[:, :])], done)

            def scores(b, u):
                g, i, j = unit(u)
                slot = (g % 2) * GROUP + j
                if u % 16 == 0:
                    n = b * NG + g
                    pe.wait_ge(s_qk, n * (16 * QK_DMAS) + 2 * (16 * QK_DMAS))
                    pe.wait_ge(s_nk, n * (2 * GROUP) + 2 * GROUP)
                ps, done = tile("units", ("S", u), b)
                te.matmul(ps[:, 0:(i + 1) * P], QT[:, slot, i * P:(i + 1) * P], KT[:, slot, 0:(i + 1) * P],
                          start=True, stop=False)
                te.matmul(ps[:, i * P:(i + 1) * P], identb[:, :], maskb[:, :], start=False, stop=True).then_inc(done, 1)

            def transposes(b, u):
                _, i, _ = unit(u)
                pe.wait_ge(s_exp, b * UNITS + u + 1)
                ps, done = tile("units", ("PT", u), b)
                for j in range(i + 1):
                    last = te.transpose(ps[:, j * P:(j + 1) * P], probs[:, u % LEAD, j * P:(j + 1) * P], ident[:, :])
                last.then_inc(done, 1)

            def values(b, q):
                g, i = q // TB, q % TB
                for u in range(q * GROUP + 2, q * GROUP + GROUP):
                    evacuated("units", ("PT", u), b)
                if i == 0:
                    tile("units", ("out", g), b)
                k, _ = plan.place("units", ("out", g), b)
                for j in range(i + 1):
                    for h in range(GROUP):
                        last = te.matmul(bank[k][h * VD:(h + 1) * VD, i * P:(i + 1) * P],
                                         V[:, j, (g * GROUP + h) * VD:(g * GROUP + h + 1) * VD],
                                         PTs[:, q % 2, h, j * P:(j + 1) * P], start=(j == 0), stop=(j == i))
                if i == TB - 1:
                    last.then_inc(filled[k], 1)

            def spread(section, b, g):
                pe.wait_ge(s_rb, b * NG + g + 2)
                ps, done = tile(section, ("R", g), b)
                for i in range(TB):
                    last = te.transpose(ps[:, i * P:(i + 1) * P],
                                        rsum[:, i * GROUP:(i + 1) * GROUP, :].rearrange("p j d -> p (j d)"), ident[:, :])
                last.then_inc(done, 1)

            def units(b):
                pe.wait_ge(s_kr, b * 16 + 16)
                for t in range(TB):
                    evacuated("pro", ("V", t), b)
                for s in steps():
                    if s + LEAD < UNITS:
                        scores(b, s + LEAD)
                    p = proj_at(s)
                    if p:
                        project("units", p[0], b, p[1])
                    if inverted_at(s) is not None:
                        spread("units", b, inverted_at(s))
                    if 0 <= s + 1 < UNITS:
                        transposes(b, s + 1)
                    if quad_at(s) is not None:
                        values(b, quad_at(s))
                values(b, UNITS // GROUP - 1)

            def epi(b):
                spread("epi", b, NG - 1)
                pe.wait_ge(s_wl, DC)
                pe.wait_ge(s_on, b * NG + NG)

                def products(t, ps, groups):
                    tokens = slice(t * P, (t + 1) * P)
                    for c in groups:
                        te.matmul(ps[:, :], OT_high[:, c, tokens], wo_high[:, c, :], start=(c == 0), stop=False)
                        te.matmul(ps[:, :], OT_high[:, c, tokens], wo_low[:, c, :], start=False, stop=False)
                        last = te.matmul(ps[:, :], OT_low[:, c, tokens], wo_high[:, c, :], start=False, stop=(c == NG - 1))
                    return last

                AHEAD = TB - 1
                places = [tile("epi", ("Wo", t), b) for t in range(AHEAD)]
                for t in range(AHEAD):
                    products(t, places[t][0], range(NG - 1))
                pe.wait_ge(s_on, b * NG + NG + 1)
                for t in range(AHEAD):
                    products(t, places[t][0], [NG - 1]).then_inc(places[t][1], 1)
                for t in range(AHEAD, TB):
                    ps, done = tile("epi", ("Wo", t), b)
                    products(t, ps, range(NG)).then_inc(done, 1)

            pe.wait_ge(s_cst, 5)
            pe.wait_ge(s_ones, 1)
            pro(0)
            pe.wait_ge(s_pick, 1)
            sort.on_tensor(te, bank[plan.OUT]).then_inc(s_rank, 1)
            with pe.Fori(0, BATCH - 1) as b:
                units(b)
                pro(b + 1)
                epi(b)
            units(BATCH - 1)
            epi(BATCH - 1)


class Keep:

    def __init__(self, nc, ctx, ext):
        def sb(name, shape, dt=F32):
            return ctx.enter_context(nc.sbuf_tensor(name, shape, dt))

        def dram(name, shape):
            return nc.dram_tensor(name, shape, F32, kind="Internal").ap()

        self.x1 = sb("x1", [P, NT, DIM])
        self.xn = sb("xn", [P, TB * DIM])
        self.pos_cur = sb("pos_cur", [P, TB], I32)
        self.ident = sb("ident", [P, P])
        self.arena = sb("arena", [P, EX_B * DC * DIM])
        self.upper = sb("upper", [P, P], BF16)
        self.ones = sb("ones", [P, P], BF16)
        self.full = sb("full", [P, NT])
        self.number = sb("number", [P, NB_C])
        self.one = sb("one", [P, NT * TOPK])
        self.token = sb("token", [P, NT], I32)
        self.ids = sb("ids", [P, NT], I32)
        self.pos_b = sb("pos_b", [P, NT], I32)
        self.ex_b = sb("ex_b", [P, NB_B], I32)
        self.xs_b = dram("xs_b", [NB_B * P, DIM])
        self.ys_b = dram("ys_b", [NB_B * P, DIM])
        self.xs_c = dram("xs_c", [NB_C * P, ROW])
        self.s_ids = ctx.enter_context(nc.semaphore("ids_loaded"))
        self.s_x0 = ctx.enter_context(nc.semaphore("x_first_loaded"))
        self.s_xr = ctx.enter_context(nc.semaphore("x_rest_loaded"))
        self.s_clr_b = ctx.enter_context(nc.semaphore("xs_b_cleared"))
        self.s_clr_c = ctx.enter_context(nc.semaphore("xs_c_cleared"))
        self.s_xs_b = ctx.enter_context(nc.semaphore("xs_b_written"))
        self.s_xs_c = [ctx.enter_context(nc.semaphore(f"xs_c_written{t}")) for t in range(TB)]
        self.s_add = ctx.enter_context(nc.semaphore("routed_rows_added"))
        self.s_ctx = ctx.enter_context(nc.semaphore("ctx_loaded"))
        self.out = ext["out"]


ROW = 576


CLEARS_C = -(-(NB_C - TB) // (BATCH - 1))


def clear_first(pool, keep, pad):
    pool.dma_start(keep.xs_b[(NB_B - 1) * P:, :], pad[:, 0:DIM]).then_inc(keep.s_xs_b, 16)
    for t in range(TB):
        n = NB_C - TB + t
        pool.dma_start(keep.xs_c[n * P:(n + 1) * P, :], pad[:, :]).then_inc(keep.s_xs_c[t], 16)
    pool.dma_start(keep.out[TOKENS:TOKENS + P, :], pad[:, 0:DIM]).then_inc(keep.s_add, 16)


def clear_b(eng, keep, pad, n):
    eng.dma_start(keep.xs_b[n * P:(n + 1) * P, :], pad[:, 0:DIM]).then_inc(keep.s_clr_b, 16)


def clear_c(eng, keep, pad, n):
    xs = keep.xs_c[0:CLEARS_C * (BATCH - 1) * P, :].rearrange("(n p) d -> n p d", p=P)
    eng.dma_start(xs[bass.ds(n, 1), :, :].rearrange("a p d -> (a p) d"), pad[:, :]).then_inc(keep.s_clr_c, 16)


class Chain:

    def __init__(self, eng, s):
        self.eng, self.s, self.n = eng, s, 0

    def __call__(self, ins):
        self.n += 1
        ins.then_inc(self.s, 1)
        self.eng.wait_ge(self.s, self.n)


def carve(region):
    used = [0]

    def take(name, shape, dt=F32):
        n = 1
        for k in shape[1:]:
            n *= k
        words = n if dt != BF16 else n // 2
        flat = region[:, used[0]:used[0] + words]
        used[0] += words
        if dt != F32:
            flat = flat.bitcast(dt)
        if len(shape) == 3:
            flat = flat.rearrange("p (a b) -> p a b", a=shape[1])
        return flat
    return take


class Sorter:

    def __init__(self, sb, keep, name, experts, tiles, blocks):
        self.keep, self.e, self.n, self.b = keep, experts, tiles, blocks
        self.pick = sb(f"{name}_pick", [P, experts, tiles])
        self.pickb = sb(f"{name}_pickb", [P, experts, tiles], BF16)
        self.cnt = sb(f"{name}_cnt", [P, experts, tiles])
        self.run = sb(f"{name}_run", [P, experts, tiles])
        self.cmp = sb(f"{name}_cmp", [P, experts, NT])
        self.nb = sb(f"{name}_nb", [P, experts])
        self.ends = sb(f"{name}_ends", [P, experts])
        self.base = sb(f"{name}_base", [P, experts])
        self.off = sb(f"{name}_off", [P, experts, tiles])
        self.posf = sb(f"{name}_posf", [P, tiles])
        self.bcmp = sb(f"{name}_bcmp", [P, blocks, experts - 1])
        self.exf = sb(f"{name}_exf", [P, blocks])

    def on_tensor(self, te, ps):
        w = self.e * self.n
        flat = self.pickb[:, :, :].rearrange("p e n -> p (e n)")
        te.matmul(ps[:, 0:w], self.keep.upper[:, :], flat, start=True, stop=True)
        return te.matmul(ps[:, w:2 * w], self.keep.ones[:, :], flat, start=True, stop=True)

    def on_vector(self, v, do, ps, pos, ex, pause=None):
        w, e, n = self.e * self.n, self.e, self.n
        above = ps[:, 0:w].rearrange("p (e n) -> p e n", e=e)
        count = ps[:, w:2 * w].rearrange("p (e n) -> p e n", e=e)
        do(v.tensor_copy(self.cnt[:, :, :], count))
        for i in range(e):
            do(v.tensor_tensor_scan(self.run[:, i, :], self.keep.one[:, 0:n], self.cnt[:, i, :], 0.0,
                                    ALU.mult, ALU.add))
        total = self.run[:, :, n - 1:n]
        do(v.tensor_tensor(out=self.cmp[:, :, :], in0=total.to_broadcast([P, e, NT]),
                           in1=self.keep.full[:, :].unsqueeze(1).to_broadcast([P, e, NT]), op=ALU.is_gt))
        do(v.tensor_reduce(out=self.nb[:, :], in_=self.cmp[:, :, :], axis=AX.X, op=ALU.add))
        do(v.tensor_tensor_scan(self.ends[:, :], self.keep.one[:, 0:e], self.nb[:, :], 0.0, ALU.mult, ALU.add))
        do(v.tensor_tensor(out=self.base[:, :], in0=self.ends[:, :], in1=self.nb[:, :], op=ALU.subtract))
        if pause:
            pause()
        do(v.tensor_tensor(out=self.off[:, :, :], in0=self.run[:, :, :], in1=self.cnt[:, :, :], op=ALU.subtract))
        do(v.scalar_tensor_tensor(out=self.off[:, :, :], in0=self.base[:, :].unsqueeze(2).to_broadcast([P, e, n]),
                                  scalar=float(P), in1=self.off[:, :, :], op0=ALU.mult, op1=ALU.add))
        do(v.tensor_tensor(out=self.off[:, :, :], in0=above, in1=self.off[:, :, :], op=ALU.add))
        do(v.tensor_tensor(out=self.off[:, :, :], in0=self.off[:, :, :], in1=self.pick[:, :, :], op=ALU.mult))
        do(v.tensor_reduce(out=self.posf[:, :], in_=self.off[:, :, :].rearrange("p e n -> p n e"), axis=AX.X, op=ALU.add))
        do(v.tensor_copy(pos, self.posf[:, :]))
        b = self.b
        do(v.tensor_tensor(out=self.bcmp[:, :, :],
                           in0=self.keep.number[:, 0:b].unsqueeze(2).to_broadcast([P, b, e - 1]),
                           in1=self.ends[:, 0:e - 1].unsqueeze(1).to_broadcast([P, b, e - 1]), op=ALU.is_ge))
        do(v.tensor_reduce(out=self.exf[:, :], in_=self.bcmp[:, :, :], axis=AX.X, op=ALU.add))
        do(v.tensor_copy(ex, self.exf[:, :]))


def setup_block(nc, ext, keep):
    with ExitStack() as ctx:
        s_pool = ctx.enter_context(nc.semaphore("setup_constants"))
        block = ctx.enter_context(nc.Block())

        @block.sync
        def _(sp):
            sp.dma_start(keep.x1[:, 0:TB, :], ext["x"].rearrange("(t p) d -> p t d", p=P)[:, 0:TB, :]).then_inc(keep.s_x0, 16)
            sp.dma_start(keep.ids[:, :], ext["ids"]).then_inc(keep.s_ids, 16)

        @block.gpsimd
        def _(pool):
            g = nc.gpsimd
            g.memset(keep.ident[:, :], 0.0).then_inc(s_pool, 1)
            g.memset(keep.upper[:, :], 1.0).then_inc(s_pool, 1)
            g.memset(keep.ones[:, :], 1.0).then_inc(s_pool, 1)
            g.memset(keep.one[:, :], 1.0).then_inc(s_pool, 1)
            g.iota(keep.full[:, :], [[P, NT]], base=0, channel_multiplier=0,
                   allow_small_or_imprecise_dtypes=True).then_inc(s_pool, 1)
            g.iota(keep.number[:, :], [[1, NB_C]], base=0, channel_multiplier=0,
                   allow_small_or_imprecise_dtypes=True).then_inc(s_pool, 1)
            g.iota(keep.token[:, :], [[P, NT]], base=0, channel_multiplier=1).then_inc(s_pool, 1)
            pool.wait_ge(s_pool, 7)
            g.affine_select(out=keep.ident[:, :], in_=keep.ident[:, :], compare_op=ALU.not_equal, fill=1.0, base=0,
                            pattern=[[-1, P]], channel_multiplier=1).then_inc(s_pool, 1)
            g.affine_select(out=keep.upper[:, :], in_=keep.upper[:, :], compare_op=ALU.is_gt, fill=0.0, base=0,
                            pattern=[[1, P]], channel_multiplier=-1).then_inc(s_pool, 1)
            pool.wait_ge(s_pool, 9)


class Experts:

    def __init__(self, nc, ctx, keep, name, w1, w2, left, right, rows=None, untransposed=0, w_low=None, w1_fixed=None, y=None):
        def sb(n, shape, dt=F32):
            return ctx.enter_context(nc.sbuf_tensor(f"{name}_{n}", shape, dt))

        def sem(n):
            return ctx.enter_context(nc.semaphore(f"{name}_{n}"))

        def ps(n):
            return ctx.enter_context(nc.psum_tensor(f"{name}_{n}", [P, 512], F32))

        self.nc, self.keep, self.w1, self.w2 = nc, keep, w1, w2
        self.left, self.right = left, right
        self.hid = left[1] - left[0]
        self.kc = self.hid // P
        self.rows = rows or [sb(f"rows{p}", [P, DIM]) for p in range(2)]
        self.skip = untransposed
        self.w_low = w_low
        self.w1_fixed = w1_fixed
        part = F32R if w_low is not None else F32
        self.xT = sb("xT", [P, 2, DC, P], part)
        self.sil = sb("sil", [P, 2, self.hid])
        self.a = sb("a", [P, 2, self.hid])
        self.aT = sb("aT", [P, 2, self.kc, P], part)
        self.y = y or [sb(f"y{p}", [P, DIM]) for p in range(2)]
        self.TX, self.HB = [ps(f"TX{p}") for p in range(2)], [ps(f"H{p}") for p in range(2)]
        self.TA, self.YB = ps("TA"), [ps(f"Y{p}") for p in range(2)]
        self.loaded = [sem(f"rows_loaded{p}") for p in range(2)]
        self.s_T, self.s_H, self.s_sil = sem("rows_transposed"), sem("first_product"), sem("silu_ready")
        self.s_xT = sem("xT_ready")
        self.s_a = sem("act_ready")
        self.s_T2 = sem("act_transposed")
        self.s_aT = sem("aT_ready")
        if w_low is not None:
            self.xTl = sb("xTl", [P, 2, DC, P], part)
            self.aTl = sb("aTl", [P, 2, self.kc, P], part)
            self.s_xTl = sem("xT_low_ready")
            self.s_aTl = sem("aT_low_ready")
        else:
            self.s_xTl, self.s_aTl = self.s_xT, self.s_aT
        self.s_Y = sem("second_product")
        self.s_yf = sem("product_taken")

    def start(self, pe):
        for s, n in ((self.s_xT, 2), (self.s_a, 2), (self.s_T2, 2), (self.s_aT, 1), (self.s_Y, 2), (self.s_yf, 2)):
            pe.sem_inc(s, n)
        if self.w_low is not None:
            pe.sem_inc(self.s_xTl, 2)
            pe.sem_inc(self.s_aTl, 1)

    def T(self, pe, it, p):
        j = it * 2 + p
        pe.wait_ge(self.loaded[p], it * 16 + (16 - self.skip // 2 * 16))
        pe.wait_ge(self.s_xTl, j + 1)
        for c in range(DC):
            last = self.nc.tensor.transpose(self.TX[p][:, c * P:(c + 1) * P], self.rows[p][:, c * P:(c + 1) * P],
                                            self.keep.ident[:, :])
        last.then_inc(self.s_T, 1)

    def weights(self, w, e, c):
        if isinstance(e, int):
            return self.w1_fixed[:, c, :] if w is self.w1 else w[:, e, c, :]
        return w[:, bass.ds(e, 1), c, :].rearrange("p a n -> p (a n)")

    def multiply(self, out, x, x_low, w, e, chunks):
        for c in range(chunks):
            terms = [(x[:, c, :], self.weights(w, e, c))]
            if self.w_low is not None:
                terms += [(x[:, c, :], self.weights(self.w_low, e, c)), (x_low[:, c, :], self.weights(w, e, c))]
            for n, (l, r) in enumerate(terms):
                last = self.nc.tensor.matmul(out, l, r, start=(c == 0 and n == 0), stop=(c == chunks - 1 and n == len(terms) - 1))
        return last

    def H(self, pe, it, p, e):
        j = it * 2 + p
        pe.wait_ge(self.s_xTl, j + 3)
        pe.wait_ge(self.s_a, j + 1)
        low = self.xTl[:, p, :, :] if self.w_low is not None else None
        self.multiply(self.HB[p][:, :], self.xT[:, p, :, :], low, self.w1, e, DC).then_inc(self.s_H, 1)

    def T2(self, pe, it, p):
        j = it * 2 + p
        pe.wait_ge(self.s_a, j + 3)
        pe.wait_ge(self.s_aTl, j + 1)
        for c in range(self.kc):
            last = self.nc.tensor.transpose(self.TA[:, c * P:(c + 1) * P], self.a[:, p, c * P:(c + 1) * P],
                                            self.keep.ident[:, :])
        last.then_inc(self.s_T2, 1)

    def Y(self, pe, it, p, e):
        j = it * 2 + p
        pe.wait_ge(self.s_aTl, j + 2)
        pe.wait_ge(self.s_yf, j + 1)
        low = self.aTl[:, p, :, :] if self.w_low is not None else None
        self.multiply(self.YB[p][:, :], self.aT[:, p, :, :], low, self.w2, e, self.kc).then_inc(self.s_Y, 1)

    def copy_xT(self, act, it, p):
        j = it * 2 + p
        act.wait_ge(self.s_T, j + (1 - self.skip))
        self.nc.scalar.copy(self.xT[:, p, :, :], self.TX[p][:, :].rearrange("p (c q) -> p c q", c=DC)).then_inc(self.s_xT, 1)

    def silu(self, act, it, p):
        j = it * 2 + p
        act.wait_ge(self.s_H, j + 1)
        act.wait_ge(self.s_a, j + 1)
        self.nc.scalar.activation(self.sil[:, p, :], self.HB[p][:, self.left[0]:self.left[1]], ACT.Silu).then_inc(self.s_sil, 1)

    def copy_aT(self, act, it, p):
        j = it * 2 + p
        act.wait_ge(self.s_T2, j + 3)
        act.wait_ge(self.s_Y, j + 1)
        self.nc.scalar.copy(self.aT[:, p, :, :],
                            self.TA[:, 0:self.hid].rearrange("p (c q) -> p c q", c=self.kc)).then_inc(self.s_aT, 1)

    def copy_y(self, act, it, p):
        j = it * 2 + p
        act.wait_ge(self.s_Y, j + 3)
        self.nc.scalar.copy(self.y[p][:, :], self.YB[p][:, :]).then_inc(self.s_yf, 1)

    def product(self, dve, it, p):
        j = it * 2 + p
        dve.wait_ge(self.s_sil, j + 1)
        dve.wait_ge(self.s_T2, j + 1)
        self.nc.vector.tensor_tensor(out=self.a[:, p, :], in0=self.HB[p][:, self.right[0]:self.right[1]],
                                     in1=self.sil[:, p, :], op=ALU.mult).then_inc(self.s_a, 1)

    def xT_low(self, dve, it, p):
        j = it * 2 + p
        dve.wait_ge(self.s_xT, j + 3)
        self.nc.vector.tensor_tensor(out=self.xTl[:, p, :, :], in0=self.TX[p][:, :].rearrange("p (c q) -> p c q", c=DC),
                                     in1=self.xT[:, p, :, :].bitcast(F32), op=ALU.subtract).then_inc(self.s_xTl, 1)

    def aT_low(self, dve, it, p):
        j = it * 2 + p
        dve.wait_ge(self.s_aT, j + 2)
        self.nc.vector.tensor_tensor(out=self.aTl[:, p, :, :], in0=self.TA[:, 0:self.hid].rearrange("p (c q) -> p c q", c=self.kc),
                                     in1=self.aT[:, p, :, :].bitcast(F32), op=ALU.subtract).then_inc(self.s_aTl, 1)


def load_w13(sp, ext, keep, e):
    sp.dma_start(keep.w13[:, bass.ds(e, 1), :, :].rearrange("p a c n -> p (a c) n"),
                 ext["w13"][:, bass.ds(e, 1), :, :].rearrange("p a c n -> p (a c) n")).then_inc(keep.s_wc, 16)


def load_w2(sp, ext, keep, e):
    sp.dma_start(keep.w2[:, bass.ds(e, 1), :, :].rearrange("p a c n -> p (a c) n"),
                 ext["w2"][:, bass.ds(e, 1), :, :].rearrange("p a c n -> p (a c) n")).then_inc(keep.s_wc, 16)


LOADS_EARLY = 1 + EX_C + 2
LOADS_ALL = LOADS_EARLY + EX_C


def id_expert_block(nc, ext, keep):
    with ExitStack() as ctx:
        ctxT = keep.arena[:, :].rearrange("p (e c n) -> p e c n", e=EX_B, c=DC)
        high, low = (ctx.enter_context(nc.sbuf_tensor(n, [P, EX_B, DC, DIM], F32R)) for n in ("ctx_high", "ctx_low"))
        quarters = [keep.xn[:, p * DIM:(p + 1) * DIM] for p in range(4)]
        ex = Experts(nc, ctx, keep, "b", high, high, (0, DIM), (0, DIM), quarters[0:2], w_low=low, y=quarters[2:4])
        s_high, s_low = (ctx.enter_context(nc.semaphore(n)) for n in ("ctx_high_ready", "ctx_low_ready"))
        stored = [ctx.enter_context(nc.semaphore(f"b_stored{p}")) for p in range(2)]
        block = ctx.enter_context(nc.Block())
        PAIRS = NB_B // 2
        LAST = NB_B - 1
        xs = keep.xs_b.rearrange("(n p) d -> n p d", p=P)
        ys = keep.ys_b.rearrange("(n p) d -> n p d", p=P)

        def at(view, j):
            return view[j, :, :] if isinstance(j, int) else view[bass.ds(j, 1), :, :].rearrange("a p d -> (a p) d")

        @block.gpsimd
        def _(pool):
            for t in range(TB):
                nc.gpsimd.indirect_dma_start(
                    out=keep.xs_b, out_offset=bass.IndirectOffsetOnAxis(ap=keep.pos_cur[:, t:t + 1].bitcast(U32), axis=0),
                    in_=keep.xn[:, t * DIM:(t + 1) * DIM], in_offset=None).then_inc(keep.s_xs_b, 16)

        @block.sync
        def _(sp):
            sp.wait_ge(keep.s_xs_b, BATCH * (16 * TB) + 16)
            for p in range(2):
                sp.dma_start(ex.rows[p][:, :], at(xs, p)).then_inc(ex.loaded[p], 16)
            sp.dma_start(keep.gate[:, :, :], ext["gate"]).then_inc(keep.s_wc, 16)
            assert PAIRS - 1 == EX_C

            def load_pair(it):
                for p in range(2):
                    sp.wait_ge(ex.s_T, it * 2 + p + 1)
                    sp.dma_start(ex.rows[p][:, :], at(xs, it * 2 + p + 2)).then_inc(ex.loaded[p], 16)
                load_w2(sp, ext, keep, it)

            with sp.Fori(0, EX_C) as it:
                load_pair(it)
            sp.wait_ge(ex.s_T, LAST - 1)
            sp.dma_start(ex.rows[0][:, :], at(xs, LAST)).then_inc(ex.loaded[0], 16)
            sp.dma_start(keep.w13s[:, :, :], ext["w13"][:, EX_C, :, :]).then_inc(keep.s_wc, 16)
            load_w2(sp, ext, keep, EX_C)

        @block.scalar
        def _(act):
            def y_out(it, p):
                if not (isinstance(it, int) and it == 0):
                    act.wait_ge(stored[p], it * 16)
                ex.copy_y(act, it, p)
                act.wait_ge(ex.s_yf, it * 2 + p + 3)
                act.dma_start(at(ys, it * 2 + p), ex.y[p][:, :]).then_inc(stored[p], 16)

            def step(it, p, more):
                nit, np_ = (it, 1) if p == 0 else (it + 1, 0)
                ex.copy_aT(act, it, p)
                ex.silu(act, nit, np_)
                if more:
                    ex.copy_xT(act, it + 1, p)
                y_out(it, p)

            act.wait_ge(keep.s_ctx, 16 * EX_B)
            for e in range(EX_B):
                nc.scalar.copy(high[:, e, :, :], ctxT[:, e, :, :]).then_inc(s_high, 1)
            ex.copy_xT(act, 0, 0)
            ex.copy_xT(act, 0, 1)
            ex.silu(act, 0, 0)
            step(0, 0, True)
            step(0, 1, True)
            with act.Fori(1, PAIRS - 1) as it:
                step(it, 0, True)
                step(it, 1, True)
            step(PAIRS - 1, 0, True)
            step(PAIRS - 1, 1, False)
            ex.copy_aT(act, PAIRS, 0)
            y_out(PAIRS, 0)
            act.wait_ge(stored[0], (PAIRS + 1) * 16)
            act.wait_ge(stored[1], PAIRS * 16)

        @block.vector
        def _(dve):
            for e in range(EX_B):
                dve.wait_ge(s_high, e + 1)
                nc.vector.tensor_tensor(out=low[:, e, :, :], in0=ctxT[:, e, :, :], in1=high[:, e, :, :].bitcast(F32),
                                        op=ALU.subtract).then_inc(s_low, 1)

            def step(it, p, more):
                nit, np_ = (it, 1) if p == 0 else (it + 1, 0)
                ex.aT_low(dve, it, p)
                ex.product(dve, nit, np_)
                if more:
                    ex.xT_low(dve, it + 1, p)

            ex.xT_low(dve, 0, 0)
            ex.xT_low(dve, 0, 1)
            ex.product(dve, 0, 0)
            with dve.Fori(0, PAIRS - 1) as it:
                step(it, 0, True)
                step(it, 1, True)
            step(PAIRS - 1, 0, True)
            step(PAIRS - 1, 1, False)
            ex.aT_low(dve, PAIRS, 0)

        @block.tensor
        def _(pe):
            def expert(j):
                e = keep.ex_b[0:1, j:j + 1] if isinstance(j, int) else keep.ex_b[0:1, bass.ds(j, 1)]
                return pe.value_load(e, min_val=0, max_val=EX_B - 1)

            def step(it, p, more):
                nit, np_ = (it, 1) if p == 0 else (it + 1, 0)
                ex.T2(pe, it, p)
                ex.H(pe, nit, np_, expert(it * 2 + p + 1))
                if more:
                    ex.T(pe, it + 1, p)
                ex.Y(pe, it, p, expert(it * 2 + p))

            ex.start(pe)
            ex.T(pe, 0, 0)
            ex.T(pe, 0, 1)
            pe.wait_ge(s_low, EX_B)
            ex.H(pe, 0, 0, expert(0))
            with pe.Fori(0, PAIRS - 1) as it:
                step(it, 0, True)
                step(it, 1, True)
            step(PAIRS - 1, 0, True)
            step(PAIRS - 1, 1, False)
            ex.T2(pe, PAIRS, 0)
            ex.Y(pe, PAIRS, 0, expert(LAST))


def weights_c(nc, ctx, keep):
    keep.w13s = ctx.enter_context(nc.sbuf_tensor("w13s", [P, DC, 2 * HID], F32))
    keep.w2 = ctx.enter_context(nc.sbuf_tensor("w2", [P, EX_C + 1, HID // P, DIM], F32))
    keep.gate = ctx.enter_context(nc.sbuf_tensor("gate", [P, DC, EX_C], F32))
    keep.s_wc = ctx.enter_context(nc.semaphore("c_weights_loaded"))


def gate_expert_block(nc, ext, keep):
    x2 = keep.x1
    Q = BATCH
    S_PAIRS = NT // 2
    FIRST = Q // 2
    SCALE = FIRST + 1
    R_PAIRS = NB_C // 2
    LAST = S_PAIRS + R_PAIRS
    SHARED = EX_C
    with ExitStack() as ctx:
        def sb(name, shape, dt=F32):
            return ctx.enter_context(nc.sbuf_tensor(name, shape, dt))

        def sem(name):
            return ctx.enter_context(nc.semaphore(name))

        xT_all = keep.arena[:, :].rearrange("p (t c q) -> p t c q", t=NT, c=DC)
        xn_flat = keep.xn
        xn = xn_flat[:, :].rearrange("p (t d) -> p t d", t=TB)
        rows = [xn_flat[:, p * ROW:(p + 1) * ROW] for p in range(2)]
        stage_flat = sb("gstage", [P, TB * ROW])
        yg = stage_flat[:, 0:TB * DIM].rearrange("p (t d) -> p t d", t=TB)
        stage = stage_flat[:, :].rearrange("p (t w) -> p t w", t=TB)
        between = carve(stage_flat)
        sort = Sorter(between, keep, "sc", EX_C, NT * TOPK, NB_C)
        keep.w13 = sb("w13", [P, EX_C, DC, 2 * HID])
        ex = Experts(nc, ctx, keep, "c", keep.w13, keep.w2, (0, HID), (HID, 2 * HID), rows, NT, w1_fixed=keep.w13s)
        pos_cur = keep.pos_cur
        st = sb("gst", [P, TB, 6])
        mv = sb("gmv", [P, TB, 2])
        var = sb("gvar", [P, TB])
        rstd = sb("grstd", [P, TB])
        half = sb("ghalf", [P, TB])
        epsc = sb("gepsc", [P, TB])
        lg = ex.y[1][0:EX_C, :]
        sc = sb("scores", [P, NT, EX_C])
        best = between("best", [P, NT, 8])
        besti = between("besti", [P, NT, 8], U32)
        chosen = between("chosen", [P, TOPK, NT])
        mean = sb("mean", [P, NT])
        dev = sb("dev", [P, NT])
        gain = sb("gain", [P, TOPK, NT])
        pos = sb("pos_c", [P, TOPK * NT], I32)
        ex_c = sb("ex_c", [P, NB_C], I32)
        mean_cur = sb("mean_cur", [P, TB])
        gain_cur = sb("gain_cur", [P, TOPK, TB])
        slot_cur = sb("slot_cur", [P, TOPK, 2 * TB], I32)
        tokens = sb("tokens", [P, NB_C], I32)
        tokens_cur = sb("tokens_cur", [P, 1], I32)
        lps = ctx.enter_context(nc.psum_tensor("glogits", [P, 512], F32))
        xb = [ex.TX[0], ex.TX[1], ex.HB[1], ex.YB[1]]
        tps = lps

        s_cst = sem("gate_constants")
        s_pos, s_g = sem("gate_positions"), [sem(f"gathered{r}") for r in range(TB)]
        s_x2 = sem("x2_ready")
        s_ch = sem("gate_chain")
        s_mv, s_var, s_rstd = sem("stats3_ready"), sem("var3_ready"), sem("rstd3_ready")
        s_xn = sem("xn3_ready")
        s_tx, s_tc = sem("xn3_transposed"), sem("xT3_ready")
        s_lg, s_lc, s_lt, s_ls = (sem("logits_summed"), sem("logits_copied"), sem("logits_transposed"),
                                  sem("logits_stored"))
        s_ex = sem("exp_ready")
        s_best, s_pick, s_rank = sem("best_ready"), sem("gate_pick_ready"), sem("gate_rank_ready")
        s_sort = sem("gate_sorted")
        s_cur = sem("gains_current")
        s_stage = sem("scaled_rows_ready")
        s_slot, s_sc = sem("slots_current"), keep.s_xs_c
        s_base0 = sem("quarter_rows_stored")
        s_base = [sem(f"base_rows_stored{p}") for p in range(2)]
        s_id, s_tok = sem("row_tokens_copied"), sem("tokens_current")
        s_add = keep.s_add
        s_left = sem("y_buffer_steps")
        s_aux = sem("c_unused_count")
        block = ctx.enter_context(nc.Block())
        STORES = (S_PAIRS - FIRST) * 16 + 16

        def at(view, j):
            return view[bass.ds(j, 1), :, :].rearrange("a p d -> (a p) d")

        def quarter(ap, q):
            return ap[:, bass.ds(q * TB, TB)]

        @block.sync
        def _(sp):
            xs = keep.xs_c.rearrange("(n p) d -> n p d", p=P)
            out = keep.out[0:TOKENS, :].rearrange("(n p) d -> n p d", p=P)
            sp.sem_inc(s_base0, 16)
            for p in range(2):
                sp.sem_inc(s_base[p], 16)

            def store(j, p, done):
                sp.wait_ge(ex.s_yf, j + 3)
                sp.sem_inc(s_aux, 1)
                sp.dma_start(at(out, j), ex.y[p][:, :]).then_inc(done, 16)

            with sp.Fori(0, Q) as q:
                store(q, 0, s_base0)
                load_w13(sp, ext, keep, q)
            LOADING = EX_C - Q
            with sp.Fori(FIRST, FIRST + LOADING) as it:
                for p in range(2):
                    store(it * 2 + p, p, s_base[p])
                load_w13(sp, ext, keep, it + (Q - FIRST))
            with sp.Fori(FIRST + LOADING, S_PAIRS - 1) as it:
                for p in range(2):
                    store(it * 2 + p, p, s_base[p])
            for t in range(TB):
                sp.wait_ge(s_sc[t], 16 * TOPK * Q + 16)
            for p in range(2):
                sp.dma_start(ex.rows[p], at(xs, p)).then_inc(ex.loaded[p], 16)
            for p in range(2):
                store(NT - 2 + p, p, s_base[p])

            def load_routed(m, p):
                sp.wait_ge(ex.s_T, m - 1)
                sp.sem_inc(s_aux, 1)
                sp.wait_ge(s_id, m - 1)
                sp.sem_inc(s_aux, 1)
                sp.dma_start(ex.rows[p], at(xs, m)).then_inc(ex.loaded[p], 16)

            with sp.Fori(0, R_PAIRS - 1) as r:
                for p in range(2):
                    load_routed(r * 2 + (p + 2), p)
            load_routed(NB_C - 1, 0)

        @block.gpsimd
        def _(pool):
            g = nc.gpsimd
            pool.sem_inc(s_left, 1)
            g.memset(half[:, :], -0.5).then_inc(s_cst, 1)
            g.memset(epsc[:, :], EPS).then_inc(s_cst, 1)
            pool.wait_ge(s_cst, 2)

            def gather(q):
                if not (isinstance(q, int) and q == 0):
                    for r in range(TB):
                        pool.wait_ge(s_g[r], q * 16)
                    pool.sem_inc(s_aux, 1)
                g.tensor_copy(pos_cur[:, :], keep.pos_b[:, bass.ds(q * TB, TB)]).then_inc(s_pos, 1)
                pool.wait_ge(s_pos, q + 1)
                for r in range(TB):
                    pool.wait_ge(s_x2, q * TB + r + 1)
                    pool.sem_inc(s_aux, 1)
                    g.indirect_dma_start(out=yg[:, r, :], out_offset=None, in_=keep.ys_b,
                                         in_offset=bass.IndirectOffsetOnAxis(ap=pos_cur[:, r:r + 1].bitcast(U32), axis=0)
                                         ).then_inc(s_g[r], 16)

            def inverse_root(q):
                pool.wait_ge(s_mv, q * TB + TB)
                g.tensor_tensor(out=var[:, :], in0=mv[:, :, 1], in1=epsc[:, :], op=ALU.add).then_inc(s_var, 1)
                pool.wait_ge(s_var, q + 1)
                g.tensor_tensor(out=rstd[:, :], in0=var[:, :], in1=half[:, :], op=ALU.pow).then_inc(s_rstd, 1)

            pool.wait_ge(s_x2, TB)
            gather(0)
            inverse_root(0)
            gather(1)
            with pool.Fori(0, Q - 2) as q:
                gather(q + 2)
                inverse_root(q + 1)
            inverse_root(Q - 1)

            pool.wait_ge(keep.s_clr_c, 16 * CLEARS_C * (BATCH - 1))
            pool.wait_ge(s_sort, SORTED)
            with pool.Fori(0, Q // 2) as h:
                for t in range(TB):
                    pool.wait_ge(s_sc[t], h * (2 * 16 * TOPK) + 16)
                pool.sem_inc(s_aux, 1)
                g.tensor_copy(slot_cur[:, :, :], pos[:, :].rearrange("p (k n) -> p k n", k=TOPK)[:, :, bass.ds(h * (2 * TB), 2 * TB)]
                              ).then_inc(s_slot, 1)
                pool.wait_ge(s_slot, h + 1)
                for n in range(2 * TOPK):
                    for t in range(TB):
                        pool.wait_ge(s_stage, h * (2 * TOPK * STAGED) + (n * STAGED + 2 * t + 3))
                        pool.sem_inc(s_aux, 1)
                        col = (n // TOPK) * TB + t
                        g.indirect_dma_start(out=keep.xs_c, in_=stage[:, t, :], in_offset=None,
                                             out_offset=bass.IndirectOffsetOnAxis(ap=slot_cur[:, n % TOPK, col:col + 1].bitcast(U32), axis=0)
                                             ).then_inc(s_sc[t], 16)
            pool.wait_ge(s_base0, 16 * Q + 16)
            for p in range(2):
                pool.wait_ge(s_base[p], STORES)

            def add(m, p):
                pool.wait_ge(s_id, m + 1)
                pool.wait_ge(s_add, m * 16 + 16)
                pool.sem_inc(s_left, 1)
                g.tensor_copy(tokens_cur[:, :], tokens[:, bass.ds(m, 1)]).then_inc(s_tok, 1)
                pool.wait_ge(s_tok, m + 1)
                pool.wait_ge(ex.s_yf, m + (2 * S_PAIRS + 3))
                pool.sem_inc(s_aux, 1)
                g.indirect_dma_start(out=keep.out, out_offset=bass.IndirectOffsetOnAxis(ap=tokens_cur[:, 0:1].bitcast(U32), axis=0),
                                     in_=ex.y[p][:, :], in_offset=None, compute_op=ALU.add).then_inc(s_add, 16)

            with pool.Fori(0, R_PAIRS) as r:
                for p in range(2):
                    add(r * 2 + p, p)
            add(NB_C - 1, 0)
            pool.wait_ge(s_add, 16 * NB_C + 16)

        @block.vector
        def _(dve):
            v = nc.vector
            dve.sem_inc(s_x2, TB)
            dve.sem_inc(s_stage, 1)

            def tile(n):
                return x2[:, bass.ds(n, 1), :].rearrange("p a d -> p (a d)")

            def add_experts(q):
                def add(r):
                    dve.wait_ge(s_g[r], q * 16 + 16)
                    v.tensor_tensor(out=tile(q * TB + r), in0=tile(q * TB + r), in1=yg[:, r, :], op=ALU.add).then_inc(s_x2, 1)

                def statistics(r):
                    dve.wait_ge(s_x2, q * TB + TB + r + 1)
                    dve.sem_inc(s_aux, 1)
                    v.bn_stats(st[:, r, :], tile(q * TB + r)).then_inc(s_ch, 1)

                add(0)
                for r in range(1, TB):
                    add(r)
                    statistics(r - 1)
                statistics(TB - 1)
                for r in range(TB):
                    dve.wait_ge(s_ch, q * TB + r + 1)
                    dve.sem_inc(s_aux, 1)
                    v.bn_aggr(mv[:, r, :], st[:, r, :]).then_inc(s_mv, 1)

            def normalise(q):
                dve.wait_ge(s_rstd, q + 1)
                for r in range(TB):
                    v.tensor_scalar(out=xn[:, r, :], in0=tile(q * TB + r), scalar1=mv[:, r, 0:1], scalar2=rstd[:, r:r + 1],
                                    op0=ALU.subtract, op1=ALU.mult).then_inc(s_xn, 1)
                v.tensor_copy(quarter(mean, q), mv[:, :, 0]).then_inc(s_aux, 1)
                v.tensor_copy(quarter(dev, q), rstd[:, :]).then_inc(s_aux, 1)

            def base(j, p, guard, value):
                dve.wait_ge(guard, value)
                dve.sem_inc(s_aux, 1)
                dve.wait_ge(ex.s_Y, j + 3)
                v.tensor_tensor(out=ex.y[p][:, :], in0=ex.YB[p][:, :], in1=tile(j), op=ALU.add).then_inc(ex.s_yf, 1)

            def base_q(q):
                base(q, 0, s_base0, q * 16 + 16)

            def base_p(it, p):
                base(it * 2 + p, p, s_base[p], it * 16 - (16 * FIRST - 16))

            def quarter_product(q):
                dve.wait_ge(ex.s_sil, q + 1)
                v.tensor_tensor(out=ex.a[:, 0, :], in0=ex.HB[0][:, ex.right[0]:ex.right[1]], in1=ex.sil[:, 0, :],
                                op=ALU.mult).then_inc(ex.s_a, 1)

            add_experts(0)
            normalise(0)
            add_experts(1)
            with dve.Fori(0, Q - 2) as q:
                quarter_product(q)
                normalise(q + 1)
                add_experts(q + 2)
                base_q(q)
            quarter_product(Q - 2)
            normalise(Q - 1)
            base_q(Q - 2)
            quarter_product(Q - 1)
            base_q(Q - 1)

            do = Chain(dve, s_best)
            dve.wait_ge(s_ex, 1)
            do(v.tensor_scalar(out=sc[:, :, :], in0=sc[:, :, :], scalar1=1.0, scalar2=None, op0=ALU.add))
            do(v.reciprocal(sc[:, :, :], sc[:, :, :]))
            for n in range(NT):
                v.max(best[:, n, :], sc[:, n, :]).then_inc(s_best, 1)
            ex.product(dve, FIRST, 0)
            dve.wait_ge(s_best, 2 + NT)
            for n in range(NT):
                v.max_index(besti[:, n, :], best[:, n, :], sc[:, n, :]).then_inc(s_best, 1)
            dve.wait_ge(s_best, 2 + 2 * NT)
            do = Chain(dve, s_pick)
            do(v.tensor_copy(chosen[:, :, :], besti[:, :, 0:TOPK].rearrange("p n k -> p k n")))
            for e in range(EX_C):
                v.tensor_scalar(out=sort.pick[:, e, :], in0=chosen[:, :, :].rearrange("p k n -> p (k n)"),
                                scalar1=float(e), scalar2=None, op0=ALU.is_equal).then_inc(s_pick, 1)
            dve.wait_ge(s_pick, 1 + EX_C)
            v.tensor_copy(sort.pickb[:, :, :], sort.pick[:, :, :]).then_inc(s_pick, 1)
            ex.product(dve, FIRST, 1)
            do = Chain(dve, s_sort)
            dve.wait_ge(s_rank, 1)
            sort.on_vector(v, do, lps, pos[:, :], ex_c[:, :], pause=lambda: ex.product(dve, FIRST + 1, 0))
            do(v.tensor_tensor(out=gain[:, :, :], in0=best[:, :, 0:TOPK].rearrange("p n k -> p k n"),
                               in1=dev[:, :].unsqueeze(1).to_broadcast([P, TOPK, NT]), op=ALU.mult))
            assert do.n == SORTED
            dve.wait_ge(s_base0, 16 * Q + 16)
            base_p(FIRST, 0)
            base_p(FIRST, 1)

            def scale(q, k):
                for t in range(TB):
                    dve.wait_ge(s_sc[t], q * (16 * TOPK) + (16 * k + 16))
                    dve.sem_inc(s_aux, 1)
                    v.tensor_copy(stage[:, t, DIM:ROW].bitcast(I32),
                                  keep.token[:, bass.ds(q * TB + t, 1)].to_broadcast([P, ROW - DIM])).then_inc(s_stage, 1)
                    v.tensor_scalar(out=stage[:, t, 0:DIM], in0=tile(q * TB + t), scalar1=mean_cur[:, t:t + 1],
                                    scalar2=gain_cur[:, k, t:t + 1], op0=ALU.subtract, op1=ALU.mult).then_inc(s_stage, 1)

            with dve.Fori(0, Q) as q:
                it = q + SCALE
                dve.wait_ge(s_stage, q * (STAGED * TOPK) + 1)
                dve.sem_inc(s_aux, 1)
                v.tensor_copy(mean_cur[:, :], quarter(mean, q)).then_inc(s_cur, 1)
                v.tensor_copy(gain_cur[:, :, :], gain[:, :, bass.ds(q * TB, TB)]).then_inc(s_cur, 1)
                dve.wait_ge(s_cur, q * 2 + 2)
                scale(q, 0)
                ex.product(dve, it, 1)
                base_p(it, 0)
                scale(q, 1)
                ex.product(dve, it + 1, 0)
                base_p(it, 1)

            def take_tokens(it, p):
                dve.wait_ge(ex.loaded[p], it * 16 + (16 - S_PAIRS * 16))
                dve.sem_inc(s_aux, 1)
                v.tensor_copy(tokens[:, bass.ds(it * 2 + (p - 2 * S_PAIRS), 1)],
                              ex.rows[p][:, DIM:DIM + 1].bitcast(I32)).then_inc(s_id, 1)

            ex.product(dve, S_PAIRS - 1, 1)
            base_p(S_PAIRS - 1, 0)
            take_tokens(S_PAIRS, 0)
            ex.product(dve, S_PAIRS, 0)
            take_tokens(S_PAIRS, 1)
            base_p(S_PAIRS - 1, 1)
            with dve.Fori(S_PAIRS, LAST - 1) as it:
                ex.product(dve, it, 1)
                take_tokens(it + 1, 0)
                ex.product(dve, it + 1, 0)
                take_tokens(it + 1, 1)
            ex.product(dve, LAST - 1, 1)
            take_tokens(LAST, 0)
            ex.product(dve, LAST, 0)

        @block.scalar
        def _(act):
            a = nc.scalar

            def copy_tile(j, p):
                a.copy(ex.xT[:, p, :, :], xT_all[:, bass.ds(j, 1), :, :].rearrange("p a c q -> p (a c) q")).then_inc(ex.s_xT, 1)

            def copy_aT(it, p, j):
                act.wait_ge(ex.s_T2, j + 3)
                a.copy(ex.aT[:, p, :, :], ex.TA[:, 0:ex.hid].rearrange("p (c q) -> p c q", c=ex.kc)).then_inc(ex.s_aT, 1)

            def copy_quarter(q):
                for c in range(DC):
                    act.wait_ge(s_tx, q * DC + c + 1)
                    a.copy(xT_all[:, bass.ds(q * TB, TB), c, :], xb[c][:, :].rearrange("p (t q) -> p t q", t=TB)).then_inc(s_tc, 1)
                act.wait_ge(s_tc, q * DC + DC)
                copy_tile(q, 0)

            def quarter_silu(q):
                act.wait_ge(ex.s_H, q + 1)
                a.activation(ex.sil[:, 0, :], ex.HB[0][:, ex.left[0]:ex.left[1]], ACT.Silu).then_inc(ex.s_sil, 1)

            def copy_logits(q):
                act.wait_ge(s_lg, q + 1)
                a.copy(lg, lps[0:EX_C, :]).then_inc(s_lc, 1)

            def copy_scores(q):
                act.wait_ge(s_lt, q + 1)
                a.copy(sc[:, bass.ds(q * TB, TB), :], tps[:, 0:TB * EX_C].rearrange("p (t e) -> p t e", e=EX_C)).then_inc(s_ls, 1)

            copy_quarter(0)
            quarter_silu(0)
            copy_logits(0)
            with act.Fori(0, Q - 1) as q:
                copy_aT(0, 0, q)
                copy_quarter(q + 1)
                copy_scores(q)
                quarter_silu(q + 1)
                copy_logits(q + 1)
            copy_aT(0, 0, Q - 1)
            copy_scores(Q - 1)
            act.wait_ge(s_ls, Q)
            a.activation(sc[:, :, :], sc[:, :, :], ACT.Exp, scale=-1.0).then_inc(s_ex, 1)
            copy_tile(2 * FIRST, 0)
            copy_tile(2 * FIRST + 1, 1)
            ex.silu(act, FIRST, 0)

            def y_out(it, p):
                act.wait_ge(s_left, it * 2 + (p - (2 * S_PAIRS - 1)))
                ex.copy_y(act, it, p)

            def step(it, p, fetch=None, routed=False):
                nit, np_ = (it, 1) if p == 0 else (it + 1, 0)
                ex.copy_aT(act, it, p)
                ex.silu(act, nit, np_)
                if fetch:
                    fetch(it + 1, p)
                if routed:
                    y_out(it, p)

            def shared_tile(it, p):
                copy_tile(it * 2 + p, p)

            def transposed(it, p):
                ex.copy_xT(act, it, p)

            with act.Fori(FIRST, S_PAIRS - 1) as it:
                for p in range(2):
                    step(it, p, shared_tile)
            for p in range(2):
                step(S_PAIRS - 1, p, transposed)
            act.wait_ge(ex.s_yf, 2 * S_PAIRS + 2)
            for p in range(2):
                act.wait_ge(s_base[p], STORES)
            with act.Fori(S_PAIRS, LAST - 1) as it:
                for p in range(2):
                    step(it, p, transposed, routed=True)
            step(LAST - 1, 0, transposed, routed=True)
            step(LAST - 1, 1, routed=True)
            ex.copy_aT(act, LAST, 0)
            y_out(LAST, 0)

        @block.tensor
        def _(pe):
            te = nc.tensor

            def expert(m):
                e = ex_c[0:1, m:m + 1] if isinstance(m, int) else ex_c[0:1, bass.ds(m, 1)]
                return pe.value_load(e, min_val=0, max_val=EX_C - 1)

            def transpose_quarter(q):
                pe.wait_ge(s_xn, q * TB + TB)
                for c in range(DC):
                    for r in range(TB):
                        last = te.transpose(xb[c][:, r * P:(r + 1) * P], xn[:, r, c * P:(c + 1) * P], keep.ident[:, :])
                    last.then_inc(s_tx, 1)

            def first_products(q):
                pe.wait_ge(ex.s_xT, q + 3)
                for c in range(DC):
                    last = te.matmul(ex.HB[0][:, :], ex.xT[:, 0, c, :], keep.w13s[:, c, :], start=(c == 0), stop=(c == DC - 1))
                last.then_inc(ex.s_H, 1)
                if not (isinstance(q, int) and q == 0):
                    pe.wait_ge(s_ls, q)
                for c in range(DC):
                    last = te.matmul(lps[0:EX_C, :], keep.gate[:, c, :],
                                     xT_all[:, bass.ds(q * TB, TB), c, :],
                                     start=(c == 0), stop=(c == DC - 1))
                last.then_inc(s_lg, 1)

            def transpose_act(q):
                pe.wait_ge(ex.s_a, q + 3)
                for c in range(ex.kc):
                    last = te.transpose(ex.TA[:, c * P:(c + 1) * P], ex.a[:, 0, c * P:(c + 1) * P], keep.ident[:, :])
                last.then_inc(ex.s_T2, 1)

            def second_product(q):
                pe.wait_ge(s_lc, q + 1)
                pe.sem_inc(s_aux, 1)
                for r in range(TB):
                    last = te.transpose(tps[:, r * EX_C:(r + 1) * EX_C], lg[:, r * P:(r + 1) * P],
                                        keep.ident[0:EX_C, 0:EX_C])
                last.then_inc(s_lt, 1)
                pe.wait_ge(ex.s_yf, q + 2)
                pe.wait_ge(ex.s_aT, q + 2)
                for c in range(ex.kc):
                    last = te.matmul(ex.YB[0][:, :], ex.aT[:, 0, c, :], keep.w2[:, SHARED, c, :], start=(c == 0), stop=(c == ex.kc - 1))
                last.then_inc(ex.s_Y, 1)

            def shared():
                return SHARED

            def step(it, p, e_next, e, fetch):
                nit, np_ = (it, 1) if p == 0 else (it + 1, 0)
                ex.T2(pe, it, p)
                ex.H(pe, nit, np_, e_next())
                if fetch:
                    ex.T(pe, it + 1, p)
                ex.Y(pe, it, p, e())

            ex.start(pe)
            pe.wait_ge(keep.s_wc, 16 * LOADS_EARLY)
            transpose_quarter(0)
            first_products(0)
            with pe.Fori(0, Q - 1) as q:
                transpose_act(q)
                transpose_quarter(q + 1)
                second_product(q)
                first_products(q + 1)
            transpose_act(Q - 1)
            second_product(Q - 1)
            pe.wait_ge(ex.s_yf, 2 * FIRST + 2)
            ex.H(pe, FIRST, 0, SHARED)
            ex.T2(pe, FIRST, 0)
            ex.H(pe, FIRST, 1, SHARED)
            pe.wait_ge(s_pick, EX_C + 2)
            sort.on_tensor(te, lps).then_inc(s_rank, 1)
            ex.Y(pe, FIRST, 0, SHARED)
            step(FIRST, 1, shared, shared, False)
            with pe.Fori(SCALE, S_PAIRS - 1) as it:
                for p in range(2):
                    step(it, p, shared, shared, False)
            step(S_PAIRS - 1, 0, shared, shared, True)
            pe.wait_ge(keep.s_wc, 16 * LOADS_ALL)
            step(S_PAIRS - 1, 1, lambda: expert(0), shared, True)
            with pe.Fori(0, R_PAIRS - 1) as r:
                for p in range(2):
                    step(r + S_PAIRS, p, lambda: expert(r * 2 + (p + 1)), lambda: expert(r * 2 + p), True)
            for p in range(2):
                m = (R_PAIRS - 1) * 2 + p
                step(LAST - 1, p, lambda: expert(m + 1), lambda: expert(m), p == 0)
            ex.T2(pe, LAST, 0)
            ex.Y(pe, LAST, 0, expert(NB_C - 1))


STAGED = 2 * TB
SORTED = EX_C + 15


def build(nc, ext):
    with ExitStack() as ctx:
        keep = Keep(nc, ctx, ext)
        setup_block(nc, ext, keep)
        attention_block(nc, ext, keep)
        weights_c(nc, ctx, keep)
        id_expert_block(nc, ext, keep)
        gate_expert_block(nc, ext, keep)


def _layout(np, x, itok_BxS_13_99985, ctx_2048, L0_attn_Wqa, L0_attn_Wqb, L0_attn_Wkva, L0_attn_Wkvb, L0_attn_Wo,
            L0_ffn_gate_w, L0_ffn_w1, L0_ffn_w2, L0_ffn_w3, L0_ffn_ws1, L0_ffn_ws2, L0_ffn_ws3):
    def rows(w):
        return w.reshape(w.shape[0] // P, P, w.shape[1]).transpose(1, 0, 2)

    def experts(ws):
        return np.stack([rows(w) for w in ws], axis=1)

    pe = L0_attn_Wkva[:, LORA:]
    even, odd = pe[:, 0::2], pe[:, 1::2]
    wqb = L0_attn_Wqb.reshape(LORA, NG, GROUP, QK)
    wqb = [wqb[..., NOPE::2], wqb[..., NOPE + 1::2], wqb[..., :NOPE]]
    wkvb = L0_attn_Wkvb.reshape(LORA, HEADS, NOPE + VD)

    freq = np.float32(10000.0) ** (-np.arange(0, ROPE, 2, dtype=np.float32) / np.float32(ROPE))
    angle = (np.arange(SEQ, dtype=np.float32)[:, None] * freq[None, :]).astype(np.float64).T
    cos, sin = np.cos(angle), np.sin(angle)
    return {
        "x": x.reshape(TOKENS, DIM),
        "ids": itok_BxS_13_99985.reshape(NT, P).T,
        "wqa": rows(L0_attn_Wqa),
        "wkva": rows(np.concatenate([L0_attn_Wkva[:, :LORA], even, odd, odd, even], axis=1)),
        "wqb": np.stack(wqb, axis=2).reshape(LORA, NG * 3, P),
        "wk": wkvb[..., :NOPE].reshape(LORA, NG, P),
        "wv": wkvb[..., NOPE:].reshape(LORA, HEADS * VD),
        "wo": rows(L0_attn_Wo),
        "cos4": np.tile(cos * QK ** -0.5, (GROUP, 1)).astype(np.float32),
        "sin4": np.tile(sin * QK ** -0.5, (GROUP, 1)).astype(np.float32),
        "kcs": np.concatenate([cos, cos, -sin, sin]).astype(np.float32),
        "ctxT": experts([w.T for w in ctx_2048]).reshape(P, EX_B * DC * DIM),
        "w13": experts([np.concatenate([a.T, b.T], axis=1) for a, b in
                        zip([*L0_ffn_w1, L0_ffn_ws1], [*L0_ffn_w3, L0_ffn_ws3])]),
        "w2": experts([w.T for w in [*L0_ffn_w2, L0_ffn_ws2]]),
        "gate": rows(L0_ffn_gate_w.T),
    }


def kernel(**inputs):
    import numpy as _np
    import concourse.bacc as _bacc
    from concourse.bass_utils import run_bass_kernel_spmd as _run

    laid = _layout(_np, **{name: _np.asarray(a) for name, a in inputs.items()})
    nc = _bacc.Bacc("TRN2", target_bir_lowering=False, num_devices=1)
    arrays, ext = {}, {}
    for name, a in laid.items():
        a = _np.ascontiguousarray(a)
        arrays[f"in_{name}"] = a
        ext[name] = nc.dram_tensor(f"in_{name}", a.shape, mybir.dt.from_np(a.dtype), kind="ExternalInput").ap()
    ext["out"] = nc.dram_tensor("out", (TOKENS + P, DIM), F32, kind="ExternalOutput").ap()
    build(nc, ext)
    r = _run(nc, [arrays], core_ids=[0])
    return r.results[0]["out"][:TOKENS].reshape(BATCH, SEQ, DIM)
```
